# Optimizing a Trainium2 kernel written in Bass

```python
import numpy as np
import jax
import jax.numpy as jnp

def _softmax(x, axis=-1):
    return jax.nn.softmax(x, axis=axis)

def _gelu(x):
    return jax.nn.gelu(x, approximate=True)

def _silu(x):
    return jax.nn.silu(x)

def _sigmoid(x):
    return jax.nn.sigmoid(x)

def _layernorm(x, axis=-1, eps=1e-05):
    m = jnp.mean(x, axis=axis, keepdims=True)
    v = jnp.var(x, axis=axis, keepdims=True)
    return (x - m) / jnp.sqrt(v + eps)

def _scatter_add(tgt, idx, src, axis=0):
    return tgt.at[idx].add(src)

def _segment_sum(src, seg, n):
    return jax.ops.segment_sum(src, seg, n)
kernel_name = 'mk_decoder_postln_d2_seqx_r8_7c4b15'

def setup_inputs(seed: int=0):
    np.random.seed(seed)
    _w = jnp.asarray

    def _rec_inputs():
        import jax
        import jax.numpy as jnp
        _rk = jax.random.key(seed)
        x = -0.0002928 + 1 * jax.random.normal(jax.random.fold_in(_rk, 1), (4, 256, 128), jnp.float32)
        _lenS = 256 - jax.random.randint(jax.random.fold_in(_rk, 7), (4,), 0, max(1, 256 // 4) + 1, jnp.int32)
        _lenS2 = 256 - jax.random.randint(jax.random.fold_in(_rk, 8), (4,), 0, max(1, 256 // 4) + 1, jnp.int32)
        _ctx_1024P = jax.random.normal(jax.random.fold_in(_rk, 11), (4, 16, 128), jnp.float32)
        _ctx_1024c = jax.random.dirichlet(jax.random.fold_in(_rk, 511), 0.3 * jnp.ones((16,), jnp.float32), (4, 256))
        _ctx_1024t = jnp.einsum('bsk,bkd->bsd', _ctx_1024c, _ctx_1024P)
        _ctx_1024t = _ctx_1024t * jax.lax.rsqrt(jnp.mean(jnp.square(_ctx_1024t)) + 1e-12) * 0.953939
        ctx_1024 = -1.39393e-06 + 0.999914 * (_ctx_1024t + 0.3 * jax.random.normal(jax.random.fold_in(_rk, 611), (4, 256, 128), jnp.float32))
        return (x, ctx_1024)
    x, ctx_1024 = _rec_inputs()

    def _L0_attn_setup():
        import jax, jax.numpy as jnp
        import numpy as np
        B, L, D, H = (4, 512, 128, 16)
        LN_EPS = 1e-05

        def _gated_delta_rule(q, k, v, lam, beta, d):

            def step(S, inp):
                k_t, v_t, q_t = inp
                S = lam * S
                u = beta * (v_t - jnp.einsum('kv,k->v', S, k_t))
                S = S + k_t[:, None] * u[None, :]
                o = jnp.einsum('kv,k->v', S, q_t)
                return (S, o)

            def scan_one(k_h, v_h, q_h):
                S0 = jnp.zeros((d, d), dtype=q.dtype)
                _, o = jax.lax.scan(step, S0, (k_h, v_h, q_h))
                return o
            return jax.vmap(scan_one)(k, v, q)
        key = jax.random.key(seed)
        k0, k1 = jax.random.split(key, 2)
        x = jax.random.normal(k0, (B, L, D), dtype=jnp.float32)
        W = jax.random.normal(k1, (D, D), dtype=jnp.float32) / jnp.sqrt(D).astype(jnp.float32)
        ln_gamma = jnp.ones((D,), dtype=jnp.float32)
        ln_beta = jnp.zeros((D,), dtype=jnp.float32)
        eta = jnp.asarray(0.01, dtype=jnp.float32)
        lam_logit = jnp.asarray(np.log(0.99) - np.log(0.01), dtype=jnp.float32)
        return {'x': x, 'W': W, 'ln_gamma': ln_gamma, 'ln_beta': ln_beta, 'eta': eta, 'lam_logit': lam_logit}
    _L0_attn_all = _L0_attn_setup()
    _L0_attn_in = {k: v for k, v in _L0_attn_all.items() if k in ('W', 'ln_gamma', 'ln_beta', 'eta', 'lam_logit')}
    del _L0_attn_all

    def _L0_xattn_setup():
        import jax, jax.numpy as jnp
        import numpy as np
        B, S, H, NH = (2, 256, 128, 4)
        DH = H // NH
        EPS = 1e-06

        def _parallel_stabilized(qh, kh, vh, ig, fg):
            log_fg = jax.nn.log_sigmoid(fg)
            cs = jnp.cumsum(log_fg, axis=2)
            ltr = jnp.tril(jnp.ones((qh.shape[2], qh.shape[2]), dtype=bool))
            log_fg_mat = jnp.where(ltr, cs - jnp.swapaxes(cs, 2, 3), -jnp.inf)
            log_D = log_fg_mat + jnp.swapaxes(ig, 2, 3)
            max_log_D = jnp.max(log_D, axis=-1, keepdims=True)
            D = jnp.exp(log_D - max_log_D)
            qk = jnp.einsum('bhsd,bhtd->bhst', qh, kh) / jnp.sqrt(jnp.float32(DH))
            C = qk * D
            normalizer = jnp.maximum(jnp.abs(jnp.sum(C, axis=-1, keepdims=True)), jnp.exp(-max_log_D))
            return jnp.einsum('bhst,bhtd->bhsd', C / (normalizer + EPS), vh)
        key = jax.random.key(seed)
        ks = jax.random.split(key, 6)
        q = jax.random.normal(ks[0], (B, S, H), dtype=jnp.float32)
        k = jax.random.normal(ks[1], (B, S, H), dtype=jnp.float32)
        v = jax.random.normal(ks[2], (B, S, H), dtype=jnp.float32)
        igate_kernel = jax.random.normal(ks[3], (3 * H, NH), dtype=jnp.float32) * 0.02
        fgate_kernel = jax.random.normal(ks[4], (3 * H, NH), dtype=jnp.float32) * 0.02
        igate_bias = jax.random.normal(ks[5], (NH,), dtype=jnp.float32) * 0.1
        fgate_bias = jnp.linspace(3.0, 6.0, NH, dtype=jnp.float32)
        outnorm_scale = jnp.ones((H,), dtype=jnp.float32)
        return {'q': q, 'k': k, 'v': v, 'igate_kernel': igate_kernel, 'igate_bias': igate_bias, 'fgate_kernel': fgate_kernel, 'fgate_bias': fgate_bias, 'outnorm_scale': outnorm_scale}
    _L0_xattn_all = _L0_xattn_setup()
    _L0_xattn_in = {k: v for k, v in _L0_xattn_all.items() if k in ('igate_kernel', 'igate_bias', 'fgate_kernel', 'fgate_bias', 'outnorm_scale')}
    del _L0_xattn_all

    def _L0_ffn_setup():
        import jax, jax.numpy as jnp
        import numpy as np
        B, S, D, E, F = (2, 256, 128, 14, 256)
        key = jax.random.key(seed)
        k = jax.random.split(key, 4)
        h = jax.random.normal(k[0], (B, S, D), dtype=jnp.float32)
        router_w = jax.random.normal(k[1], (D, E), dtype=jnp.float32) * 0.02
        w1 = jax.random.uniform(k[2], (E, D, F), dtype=jnp.float32, minval=-1.0, maxval=1.0) * float(np.sqrt(6.0 / D))
        w2 = jax.random.uniform(k[3], (E, F, D), dtype=jnp.float32, minval=-1.0, maxval=1.0) * float(np.sqrt(6.0 / F))
        b1 = jnp.zeros((E, F), dtype=jnp.float32)
        b2 = jnp.zeros((E, D), dtype=jnp.float32)
        return {'h': h, 'router_w': router_w, 'w1': w1, 'b1': b1, 'w2': w2, 'b2': b2}
    _L0_ffn_all = _L0_ffn_setup()
    _L0_ffn_in = {k: v for k, v in _L0_ffn_all.items() if k in ('router_w', 'w1', 'b1', 'w2', 'b2')}
    del _L0_ffn_all

    def _L1_attn_setup():
        import jax, jax.numpy as jnp
        import numpy as np
        CHUNK = 64
        NORM_EPS = 1e-05
        DENOM_EPS = 1.0
        B, S, HID, H = (4, 512, 128, 8)
        D = HID // H

        def rmsnorm(x, w, eps=NORM_EPS):
            var = jnp.mean(x * x, axis=-1, keepdims=True)
            return x * jax.lax.rsqrt(var + eps) * w

        def chunked_linear_attn(q, k, v):
            b, s, h, d = q.shape
            n = s // CHUNK

            def to_chunks(x):
                return x.reshape(b, n, CHUNK, h, d).transpose(1, 0, 3, 2, 4)
            qc, kc, vc = (to_chunks(q), to_chunks(k), to_chunks(v))
            mask = jnp.tril(jnp.ones((CHUNK, CHUNK), dtype=q.dtype))

            def step(state, inp):
                qq, kk, vv = inp
                inter = jnp.einsum('bhcd,bhde->bhce', qq, state)
                scores = jnp.einsum('bhcd,bhed->bhce', qq, kk) * mask
                intra = jnp.einsum('bhce,bhed->bhcd', scores, vv)
                state = state + jnp.einsum('bhcd,bhce->bhde', kk, vv)
                return (state, inter + intra)
            init = jnp.zeros((b, h, d, d), dtype=q.dtype)
            _, o = jax.lax.scan(step, init, (qc, kc, vc))
            return o.transpose(1, 0, 3, 2, 4).reshape(b, s, h, d)
        key = jax.random.key(seed)
        k0, k1, k2, k3, k4 = jax.random.split(key, 5)
        hidden_states = jax.random.normal(k0, (B, S, HID), dtype=jnp.float32)
        Wq = jax.random.normal(k1, (HID, HID), dtype=jnp.float32) * 0.02
        Wk = jax.random.normal(k2, (HID, HID), dtype=jnp.float32) * 0.02
        Wv = jax.random.normal(k3, (HID, HID), dtype=jnp.float32) * 0.02
        Wo = jax.random.normal(k4, (HID, HID), dtype=jnp.float32) * 0.02
        norm_w = jnp.ones((D,), dtype=jnp.float32)
        return {'hidden_states': hidden_states, 'Wq': Wq, 'Wk': Wk, 'Wv': Wv, 'Wo': Wo, 'norm_w': norm_w}
    _L1_attn_all = _L1_attn_setup()
    _L1_attn_in = {k: v for k, v in _L1_attn_all.items() if k in ('Wq', 'Wk', 'Wv', 'Wo', 'norm_w')}
    del _L1_attn_all

    def _L1_xattn_setup():
        import jax, jax.numpy as jnp
        import numpy as np
        D_MODEL = 128
        NUM_HEADS = 16
        HEAD_DIM = D_MODEL // NUM_HEADS
        B, S = (4, 256)
        key = jax.random.key(seed)
        ks = jax.random.split(key, 11)
        scale = 1.0 / np.sqrt(D_MODEL)
        return {'query': jax.random.normal(ks[0], (B, S, D_MODEL), dtype=jnp.float32), 'key': jax.random.normal(ks[1], (B, S, D_MODEL), dtype=jnp.float32), 'value': jax.random.normal(ks[2], (B, S, D_MODEL), dtype=jnp.float32), 'Wq': jax.random.normal(ks[3], (D_MODEL, D_MODEL), dtype=jnp.float32) * scale, 'bq': jnp.zeros((D_MODEL,), dtype=jnp.float32), 'Wk': jax.random.normal(ks[4], (D_MODEL, D_MODEL), dtype=jnp.float32) * scale, 'bk': jnp.zeros((D_MODEL,), dtype=jnp.float32), 'Wv': jax.random.normal(ks[5], (D_MODEL, D_MODEL), dtype=jnp.float32) * scale, 'bv': jnp.zeros((D_MODEL,), dtype=jnp.float32), 'Wo': jax.random.normal(ks[6], (D_MODEL, D_MODEL), dtype=jnp.float32) * scale, 'bo': jnp.zeros((D_MODEL,), dtype=jnp.float32)}
    _L1_xattn_all = _L1_xattn_setup()
    _L1_xattn_in = {k: v for k, v in _L1_xattn_all.items() if k in ('Wq', 'bq', 'Wk', 'bk', 'Wv', 'bv', 'Wo', 'bo')}
    del _L1_xattn_all

    def _L1_ffn_setup():
        import jax, jax.numpy as jnp
        import numpy as np
        D_IN, D_HID = (128, 512)

        def _ternary(key, shape):
            return jax.random.randint(key, shape, -1, 2).astype(jnp.float32)

        def _tlin(x, w, s):
            return jnp.einsum('bsi,oi->bso', x, w) * s
        key = jax.random.key(seed)
        ks = jax.random.split(key, 12)
        inv = lambda fan: 1.0 / np.sqrt(fan).astype(np.float32)
        return {'x': jax.random.normal(ks[0], (4, 256, D_IN), dtype=jnp.float32), 'w1_w': _ternary(ks[1], (D_HID, D_IN)), 'w1_s': jax.random.uniform(ks[2], (D_HID,), dtype=jnp.float32) * inv(D_IN), 'w2_w': _ternary(ks[3], (D_HID, D_IN)), 'w2_s': jax.random.uniform(ks[4], (D_HID,), dtype=jnp.float32) * inv(D_IN), 'h1_w': _ternary(ks[5], (D_HID, D_HID)), 'h1_s': jax.random.uniform(ks[6], (D_HID,), dtype=jnp.float32) * inv(D_HID), 'h2_w': _ternary(ks[7], (D_HID, D_HID)), 'h2_s': jax.random.uniform(ks[8], (D_HID,), dtype=jnp.float32) * inv(D_HID), 'w3_w': _ternary(ks[9], (D_IN, D_HID)), 'w3_s': jax.random.uniform(ks[10], (D_IN,), dtype=jnp.float32) * inv(D_HID)}
    _L1_ffn_all = _L1_ffn_setup()
    _L1_ffn_in = {k: v for k, v in _L1_ffn_all.items() if k in ('w1_w', 'w1_s', 'w2_w', 'w2_s', 'h1_w', 'h1_s', 'h2_w', 'h2_s', 'w3_w', 'w3_s')}
    del _L1_ffn_all
    return {'x': x, 'ctx_1024': ctx_1024, 'L0_attn_W': _L0_attn_in['W'], 'L0_attn_ln_gamma': _L0_attn_in['ln_gamma'], 'L0_attn_ln_beta': _L0_attn_in['ln_beta'], 'L0_attn_eta': _L0_attn_in['eta'], 'L0_attn_lam_logit': _L0_attn_in['lam_logit'], 'L0_xattn_igate_kernel': _L0_xattn_in['igate_kernel'], 'L0_xattn_igate_bias': _L0_xattn_in['igate_bias'], 'L0_xattn_fgate_kernel': _L0_xattn_in['fgate_kernel'], 'L0_xattn_fgate_bias': _L0_xattn_in['fgate_bias'], 'L0_xattn_outnorm_scale': _L0_xattn_in['outnorm_scale'], 'L0_ffn_router_w': _L0_ffn_in['router_w'], 'L0_ffn_w1': _L0_ffn_in['w1'], 'L0_ffn_b1': _L0_ffn_in['b1'], 'L0_ffn_w2': _L0_ffn_in['w2'], 'L0_ffn_b2': _L0_ffn_in['b2'], 'L1_attn_Wq': _L1_attn_in['Wq'], 'L1_attn_Wk': _L1_attn_in['Wk'], 'L1_attn_Wv': _L1_attn_in['Wv'], 'L1_attn_Wo': _L1_attn_in['Wo'], 'L1_attn_norm_w': _L1_attn_in['norm_w'], 'L1_xattn_Wq': _L1_xattn_in['Wq'], 'L1_xattn_bq': _L1_xattn_in['bq'], 'L1_xattn_Wk': _L1_xattn_in['Wk'], 'L1_xattn_bk': _L1_xattn_in['bk'], 'L1_xattn_Wv': _L1_xattn_in['Wv'], 'L1_xattn_bv': _L1_xattn_in['bv'], 'L1_xattn_Wo': _L1_xattn_in['Wo'], 'L1_xattn_bo': _L1_xattn_in['bo'], 'L1_ffn_w1_w': _L1_ffn_in['w1_w'], 'L1_ffn_w1_s': _L1_ffn_in['w1_s'], 'L1_ffn_w2_w': _L1_ffn_in['w2_w'], 'L1_ffn_w2_s': _L1_ffn_in['w2_s'], 'L1_ffn_h1_w': _L1_ffn_in['h1_w'], 'L1_ffn_h1_s': _L1_ffn_in['h1_s'], 'L1_ffn_h2_w': _L1_ffn_in['h2_w'], 'L1_ffn_h2_s': _L1_ffn_in['h2_s'], 'L1_ffn_w3_w': _L1_ffn_in['w3_w'], 'L1_ffn_w3_s': _L1_ffn_in['w3_s']}

def reference(x, ctx_1024, L0_attn_W, L0_attn_ln_gamma, L0_attn_ln_beta, L0_attn_eta, L0_attn_lam_logit, L0_xattn_igate_kernel, L0_xattn_igate_bias, L0_xattn_fgate_kernel, L0_xattn_fgate_bias, L0_xattn_outnorm_scale, L0_ffn_router_w, L0_ffn_w1, L0_ffn_b1, L0_ffn_w2, L0_ffn_b2, L1_attn_Wq, L1_attn_Wk, L1_attn_Wv, L1_attn_Wo, L1_attn_norm_w, L1_xattn_Wq, L1_xattn_bq, L1_xattn_Wk, L1_xattn_bk, L1_xattn_Wv, L1_xattn_bv, L1_xattn_Wo, L1_xattn_bo, L1_ffn_w1_w, L1_ffn_w1_s, L1_ffn_w2_w, L1_ffn_w2_s, L1_ffn_h1_w, L1_ffn_h1_s, L1_ffn_h2_w, L1_ffn_h2_s, L1_ffn_w3_w, L1_ffn_w3_s):
    import jax
    import jax.numpy as jnp

    def _L0_attn_ref(x, W, ln_gamma, ln_beta, eta, lam_logit):
        import jax, jax.numpy as jnp
        import numpy as np
        B, L, D, H = (4, 512, 128, 16)
        LN_EPS = 1e-05

        def _gated_delta_rule(q, k, v, lam, beta, d):

            def step(S, inp):
                k_t, v_t, q_t = inp
                S = lam * S
                u = beta * (v_t - jnp.einsum('kv,k->v', S, k_t))
                S = S + k_t[:, None] * u[None, :]
                o = jnp.einsum('kv,k->v', S, q_t)
                return (S, o)

            def scan_one(k_h, v_h, q_h):
                S0 = jnp.zeros((d, d), dtype=q.dtype)
                _, o = jax.lax.scan(step, S0, (k_h, v_h, q_h))
                return o
            return jax.vmap(scan_one)(k, v, q)
        Bx, Lx, Dx = x.shape
        d = Dx // H
        lam = jax.nn.sigmoid(lam_logit)
        beta = eta * (1.0 - lam) / d
        x_act = jnp.tanh(x)
        static_out = jnp.einsum('bld,ed->ble', x_act, W)

        def to_heads(t):
            return t.reshape(Bx, Lx, H, d).transpose(0, 2, 1, 3).reshape(Bx * H, Lx, d)
        q = to_heads(x_act)
        k = q
        v = to_heads(static_out)
        o = _gated_delta_rule(q, k, v, lam, beta, d)
        o_dyn = o.reshape(Bx, H, Lx, d).transpose(0, 2, 1, 3).reshape(Bx, Lx, Dx)
        y = static_out + o_dyn
        mu = jnp.mean(y, axis=-1, keepdims=True)
        var = jnp.mean(jnp.square(y - mu), axis=-1, keepdims=True)
        return (y - mu) * jax.lax.rsqrt(var + LN_EPS) * ln_gamma + ln_beta

    def _L0_xattn_ref(q, k, v, igate_kernel, igate_bias, fgate_kernel, fgate_bias, outnorm_scale):
        import jax, jax.numpy as jnp
        import numpy as np
        B, S, H, NH = (2, 256, 128, 4)
        DH = H // NH
        EPS = 1e-06

        def _parallel_stabilized(qh, kh, vh, ig, fg):
            log_fg = jax.nn.log_sigmoid(fg)
            cs = jnp.cumsum(log_fg, axis=2)
            ltr = jnp.tril(jnp.ones((qh.shape[2], qh.shape[2]), dtype=bool))
            log_fg_mat = jnp.where(ltr, cs - jnp.swapaxes(cs, 2, 3), -jnp.inf)
            log_D = log_fg_mat + jnp.swapaxes(ig, 2, 3)
            max_log_D = jnp.max(log_D, axis=-1, keepdims=True)
            D = jnp.exp(log_D - max_log_D)
            qk = jnp.einsum('bhsd,bhtd->bhst', qh, kh) / jnp.sqrt(jnp.float32(DH))
            C = qk * D
            normalizer = jnp.maximum(jnp.abs(jnp.sum(C, axis=-1, keepdims=True)), jnp.exp(-max_log_D))
            return jnp.einsum('bhst,bhtd->bhsd', C / (normalizer + EPS), vh)
        Bq, Sq, Hq = q.shape
        x = jnp.concatenate([q, k, v], axis=-1)
        ig = x @ igate_kernel + igate_bias
        fg = x @ fgate_kernel + fgate_bias
        ig = jnp.transpose(ig, (0, 2, 1))[..., None]
        fg = jnp.transpose(fg, (0, 2, 1))[..., None]
        qh = jnp.transpose(q.reshape(Bq, Sq, NH, DH), (0, 2, 1, 3))
        kh = jnp.transpose(k.reshape(Bq, Sq, NH, DH), (0, 2, 1, 3))
        vh = jnp.transpose(v.reshape(Bq, Sq, NH, DH), (0, 2, 1, 3))
        h = _parallel_stabilized(qh, kh, vh, ig, fg)
        mean = jnp.mean(h, axis=-1, keepdims=True)
        var = jnp.mean((h - mean) ** 2, axis=-1, keepdims=True)
        h_norm = (h - mean) * jax.lax.rsqrt(var + 1e-05)
        h_norm = h_norm * outnorm_scale.reshape(1, NH, 1, DH)
        out = jnp.transpose(h_norm, (0, 2, 1, 3)).reshape(Bq, Sq, Hq)
        return out

    def _L0_ffn_ref(h, router_w, w1, b1, w2, b2):
        import jax, jax.numpy as jnp
        import numpy as np
        B, S, D, E, F = (2, 256, 128, 14, 256)
        Bb, Ss, Dd = h.shape
        x = h.reshape(-1, Dd)
        logits = x @ router_w
        assignments = jnp.argmax(logits, axis=-1)
        probs = jax.nn.softmax(logits, axis=-1)
        weights = jnp.take_along_axis(probs, assignments[:, None], axis=1)[:, 0]
        hid = jnp.einsum('nd,edf->nef', x, w1) + b1
        hid = jax.nn.gelu(hid, approximate=False)
        all_out = jnp.einsum('nef,efd->ned', hid, w2) + b2
        sel = jnp.take_along_axis(all_out, assignments[:, None, None], axis=1)[:, 0, :]
        moe_out = (sel * weights[:, None]).reshape(Bb, Ss, Dd)
        return moe_out

    def _L1_attn_ref(hidden_states, Wq, Wk, Wv, Wo, norm_w):
        import jax, jax.numpy as jnp
        import numpy as np
        CHUNK = 64
        NORM_EPS = 1e-05
        DENOM_EPS = 1.0
        B, S, HID, H = (4, 512, 128, 8)
        D = HID // H

        def rmsnorm(x, w, eps=NORM_EPS):
            var = jnp.mean(x * x, axis=-1, keepdims=True)
            return x * jax.lax.rsqrt(var + eps) * w

        def chunked_linear_attn(q, k, v):
            b, s, h, d = q.shape
            n = s // CHUNK

            def to_chunks(x):
                return x.reshape(b, n, CHUNK, h, d).transpose(1, 0, 3, 2, 4)
            qc, kc, vc = (to_chunks(q), to_chunks(k), to_chunks(v))
            mask = jnp.tril(jnp.ones((CHUNK, CHUNK), dtype=q.dtype))

            def step(state, inp):
                qq, kk, vv = inp
                inter = jnp.einsum('bhcd,bhde->bhce', qq, state)
                scores = jnp.einsum('bhcd,bhed->bhce', qq, kk) * mask
                intra = jnp.einsum('bhce,bhed->bhcd', scores, vv)
                state = state + jnp.einsum('bhcd,bhce->bhde', kk, vv)
                return (state, inter + intra)
            init = jnp.zeros((b, h, d, d), dtype=q.dtype)
            _, o = jax.lax.scan(step, init, (qc, kc, vc))
            return o.transpose(1, 0, 3, 2, 4).reshape(b, s, h, d)
        b, s, _ = hidden_states.shape
        q = jnp.einsum('bsd,ed->bse', hidden_states, Wq).reshape(b, s, H, D)
        k = jnp.einsum('bsd,ed->bse', hidden_states, Wk).reshape(b, s, H, D)
        v = jnp.einsum('bsd,ed->bse', hidden_states, Wv).reshape(b, s, H, D)
        o = chunked_linear_attn(q, k, v)
        z = jnp.cumsum(k, axis=1)
        denom = jnp.maximum(jnp.abs(jnp.sum(q * z, axis=-1)), DENOM_EPS)[..., None]
        o = o / denom
        o = rmsnorm(o, norm_w)
        o = o.reshape(b, s, H * D)
        return jnp.einsum('bse,de->bsd', o, Wo)

    def _L1_xattn_ref(query, key, value, Wq, bq, Wk, bk, Wv, bv, Wo, bo):
        import jax, jax.numpy as jnp
        import numpy as np
        D_MODEL = 128
        NUM_HEADS = 16
        HEAD_DIM = D_MODEL // NUM_HEADS
        B, S = (4, 256)
        b = query.shape[0]
        Q = (query @ Wq + bq).reshape(b, -1, NUM_HEADS, HEAD_DIM).transpose(0, 2, 1, 3)
        K = (key @ Wk + bk).reshape(b, -1, NUM_HEADS, HEAD_DIM).transpose(0, 2, 1, 3)
        V = (value @ Wv + bv).reshape(b, -1, NUM_HEADS, HEAD_DIM).transpose(0, 2, 1, 3)
        scores = jnp.einsum('bhqd,bhkd->bhqk', Q, K) / jnp.sqrt(jnp.asarray(HEAD_DIM, dtype=jnp.float32))
        attn = jax.nn.softmax(scores, axis=-1)
        out = jnp.einsum('bhqk,bhkd->bhqd', attn, V)
        out = out.transpose(0, 2, 1, 3).reshape(b, -1, D_MODEL)
        return out @ Wo + bo

    def _L1_ffn_ref(x, w1_w, w1_s, w2_w, w2_s, h1_w, h1_s, h2_w, h2_s, w3_w, w3_s):
        import jax, jax.numpy as jnp
        import numpy as np
        D_IN, D_HID = (128, 512)

        def _ternary(key, shape):
            return jax.random.randint(key, shape, -1, 2).astype(jnp.float32)

        def _tlin(x, w, s):
            return jnp.einsum('bsi,oi->bso', x, w) * s
        h = jax.nn.silu(_tlin(x, w1_w, w1_s)) * _tlin(x, w2_w, w2_s)
        h = jax.nn.gelu(_tlin(h, h1_w, h1_s), approximate=False)
        h = jax.nn.gelu(_tlin(h, h2_w, h2_s), approximate=False)
        return _tlin(h, w3_w, w3_s)
    x = _layernorm(x + _L0_attn_ref(x, L0_attn_W, L0_attn_ln_gamma, L0_attn_ln_beta, L0_attn_eta, L0_attn_lam_logit), axis=-1)
    x = _layernorm(x + _L0_xattn_ref(x, ctx_1024, ctx_1024, L0_xattn_igate_kernel, L0_xattn_igate_bias, L0_xattn_fgate_kernel, L0_xattn_fgate_bias, L0_xattn_outnorm_scale), axis=-1)
    x = _layernorm(x + _L0_ffn_ref(x, L0_ffn_router_w, L0_ffn_w1, L0_ffn_b1, L0_ffn_w2, L0_ffn_b2), axis=-1)
    x = _layernorm(x + _L1_attn_ref(x, L1_attn_Wq, L1_attn_Wk, L1_attn_Wv, L1_attn_Wo, L1_attn_norm_w), axis=-1)
    x = _layernorm(x + _L1_xattn_ref(x, ctx_1024, ctx_1024, L1_xattn_Wq, L1_xattn_bq, L1_xattn_Wk, L1_xattn_bk, L1_xattn_Wv, L1_xattn_bv, L1_xattn_Wo, L1_xattn_bo), axis=-1)
    x = _layernorm(x + _L1_ffn_ref(x, L1_ffn_w1_w, L1_ffn_w1_s, L1_ffn_w2_w, L1_ffn_w2_s, L1_ffn_h1_w, L1_ffn_h1_s, L1_ffn_h2_w, L1_ffn_h2_s, L1_ffn_w3_w, L1_ffn_w3_s), axis=-1)
    return x

_drawn_inputs = setup_inputs


def setup_inputs(seed=0):
    import zlib

    import numpy as np

    out = dict(_drawn_inputs(seed))
    spreads = {'L0_attn_ln_gamma': (1.0, 0.2),
     'L0_attn_ln_beta': (0.0, 0.1),
     'L0_xattn_outnorm_scale': (1.0, 0.2),
     'L0_ffn_b1': (0.0, 0.8),
     'L0_ffn_b2': (0.0, 0.8),
     'L1_attn_norm_w': (1.0, 0.2),
     'L1_xattn_bq': (0.0, 0.404),
     'L1_xattn_bk': (0.0, 0.8),
     'L1_xattn_bv': (0.0, 0.1),
     'L1_xattn_bo': (0.0, 0.1)}
    factors = {'L0_xattn_igate_bias': 8.0,
     'L1_ffn_w1_w': 8.0,
     'L1_ffn_w1_s': 8.0,
     'L1_ffn_w2_w': 8.0,
     'L1_ffn_w2_s': 8.0,
     'L1_ffn_h1_w': 8.0,
     'L1_ffn_h1_s': 8.0,
     'L1_ffn_h2_w': 8.0,
     'L1_ffn_h2_s': 8.0,
     'L1_ffn_w3_w': 8.0,
     'L1_ffn_w3_s': 8.0}
    for name, (base, spread) in spreads.items():
        noise = np.random.default_rng([zlib.crc32(name.encode()), seed]).standard_normal(out[name].shape)
        drawn = base * np.exp(spread * noise) if base else spread * noise
        out[name] = jnp.asarray(drawn.astype(out[name].dtype))
    for name, factor in factors.items():
        out[name] = (out[name] * factor).astype(out[name].dtype)
    return out
```

```python
from contextlib import ExitStack

import numpy as np

import concourse.bass as bass
import concourse.mybir as mybir

F32 = mybir.dt.float32
BF16 = mybir.dt.bfloat16
I32 = mybir.dt.int32
ALU = mybir.AluOpType
ACT = mybir.ActivationFunctionType
AX = mybir.AxisListType

P = 128
D = 128
NB = 4
S = 256
T = NB * S
NT = T // P
HALVES = S // P
DH = 8
C = 16
NJ = S // C
XH, XD = 4, 32
E, FF = 14, 256
LH, LD = 8, 16
AH, AD = 16, 8
HID = 512
LN_EPS = 1e-5
MASKED = -float(2 ** 15)

CONST = {}


def const_table():
    p = np.arange(P)[:, None]
    q = np.arange(P)[None, :]
    t = np.arange(C)
    parts = {
        "ident": (p == q),
        "bones": (p // DH == q // DH),
        "causal": np.concatenate([p <= q, np.ones((P, P)), p <= q], 1),
        "hm32": (p % 32 // DH == np.arange(32)[None, :] // DH),
        "pw": np.broadcast_to(t[None, :] + 1, (P, C)),
        "lag": np.broadcast_to(t[None, 1:], (P, C - 1)),
        "age": np.where(p % 32 < C, C - 1 - p % 32, 0),
        "hm4": (p // XD == np.arange(XH)[None, :]),
        "hm8": (p // LD == np.arange(LH)[None, :]),
        "rank": np.broadcast_to(E - np.arange(E)[None, :], (P, E)),
    }
    cols, at = [], 0
    for name, a in parts.items():
        a = np.asarray(a, np.float32)
        CONST[name] = (at, at + a.shape[1])
        at += a.shape[1]
        cols.append(a)
    return np.concatenate(cols, 1)


const_table()
NCONST = max(b for _, b in CONST.values())


def decoder(nc, x, ctx, xT_d, ctxT_d, consts, cbf, w, out):
    es = ExitStack()
    with es:
        def sb(name, shape, dt=F32):
            return es.enter_context(nc.sbuf_tensor(name, shape, dt))

        def sem(name):
            return es.enter_context(nc.semaphore(name))

        cst = sb("cst", [P, NCONST])

        def K(name):
            a, b = CONST[name]
            return cst[:, a:b]

        cb = sb("cb", [P, 2 * P + 16 * P], BF16)
        ident_bf = cb[:, 0:P]
        neg_bf = cb[:, P:2 * P]
        sel_bf = cb[:, 2 * P:].rearrange("p (k m) -> p k m", m=P)

        xT = sb("xT", [P, T])
        xN = sb("xN", [P, NT, D])
        zN = sb("zN", [P, NT, D])
        aN = sb("aN", [P, NT, D])
        bN = sb("bN", [P, NT, D])
        ctxT = sb("ctxT", [P, T])
        ctxN = sb("ctxN", [P, NT, D])
        arena = sb("arena", [P, (C - 1) * T])
        ps = es.enter_context(nc.psum_tensor("ps", [P, 8, 512], F32))

        stats = sb("stats", [P, NT, 6])
        mv = sb("mv", [P, NT, 2])
        rs_v = sb("rs_v", [P, 64])
        rs_t = sb("rs_t", [P, 64])
        rs_y = sb("rs_y", [P, 64])

        ld_c = sem("ld_consts")
        ld_x = sem("ld_x")
        ld_w0 = sem("ld_w0")
        ld_ctx = sem("ld_ctx")
        ld_w1 = sem("ld_w1")
        ld_moe = sem("ld_moe")
        ld_l1 = sem("ld_l1")
        ld_ffn = sem("ld_ffn")
        pool_init = sem("pool_init")
        v = sem("dve_step")
        ln_out = sem("ln_out")
        xt_ps = sem("xt_ps")
        xt_sb = sem("xt_sb")
        fin = sem("stored")
        steps = {"n": 0}

        W0 = sb("W0", [P, D])
        lamb = sb("lamb", [P, 2])
        g0 = sb("g0", [P, 2, D])
        wg = sb("wg", [P, 3, 2 * XH])
        wgb = sb("wgb", [P, 2 * XH])
        ons = sb("ons", [P, D])
        wr = sb("wr", [P, E])
        w1 = sb("w1", [P, E, FF])
        w2 = sb("w2", [P, 2, E, D])
        b1 = sb("b1", [E, FF])
        b2 = sb("b2", [E, D])
        l1w = sb("l1w", [P, 4, D])
        nrm = sb("nrm", [P, LD])
        axw = sb("axw", [P, 4, D])
        abq = sb("abq", [P, 2])
        abr = sb("abr", [P, 2, D])
        fw1 = sb("fw1", [P, HID])
        fw2 = sb("fw2", [P, HID])
        fh1 = arena[:, 10 * T:12 * T].rearrange("p (k f) -> p k f", f=HID)
        fh2 = arena[:, 12 * T:14 * T].rearrange("p (k f) -> p k f", f=HID)
        fw3 = sb("fw3", [P, 4, D])
        fsc = sb("fsc", [P, 4, 4])
        fs3 = sb("fs3", [P, D])

        u_scr = nc.dram_tensor("u_scr", [NB, S, D], F32, kind="Internal").ap()
        q_scr = nc.dram_tensor("q_scr", [2, NB, 3, AD, AH * S], BF16, kind="Internal").ap()

        block = es.enter_context(nc.Block())

        NPR = NB * NJ * (C - 1)
        work = sb("work", [P, 8 * T + 4 * NPR])
        kT = work[:, 0:T]
        kN = work[:, T:2 * T].rearrange("p (n d) -> p n d", d=D)
        kd = work[:, 2 * T:4 * T].rearrange("p (j d) -> p j d", d=D)
        X = work[:, 4 * T:6 * T].rearrange("p (v t) -> p v t", v=2)
        Uall = work[:, 6 * T:8 * T].rearrange("p (j d) -> p j d", d=D)
        prod = work[:, 8 * T:8 * T + 2 * NPR].rearrange("p (s c) -> p s c", s=2)
        tmp = work[:, 8 * T + 2 * NPR:]
        S4 = sb("S4", [P, NB, 32])
        pwt = sb("pwt", [P, 2 * C])
        sc = sb("sc", [P, 12])
        nbl = sb("nbl", [P, C - 1])
        npw = sb("npw", [P, C])
        kap = sb("kap", [P, NT * 16])
        Nn = arena[:, :].rearrange("p (l t) -> p l t", t=T)

        lam_e = sem("lam_e")
        lam_ln = sem("lam_ln")
        lam_dve = sem("lam_dve")
        lam_pw = sem("lam_pw")
        tanh_k = sem("tanh_k")
        v_ps = sem("v_ps")
        v_sb = sem("v_sb")
        scal_ok = sem("scal_ok")
        pr_ok = sem("pair_products")
        n_ps = sem("n_ps")
        n_sb = sem("n_sb")
        fs_ok = sem("forward_substituted")
        ch_u = sem("chain_u_ps")
        ch_us = sem("chain_u_sb")
        ch_s = sem("chain_s_ps")
        ch_ss = sem("chain_s_sb")
        u_out = sem("u_out")
        u_in = sem("u_in")
        vn_ps = sem("vn_ps")
        y_done = sem("y_done")

        N_LAGS = C - 1
        n_of = [NJ * NB // 2 * (C - d) for d in range(1, C)]

        def sync_program(e):
            e.dma_start(lamb[:, 0:1], w["lam_logit"].partition_broadcast(P)).then_inc(ld_x, 16)
            e.dma_start(lamb[:, 1:2], w["eta"].partition_broadcast(P)).then_inc(ld_x, 16)
            e.dma_start(cst[:, :], consts).then_inc(ld_c, 16)
            e.dma_start(kT[:, :], xT_d).then_inc(ld_x, 16)
            e.dma_start(W0[:, :], w["W0T"]).then_inc(ld_w0, 16)
            for b in range(NB):
                e.dma_start(kd[32 * b:32 * b + C, :, :],
                            x[b * S:(b + 1) * S, :].rearrange("(j t) d -> t j d", t=C)).then_inc(ld_x, 16)
            e.dma_start(xN[:, :, :], x.rearrange("(n p) d -> p n d", p=P)).then_inc(ld_x, 16)
            e.dma_start(g0[:, 0, :], w["ln_gamma"].partition_broadcast(P)).then_inc(ld_w0, 16)
            e.dma_start(g0[:, 1, :], w["ln_beta"].partition_broadcast(P)).then_inc(ld_w0, 16)
            e.dma_start(cb[:, :], cbf.bitcast(BF16)).then_inc(ld_ctx, 16)
            e.dma_start(ctxT[:, :], ctxT_d).then_inc(ld_ctx, 16)
            e.dma_start(ctxN[:, :, :], ctx.rearrange("(n p) d -> p n d", p=P)).then_inc(ld_ctx, 16)
            e.dma_start(wg[:, :, 0:XH], w["igate_kernel"].rearrange("(g p) h -> p g h", p=P)).then_inc(ld_w1, 16)
            e.dma_start(wg[:, :, XH:], w["fgate_kernel"].rearrange("(g p) h -> p g h", p=P)).then_inc(ld_w1, 16)
            e.dma_start(wgb[:, 0:XH], w["igate_bias"].partition_broadcast(P)).then_inc(ld_w1, 16)
            e.dma_start(wgb[:, XH:], w["fgate_bias"].partition_broadcast(P)).then_inc(ld_w1, 16)
            e.dma_start(ons[:, :], w["outnorm_scale"].partition_broadcast(P)).then_inc(ld_w1, 16)
            e.dma_start(wr[:, :], w["router_w"]).then_inc(ld_moe, 16)
            e.dma_start(b1[:, :], w["b1"]).then_inc(ld_moe, 16)
            e.dma_start(b2[:, :], w["b2"]).then_inc(ld_moe, 16)
            e.dma_start(w1[:, :, :], w["w1"].rearrange("e d f -> d e f")).then_inc(ld_moe, 16)
            for half in range(2):
                e.dma_start(w2[:, half, :, :],
                            w["w2"].rearrange("e (c p) d -> c p e d", p=P)[half]).then_inc(ld_moe, 16)
            for i, n in enumerate(("lqT", "lkT", "lvT", "loT")):
                e.dma_start(l1w[:, i, :], w[n]).then_inc(ld_l1, 16)
            e.dma_start(nrm[:, :], w["norm_w"].partition_broadcast(P)).then_inc(ld_l1, 16)
            for i, n in enumerate(("aWq", "aWk", "aWv", "aWo")):
                e.dma_start(axw[:, i, :], w[n]).then_inc(ld_l1, 16)
            e.dma_start(abq[:, :], w["abqk"]).then_inc(ld_l1, 16)
            for i, n in enumerate(("abv", "abo")):
                e.dma_start(abr[:, i, :], w[n].partition_broadcast(P)).then_inc(ld_l1, 16)
            e.dma_start(fw1[:, :], w["w1T"]).then_inc(ld_ffn, 16)
            e.dma_start(fw2[:, :], w["w2T"]).then_inc(ld_ffn, 16)
            e.wait_ge(fs_ok, 1)
            e.dma_start(fh1[:, :, :], w["h1T"].rearrange("(k p) f -> p k f", p=P)).then_inc(ld_ffn, 16)
            e.dma_start(fh2[:, :, :], w["h2T"].rearrange("(k p) f -> p k f", p=P)).then_inc(ld_ffn, 16)
            e.dma_start(fw3[:, :, :], w["w3T"].rearrange("(k p) d -> p k d", p=P)).then_inc(ld_ffn, 16)
            e.dma_start(fsc[:, :, :], w["hidden_scales"].rearrange("p (i k) -> p i k", i=4)).then_inc(ld_ffn, 16)
            e.dma_start(fs3[:, :], w["w3_s"].partition_broadcast(P)).then_inc(ld_ffn, 16)
            e.wait_ge(ch_us, NJ)
            for b in range(NB):
                e.dma_start(u_scr[b].rearrange("(j t) d -> t j d", t=C),
                            Uall[32 * b:32 * b + C, :, :]).then_inc(u_out, 16)
            e.wait_ge(u_out, 16 * NB)
            e.dma_start(aN[:, :, :], u_scr.rearrange("b (n p) d -> p (b n) d", p=P)).then_inc(u_in, 16)
            for f in phases["sync"]:
                f(e)
            sync_tail(e)

        def done(ins, wait=True):
            steps["n"] += 1
            ins.then_inc(v, 1)
            if wait:
                nc.vector.wait_ge(v, steps["n"])

        def rsqrt(src, n):
            e = nc.vector
            done(e.tensor_scalar(rs_t[:, 0:n].bitcast(I32), src.bitcast(I32), 1, None, ALU.logical_shift_right))
            done(e.tensor_scalar(rs_y[:, 0:n].bitcast(I32), rs_t[:, 0:n].bitcast(I32), -1.0, 1597463007.0,
                                 ALU.mult, ALU.add))
            for _ in range(3):
                done(e.tensor_tensor(rs_t[:, 0:n], rs_y[:, 0:n], rs_y[:, 0:n], ALU.mult))
                done(e.scalar_tensor_tensor(rs_t[:, 0:n], rs_t[:, 0:n], -0.5, src, ALU.mult, ALU.mult))
                done(e.scalar_tensor_tensor(rs_y[:, 0:n], rs_t[:, 0:n], 1.5, rs_y[:, 0:n], ALU.add, ALU.mult))

        def norm_stats(src):
            e = nc.vector
            for n in range(NT):
                done(e.bn_stats(stats[:, n, :], src[:, n, :]), wait=(n == NT - 1))
            for n in range(NT):
                done(e.bn_aggr(mv[:, n, :], stats[:, n, :]), wait=(n == NT - 1))
            done(e.tensor_scalar(rs_v[:, 0:NT], mv[:, :, 1], LN_EPS, None, ALU.add))
            rsqrt(rs_v[:, 0:NT], NT)

        def layer_norm(src, dst, last_sem=None):
            norm_stats(src)
            for n in range(NT):
                i = nc.vector.tensor_scalar(dst[:, n, :], src[:, n, :], mv[:, n, 0:1], rs_y[:, n:n + 1],
                                            ALU.subtract, ALU.mult)
                if last_sem is None:
                    done(i, wait=(n == NT - 1))
                else:
                    i.then_inc(last_sem, 1)

        turns = {"pe": 0, "act": 0}

        def pe_turn(src, ready, base):
            k = turns["pe"]
            turns["pe"] += 1
            for n in range(NT):
                nc.tensor.wait_ge(ready, base + n + 1)
                if k and n == 0:
                    nc.tensor.wait_ge(xt_sb, 2 * k)
                nc.tensor.transpose(ps[:, 6 + n // 4, (n % 4) * P:(n % 4 + 1) * P], src[:, n, :],
                                    K("ident")).then_inc(xt_ps, 1)

        def act_turn(dst):
            k = turns["act"]
            turns["act"] += 1
            for h in range(2):
                nc.scalar.wait_ge(xt_ps, NT * k + 4 * (h + 1))
                nc.scalar.copy(dst[:, h * 512:(h + 1) * 512], ps[:, 6 + h, :]).then_inc(xt_sb, 1)

        def pool_delta(e):
            e.memset(S4[:, :, :], 0.0).then_inc(pool_init, 1)

        def act_delta(e):
            e.wait_ge(ld_x, 16 * 8)
            e.activation(kT[:, :], kT[:, :], ACT.Tanh).then_inc(tanh_k, 1)
            e.wait_ge(lam_dve, 1)
            e.activation(sc[:, 3:4], sc[:, 0:1], ACT.Exp, scale=-1.0).then_inc(lam_e, 1)
            e.activation(sc[:, 4:5], lamb[:, 0:1], ACT.Exp, scale=-1.0).then_inc(lam_e, 1)
            e.activation(kN[:, :, :], xN[:, :, :], ACT.Tanh).then_inc(tanh_k, 1)
            for b in range(NB):
                q = slice(32 * b, 32 * b + C)
                e.activation(kd[q, :, :], kd[q, :, :], ACT.Tanh).then_inc(tanh_k, 1)
            e.wait_ge(lam_e, 1)
            e.activation(sc[:, 5:6], sc[:, 3:4], ACT.Ln, bias=1.0).then_inc(lam_ln, 1)
            e.wait_ge(lam_dve, 2)
            e.activation(pwt[:, :], cst[:, CONST["pw"][0]:CONST["age"][1]], ACT.Exp,
                         scale=sc[:, 6:7]).then_inc(lam_pw, 1)
            for h in range(2):
                e.wait_ge(v_ps, h + 1)
                e.copy(X[:, 0, h * 512:(h + 1) * 512], ps[:, h, :]).then_inc(v_sb, 1)
            e.wait_ge(scal_ok, 1)
            i = 0
            for lag in range(1, C):
                for h in range(2):
                    e.wait_ge(n_ps, i + 1)
                    dst = Nn[:, lag - 1, :].rearrange("p (c t) -> p c t", t=C)[:, 32 * h:32 * h + 32, lag:]
                    e.activation(dst, ps[:, 2 + i % 4, 0:n_of[lag - 1]].rearrange("p (c t) -> p c t", c=32),
                                 ACT.Copy, scale=nbl[:, lag - 1:lag]).then_inc(n_sb, 1)
                    i += 1

        def dve_delta(e):
            e.memset(ps[:, :, :], 0.0).then_inc(pool_init, 1)
            e.wait_ge(ld_x, 16 * 8)
            done(e.scalar_tensor_tensor(sc[:, 0:1], lamb[:, 0:1], -1.0, lamb[:, 0:1], ALU.mult, ALU.max), wait=False)
            done(e.tensor_scalar(sc[:, 1:2], lamb[:, 0:1], 0.0, None, ALU.min))
            e.nop().then_inc(lam_dve, 1)
            e.wait_ge(lam_e, 2)
            done(e.tensor_scalar(sc[:, 7:8], sc[:, 4:5], 1.0, None, ALU.add))
            done(e.reciprocal(sc[:, 8:9], sc[:, 7:8]))
            done(e.tensor_scalar(sc[:, 9:10], sc[:, 8:9], -1.0, 1.0, ALU.mult, ALU.add))
            done(e.tensor_scalar(sc[:, 9:10], sc[:, 9:10], lamb[:, 1:2], 1.0 / DH, ALU.mult, ALU.mult))
            done(e.tensor_scalar(sc[:, 10:11], sc[:, 9:10], -1.0, None, ALU.mult))
            e.wait_ge(lam_ln, 1)
            e.tensor_tensor(sc[:, 6:7], sc[:, 1:2], sc[:, 5:6], ALU.subtract).then_inc(lam_dve, 1)
            e.wait_ge(tanh_k, 1)
            e.wait_ge(ld_c, 16)

            def k3(a, b):
                return kT[:, :].rearrange("p (c t) -> p c t", t=C)[:, :, a:b]

            def products(lag):
                if lag > 2:
                    e.wait_ge(n_ps, 2 * (lag - 2))
                e.tensor_tensor(prod[:, lag % 2, 0:2 * n_of[lag - 1]].rearrange("p (c t) -> p c t", c=NB * NJ),
                                k3(lag, C), k3(0, C - lag), ALU.mult).then_inc(pr_ok, 1)

            products(1)
            products(2)
            e.wait_ge(lam_pw, 1)
            done(e.tensor_scalar(nbl[:, :], pwt[:, C:2 * C - 1], sc[:, 10:11], None, ALU.mult))
            done(e.tensor_scalar(npw[:, :], pwt[:, 0:C], -1.0, None, ALU.mult))
            done(e.tensor_scalar(sc[:, 11:12], pwt[:, 2 * C - 1:2 * C], sc[:, 9:10], None, ALU.mult))
            e.nop().then_inc(scal_ok, 1)
            for lag in range(3, C):
                products(lag)
            done(e.tensor_tensor(X[:, 1, :].rearrange("p (c t) -> p c t", t=C), k3(0, C),
                                 npw[:, :].unsqueeze(1).broadcast_to([P, NB * NJ, C]), ALU.mult))
            e.wait_ge(tanh_k, 6)
            for b in range(NB):
                q = slice(32 * b, 32 * b + C)
                done(e.tensor_scalar(kd[q, :, :], kd[q, :, :], sc[q, 11:12], None, ALU.mult), wait=(b == 3))
            done(e.tensor_tensor(bN[:, :, :], kN[:, :, :], kN[:, :, :], ALU.mult))
            done(e.tensor_reduce(kap[:, :], bN[:, :, :].rearrange("p n (h k) -> p (n h) k", k=DH), AX.X, ALU.add))
            done(e.tensor_scalar(kap[:, :], kap[:, :], sc[:, 10:11], 1.0, ALU.mult, ALU.add))
            e.wait_ge(v_sb, 2)
            e.wait_ge(n_sb, 2 * N_LAGS)
            Xc = X[:, :, :].rearrange("p v (c t) -> p v c t", t=C)
            for s in range(C - 1):
                n = C - 1 - s
                pairs = bass.AP(arena, s + 1, [[(C - 1) * T, P], [0, 2], [C, NB * NJ], [T + 1, n]])
                t4 = tmp[:, 0:2 * NB * NJ * n].rearrange("p (v c t) -> p v c t", v=2, c=NB * NJ)
                for a in range(2):
                    done(e.tensor_tensor(t4[:, a], pairs[:, a], Xc[:, a, :, s:s + 1].broadcast_to([P, NB * NJ, n]),
                                         ALU.mult), wait=(a == 1))
                last = e.tensor_tensor(Xc[:, :, :, s + 1:], Xc[:, :, :, s + 1:], t4, ALU.add)
                done(last)
            e.nop().then_inc(fs_ok, 1)
            for j in range(NJ):
                e.wait_ge(ch_u, j + 1)
                e.tensor_copy(Uall[:, j, :].rearrange("p (g c) -> p g c", g=4), ps[:, 0:4, 0:32]).then_inc(ch_us, 1)
                if j == NJ - 1:
                    break
                e.wait_ge(ch_s, j + 1)
                t3 = tmp[:, 0:NB * 32].rearrange("p (b c) -> p b c", b=NB)
                done(e.tensor_tensor(t3, ps[:, 4:8, 0:32], K("hm32").unsqueeze(1).broadcast_to([P, NB, 32]), ALU.mult))
                e.scalar_tensor_tensor(S4[:, :, :], S4[:, :, :], pwt[:, C - 1:C], t3, ALU.mult, ALU.add).then_inc(ch_ss, 1)

        def pe_delta(e):
            e.wait_ge(tanh_k, 1)
            e.wait_ge(ld_w0, 16 * 3)
            e.wait_ge(ld_c, 16)
            e.wait_ge(pool_init, 2)
            for h in range(2):
                e.matmul(ps[:, h, :], W0[:, :], kT[:, h * 512:(h + 1) * 512], start=True, stop=True).then_inc(v_ps, 1)
            i = 0
            for lag in range(1, C):
                e.wait_ge(pr_ok, lag)
                for h in range(2):
                    if i >= 4:
                        e.wait_ge(n_sb, i - 3)
                    n = n_of[lag - 1]
                    e.matmul(ps[:, 2 + i % 4, 0:n], K("bones"), prod[:, lag % 2, h * n:(h + 1) * n],
                             start=True, stop=True).then_inc(n_ps, 1)
                    i += 1
            e.wait_ge(fs_ok, 1)
            for j in range(NJ):
                if j:
                    e.wait_ge(ch_us, j)
                for b in range(NB):
                    for g in range(4):
                        q = slice(32 * g, 32 * g + 32)
                        c0 = b * S + j * C
                        m = e.matmul(ps[32 * b:32 * b + C, g, 0:32], X[q, 0, c0:c0 + C], cst[q, CONST["ident"][0] + 32 * g:CONST["ident"][0] + 32 * g + 32],
                                     start=True, stop=(j == 0))
                if j:
                    e.wait_ge(ch_ss, j)
                    for b in range(NB):
                        for g in range(4):
                            q = slice(32 * g, 32 * g + 32)
                            c0 = b * S + j * C
                            m = e.matmul(ps[32 * b:32 * b + C, g, 0:32], X[q, 1, c0:c0 + C], S4[q, b, :],
                                         start=False, stop=True)
                m.then_inc(ch_u, 1)
                if j == NJ - 1:
                    break
                e.wait_ge(ch_us, j + 1)
                for b in range(NB):
                    q = slice(32 * b, 32 * b + C)
                    for g in range(4):
                        m = e.matmul(ps[32 * g:32 * g + 32, 4 + b, 0:32], kd[q, j, 32 * g:32 * g + 32],
                                     Uall[q, j, 32 * g:32 * g + 32], start=True, stop=True)
                m.then_inc(ch_s, 1)
            e.wait_ge(ch_us, NJ)
            for n in range(NT):
                m = e.matmul(ps[:, n // 4, (n % 4) * P:(n % 4 + 1) * P], kT[:, n * P:(n + 1) * P], W0[:, :],
                             start=True, stop=True)
            m.then_inc(vn_ps, 1)

        def dve_delta_out(e):
            e.wait_ge(u_in, 16)
            done(e.tensor_tensor(aN[:, :, :].rearrange("p n (h k) -> p (n h) k", k=DH),
                                 aN[:, :, :].rearrange("p n (h k) -> p (n h) k", k=DH),
                                 kap[:, :].unsqueeze(2).broadcast_to([P, NT * 16, DH]), ALU.mult))
            e.wait_ge(vn_ps, 1)
            done(e.scalar_tensor_tensor(zN[:, :, :].rearrange("p n d -> p (n d)"),
                                        ps[:, 0:2, :].rearrange("p b c -> p (b c)"), 2.0,
                                        aN[:, :, :].rearrange("p n d -> p (n d)"), ALU.mult, ALU.subtract))
            layer_norm(zN, aN)
            e.wait_ge(ld_w0, 16 * 3)
            done(e.tensor_tensor(aN[:, :, :], aN[:, :, :], g0[:, 0:1, :].broadcast_to([P, NT, D]), ALU.mult), wait=False)
            done(e.tensor_tensor(bN[:, :, :], xN[:, :, :], g0[:, 1:2, :].broadcast_to([P, NT, D]), ALU.add))
            done(e.tensor_tensor(zN[:, :, :], aN[:, :, :], bN[:, :, :], ALU.add))
            layer_norm(zN, xN, ln_out)

        phases = {"sync": [], "pool": [pool_delta], "act": [act_delta], "dve": [dve_delta, dve_delta_out], "pe": [pe_delta]}

        def turn(n_before):
            def pe(e):
                pe_turn(xN, ln_out, NT * n_before)

            def act(e):
                act_turn(xT)
            phases["pe"].append(pe)
            phases["act"].append(act)

        turn(0)


        wgc = sb("wgc", [P, 2 * XH])
        gc = sb("gc", [P, NT, 2 * XH])
        gt = sb("gt", [P, NT, 2 * XH])
        nf = sb("nf", [P, NT, XH])
        af = sb("af", [P, NT, XH])
        lf = sb("lf", [P, HALVES, 16])
        gg = sb("gg", [P, HALVES, 16])
        cs = sb("cs", [P, HALVES, 16])
        enm = sb("enm", [P, HALVES, 16])
        gT = sb("gT", [16, S])
        mT = sb("mT", [16, 2, S])
        m3 = sb("m3", [96, S], BF16)
        mp = sb("mp", [16, 2, S], BF16)
        Qz = arena[:, 0:8 * T].rearrange("p (h t) -> p h t", t=T)
        Va = arena[:, 8 * T:10 * T].rearrange("p (n h k) -> p n h k", n=NT, h=XH)
        Dm = work[:, 6 * T:6 * T + 768].rearrange("p (s c) -> p s c", s=2)
        CT = work[:, 6 * T + 768:6 * T + 1536].rearrange("p (s c) -> p s c", s=2)
        Osb = work[:, 8 * T:9 * T]
        nrm_s = sb("nrm_s", [P, HALVES, 16])
        nrm_a = sb("nrm_a", [P, HALVES, 16])
        hs1 = sb("hs1", [P, 64])
        gate_c = sem("gate_ctx_ps")
        gate_x = sem("gate_x_ps")
        gate_w = sem("gate_w")
        gf_ok = sem("gate_f_split")
        gl_ok = sem("gate_log")
        lf_ok = sem("log_f")
        cs_ps = sem("cs_ps")
        gg_ok = sem("g_ok")
        gT_ps = sem("gT_ps")
        m_ok = sem("m_ok")
        m3_ok = sem("m3_ok")
        mN_ps = sem("mN_ps")
        em_in = sem("em_in")
        em_ok = sem("em_ok")
        va_ok = sem("va_ok")
        qz_ok = sem("qz_ok")
        e_ps = sem("e_ps")
        s_ps = sem("s_ps")
        d_sb = sem("d_sb")
        ct_sb = sem("ct_sb")
        pv_ps = sem("pv_ps")
        o_sb = sem("o_sb")
        t_ps = sem("t_ps")
        h_sb = sem("h_sb")
        NXH = NB * XH

        def pool_mlstm(e):
            e.wait_ge(fs_ok, 1)
            e.memset(Va[:, :, :, XD:], 1.0).then_inc(va_ok, 1)
            e.memset(m3[:, :], 0.0).then_inc(va_ok, 1)
            e.wait_ge(ld_ctx, 48)
            e.tensor_copy(Va[:, :, :, 0:XD], ctxN[:, :, :].rearrange("p n (h k) -> p n h k", k=XD)).then_inc(va_ok, 1)

        def dve_mlstm_gates(e):
            e.wait_ge(ld_w1, 80)
            e.tensor_tensor(wgc[:, :], wg[:, 1, :], wg[:, 2, :], ALU.add).then_inc(gate_w, 1)
            e.wait_ge(gate_c, 1)
            done(e.tensor_tensor(gc[:, :, :], ps[:, 5, 0:64].rearrange("p (n g) -> p n g", n=NT),
                                 wgb[:, :].unsqueeze(1).broadcast_to([P, NT, 2 * XH]), ALU.add))

        def dve_mlstm(e):
            e.wait_ge(xt_sb, 2)
            for h in range(XH):
                e.tensor_scalar(Qz[:, h, :], xT[:, :], K("hm4")[:, h:h + 1], None, ALU.mult).then_inc(qz_ok, 1)
            e.wait_ge(gate_x, 1)
            done(e.tensor_tensor(gt[:, :, :], ps[:, 4, 0:64].rearrange("p (n g) -> p n g", n=NT), gc[:, :, :], ALU.add))
            f = gt[:, :, XH:]
            done(e.tensor_scalar(nf[:, :, :], f, 0.0, None, ALU.min), wait=False)
            done(e.scalar_tensor_tensor(af[:, :, :], f, -1.0, f, ALU.mult, ALU.max))
            e.nop().then_inc(gf_ok, 1)
            e.wait_ge(gl_ok, 2)
            e.tensor_tensor(lf[:, :, :].rearrange("p f (b h) -> p b f h", h=XH),
                            nf[:, :, :].rearrange("p (b f) h -> p b f h", f=HALVES),
                            af[:, :, :].rearrange("p (b f) h -> p b f h", f=HALVES), ALU.subtract).then_inc(lf_ok, 1)
            e.wait_ge(cs_ps, 1)
            done(e.tensor_copy(cs[:, :, :], ps[:, 4, 64:96].rearrange("p (f k) -> p f k", f=HALVES)))
            e.tensor_tensor(gg[:, :, :].rearrange("p f (b h) -> p b f h", h=XH),
                            gt[:, :, 0:XH].rearrange("p (b f) h -> p b f h", f=HALVES),
                            cs[:, :, :].rearrange("p f (b h) -> p b f h", h=XH), ALU.subtract).then_inc(gg_ok, 1)
            e.wait_ge(gT_ps, 1)
            done(e.tensor_copy(gT[:, :], ps[0:16, 5, 0:S]))
            e.tensor_tensor_scan(mT[:, 0, :], gT[:, :], gT[:, :], -3.0e38, ALU.max, ALU.max).then_inc(m_ok, 1)
            e.wait_ge(va_ok, 3)
            e.wait_ge(m_ok, 1)
            done(e.tensor_scalar(mT[:, 1, :], mT[:, 0, :], -1.0, None, ALU.mult))
            done(e.tensor_copy(m3[0:16, :], mT[:, 1, :]))
            done(e.tensor_tensor(mT[:, 1, :], mT[:, 1, :], m3[0:16, :], ALU.subtract))
            done(e.tensor_copy(mp[:, 0, :], mT[:, 1, :]))
            done(e.tensor_tensor(mT[:, 1, :], mT[:, 1, :], mp[:, 0, :], ALU.subtract), wait=False)
            done(e.tensor_copy(m3[32:48, :], mp[:, 0, :]))
            e.tensor_copy(m3[64:80, :], mT[:, 1, :]).then_inc(m3_ok, 1)
            e.wait_ge(mN_ps, 1)
            e.tensor_tensor(enm[:, :, :], ps[:, 5, 256:288].rearrange("p (f k) -> p f k", f=HALVES), cs[:, :, :],
                            ALU.add).then_inc(em_in, 1)

            def weigh(k):
                e.wait_ge(s_ps, k + 1)
                e.wait_ge(d_sb, k + 1)
                if k >= 2:
                    e.wait_ge(pv_ps, k - 1)
                e.scalar_tensor_tensor(CT[:, k % 2, :], ps[:, 2 + k % 2, 0:384], float(XD) ** -0.5, Dm[:, k % 2, :],
                                       ALU.mult, ALU.mult).then_inc(ct_sb, 1)

            def normalise(b):
                e.wait_ge(t_ps, b + 1)
                tt = ps[:, 5, :].rearrange("p (f h k) -> p f h k", f=HALVES, h=XH)
                done(e.tensor_copy(nrm_s[:, :, 0:XH], tt[:, :, :, XD]))
                done(e.scalar_tensor_tensor(nrm_a[:, :, 0:XH], nrm_s[:, :, 0:XH], -1.0, nrm_s[:, :, 0:XH], ALU.mult, ALU.max))
                done(e.tensor_tensor(nrm_a[:, :, 0:XH], nrm_a[:, :, 0:XH], enm[:, :, XH * b:XH * b + XH], ALU.max))
                done(e.tensor_scalar(nrm_a[:, :, 0:XH], nrm_a[:, :, 0:XH], 1e-6, None, ALU.add))
                done(e.reciprocal(nrm_s[:, :, 0:XH], nrm_a[:, :, 0:XH]))
                e.tensor_tensor(aN[:, 2 * b:2 * b + 2, :].rearrange("p f (h k) -> p f h k", k=XD), tt[:, :, :, 0:XD],
                                nrm_s[:, :, 0:XH].unsqueeze(3).broadcast_to([P, HALVES, XH, XD]), ALU.mult).then_inc(h_sb, 1)

            e.wait_ge(em_ok, 1)
            for k in range(NXH):
                weigh(k)
                if k % 4 == 2 and k > 4:
                    normalise(k // 4 - 1)
            normalise(NB - 1)
            e.wait_ge(h_sb, NB)
            g32 = aN[:, :, :].rearrange("p n (h k) -> p (n h) k", k=XD)
            b32 = bN[:, :, :].rearrange("p n (h k) -> p (n h) k", k=XD)
            G = NT * XH
            done(e.tensor_reduce(hs1[:, 0:G], g32, AX.X, ALU.add))
            done(e.tensor_scalar(hs1[:, 0:G], hs1[:, 0:G], 1.0 / XD, None, ALU.mult))
            done(e.tensor_tensor(g32, g32, hs1[:, 0:G].unsqueeze(2).broadcast_to([P, G, XD]), ALU.subtract))
            done(e.tensor_tensor(b32, g32, g32, ALU.mult))
            done(e.tensor_reduce(hs1[:, 0:G], b32, AX.X, ALU.add))
            done(e.tensor_scalar(rs_v[:, 0:G], hs1[:, 0:G], 1.0 / XD, LN_EPS, ALU.mult, ALU.add))
            rsqrt(rs_v[:, 0:G], G)
            done(e.tensor_tensor(g32, g32, rs_y[:, 0:G].unsqueeze(2).broadcast_to([P, G, XD]), ALU.mult))
            done(e.tensor_tensor(aN[:, :, :], aN[:, :, :], ons[:, :].unsqueeze(1).broadcast_to([P, NT, D]), ALU.mult))
            done(e.tensor_tensor(zN[:, :, :], aN[:, :, :], xN[:, :, :], ALU.add))
            layer_norm(zN, xN, ln_out)

        def act_mlstm(e):
            e.wait_ge(gf_ok, 1)
            e.activation(af[:, :, :], af[:, :, :], ACT.Exp, scale=-1.0).then_inc(gl_ok, 1)
            e.wait_ge(gl_ok, 1)
            e.activation(af[:, :, :], af[:, :, :], ACT.Ln, bias=1.0).then_inc(gl_ok, 1)
            e.wait_ge(em_in, 1)
            e.activation(enm[:, :, :], enm[:, :, :], ACT.Exp, scale=-1.0).then_inc(em_ok, 1)

            def decays(k):
                b, h = divmod(k, XH)
                e.wait_ge(e_ps, k + 1)
                if k >= 2:
                    e.wait_ge(ct_sb, k - 1)
                e.activation(Dm[:, k % 2, 0:S], ps[:, k % 2, 0:S], ACT.Exp, bias=gg[:, 0, k:k + 1])
                e.activation(Dm[:, k % 2, S:], ps[:, k % 2, S:384], ACT.Exp, bias=gg[:, 1, k:k + 1]).then_inc(d_sb, 1)

            def take_out(b):
                e.wait_ge(pv_ps, XH * (b + 1))
                if b:
                    e.wait_ge(t_ps, b)
                e.copy(Osb[:, 0:512], ps[:, 4, :]).then_inc(o_sb, 1)

            for k in range(NXH):
                decays(k)
                if k % 4 == 0 and k:
                    take_out(k // 4 - 1)
            take_out(NB - 1)

        def pe_mlstm_gates(e):
            e.wait_ge(gate_w, 1)
            e.wait_ge(ld_ctx, 48)
            for n in range(NT):
                m = e.matmul(ps[:, 5, 8 * n:8 * n + 8], ctxT[:, n * P:(n + 1) * P], wgc[:, :], start=True, stop=True)
            m.then_inc(gate_c, 1)

        def pe_mlstm(e):
            e.wait_ge(xt_sb, 2)
            for n in range(NT):
                m = e.matmul(ps[:, 4, 8 * n:8 * n + 8], xT[:, n * P:(n + 1) * P], wg[:, 0, :], start=True, stop=True)
            m.then_inc(gate_x, 1)
            e.wait_ge(lf_ok, 1)
            e.matmul(ps[:, 4, 64:80], K("causal")[:, 0:P], lf[:, 0, :], start=True, stop=True)
            e.matmul(ps[:, 4, 80:96], K("causal")[:, P:2 * P], lf[:, 0, :], start=True, stop=False)
            e.matmul(ps[:, 4, 80:96], K("causal")[:, 0:P], lf[:, 1, :], start=False, stop=True).then_inc(cs_ps, 1)
            e.wait_ge(gg_ok, 1)
            e.transpose(ps[0:16, 5, 0:P], gg[:, 0, :], K("ident"))
            e.transpose(ps[0:16, 5, P:S], gg[:, 1, :], K("ident")).then_inc(gT_ps, 1)
            e.wait_ge(m_ok, 1)
            e.transpose(ps[:, 5, 256:272], mT[:, 0, 0:P], K("ident")[0:16, 0:16])
            e.transpose(ps[:, 5, 272:288], mT[:, 0, P:S], K("ident")[0:16, 0:16]).then_inc(mN_ps, 1)
            e.wait_ge(m3_ok, 1)
            e.wait_ge(qz_ok, XH)

            def logits(k):
                b, h = divmod(k, XH)
                if k >= 2:
                    e.wait_ge(d_sb, k - 1)
                E_ = ps[:, k % 2, :]
                e.matmul(E_[:, 0:S], sel_bf[0:96, k, :], m3[:, :], start=True, stop=False, skip_group_check=True)
                e.matmul(E_[:, S:384], sel_bf[0:96, k, :], m3[:, P:S], start=False, stop=False, skip_group_check=True)
                e.matmul(E_[:, 0:P], ident_bf, neg_bf, start=False, stop=False, skip_group_check=True)
                e.matmul(E_[:, S:384], ident_bf, neg_bf, start=False, stop=True, skip_group_check=True).then_inc(e_ps, 1)
                if k >= 2:
                    e.wait_ge(ct_sb, k - 1)
                c0 = b * S
                e.matmul(ps[:, 2 + k % 2, 0:S], ctxT[:, c0:c0 + P], Qz[:, h, c0:c0 + S], start=True, stop=True)
                e.matmul(ps[:, 2 + k % 2, S:384], ctxT[:, c0 + P:c0 + S], Qz[:, h, c0 + P:c0 + S],
                         start=True, stop=True).then_inc(s_ps, 1)

            def mix(k):
                b, h = divmod(k, XH)
                if h == 0 and b:
                    e.wait_ge(o_sb, b)
                e.wait_ge(ct_sb, k + 1)
                q, g = slice(64 * (h % 2), 64 * (h % 2) + 64), h // 2
                e.matmul(ps[q, 4, g * S:(g + 1) * S], Va[:, 2 * b, h, :], CT[:, k % 2, 0:S], start=True, stop=True)
                e.matmul(ps[q, 4, g * S + P:(g + 1) * S], Va[:, 2 * b + 1, h, :], CT[:, k % 2, S:384],
                         start=False, stop=True, skip_group_check=True).then_inc(pv_ps, 1)

            def to_tokens(b):
                e.wait_ge(o_sb, b + 1)
                if b:
                    e.wait_ge(h_sb, b)
                else:
                    e.wait_ge(em_in, 1)
                for f in range(HALVES):
                    for g in range(2):
                        i = 2 * f + g
                        m = e.transpose(ps[:, 5, i * P:(i + 1) * P], Osb[:, g * S + f * P:g * S + (f + 1) * P], K("ident"))
                m.then_inc(t_ps, 1)

            for k in range(NXH):
                logits(k)
                if k:
                    mix(k - 1)
                if k % 4 == 1 and k > 4:
                    to_tokens(k // 4 - 1)
            mix(NXH - 1)
            to_tokens(NB - 1)

        phases["pool"].append(pool_mlstm)
        phases["act"].append(act_mlstm)
        phases["dve"] += [dve_mlstm_gates, dve_mlstm]
        phases["pe"] += [pe_mlstm_gates, pe_mlstm]
        turn(1)


        dl = sb("dl", [P, NT, E])
        oh = sb("oh", [P, NT, E])
        mx8 = sb("mx8", [P, 3, NT])
        ohT = work[0:E, 4 * T:5 * T]
        ohTb = work[0:E, 5 * T:5 * T + T // 2].bitcast(BF16)
        xm = work[:, 0:2 * T].rearrange("p (s t) -> p s t", s=2)
        hid = work[:, 2 * T:4 * T].rearrange("p (f t) -> p f t", f=2)
        lg_ps = sem("lg_ps")
        dl_ok = sem("dl_ok")
        ex_ok = sem("ex_ok")
        oh_ok = sem("oh_ok")
        ohT_ps = sem("ohT_ps")
        ohT_ok = sem("ohT_ok")
        mk_ps = sem("mask_ps")
        xm_ok = sem("xm_ok")
        l1_ps = sem("l1_ps")
        hid_ok = sem("hid_ok")
        b2_ps = sem("b2_ps")
        b2_ok = sem("b2_ok")
        l2_ps = sem("l2_ps")
        l2_used = sem("l2_used")
        EG = [(a, min(a + 4, E)) for a in range(0, E, 4)]

        def pe_moe(e):
            e.wait_ge(xt_sb, 4)
            e.wait_ge(ld_moe, 96)
            for n in range(NT):
                m = e.matmul(ps[:, 4, E * n:E * (n + 1)], xT[:, n * P:(n + 1) * P], wr[:, :], start=True, stop=True)
            m.then_inc(lg_ps, 1)
            e.wait_ge(oh_ok, 1)
            for n in range(NT):
                m = e.transpose(ps[0:E, 2 + n // 4, (n % 4) * P:(n % 4 + 1) * P], oh[:, n, :], K("ident"))
            m.then_inc(ohT_ps, 1)
            e.wait_ge(ohT_ok, 2)
            for f in range(2):
                for b in range(2):
                    e.matmul(ps[:, 2 * f + b, :], b1[:, f * P:(f + 1) * P], ohT[:, b * 512:(b + 1) * 512],
                             start=True, stop=False)

            def mask(k):
                if k >= 2:
                    e.wait_ge(xm_ok, k - 1)
                for b in range(2):
                    m = e.matmul(ps[:, 4 + 2 * (k % 2) + b, :], sel_bf[0:E, k, :], ohTb[:, b * 512:(b + 1) * 512],
                                 start=True, stop=True)
                m.then_inc(mk_ps, 1)

            mask(0)
            for k in range(E):
                if k + 1 < E:
                    mask(k + 1)
                e.wait_ge(xm_ok, k + 1)
                for f in range(2):
                    for b in range(2):
                        m = e.matmul(ps[:, 2 * f + b, :], w1[:, k, f * P:(f + 1) * P], xm[:, k % 2, b * 512:(b + 1) * 512],
                                     start=False, stop=(k == E - 1))
                m.then_inc(l1_ps, 1)
            for n in range(NT):
                m = e.matmul(ps[:, 4 + n // 4, (n % 4) * P:(n % 4 + 1) * P], ohT[:, n * P:(n + 1) * P], b2[:, :],
                             start=True, stop=True)
            m.then_inc(b2_ps, 1)
            e.wait_ge(hid_ok, 4)
            e.wait_ge(b2_ok, 1)
            i = 0
            for a, b in EG:
                for n in range(NT):
                    if i >= 8:
                        e.wait_ge(l2_used, i - 7)
                    for f in range(2):
                        m = e.matmul(ps[:, i % 8, 0:(b - a) * D], hid[:, f, n * P:(n + 1) * P],
                                     w2[:, f, a:b, :].rearrange("p e d -> p (e d)"), start=(f == 0), stop=(f == 1))
                    m.then_inc(l2_ps, 1)
                    i += 1

        def act_moe(e):
            e.wait_ge(dl_ok, 1)
            e.activation(bN[:, 0, 0:NT * E].rearrange("p (n e) -> p n e", e=E), dl[:, :, :], ACT.Exp).then_inc(ex_ok, 1)
            e.wait_ge(ohT_ps, 1)
            e.copy(ohT[:, :], ps[0:E, 2:4, :].rearrange("p b c -> p (b c)")).then_inc(ohT_ok, 1)
            e.wait_ge(l1_ps, E)
            for f in range(2):
                for b in range(2):
                    e.activation(hid[:, f, b * 512:(b + 1) * 512], ps[:, 2 * f + b, :], ACT.Gelu).then_inc(hid_ok, 1)

        def dve_moe(e):
            e.wait_ge(lg_ps, 1)
            lg = ps[:, 4, 0:NT * E].rearrange("p (n e) -> p n e", e=E)
            done(e.tensor_reduce(mx8[:, 0, :], lg, AX.X, ALU.max))
            e.tensor_tensor(dl[:, :, :], lg, mx8[:, 0, :].unsqueeze(2).broadcast_to([P, NT, E]), ALU.subtract).then_inc(dl_ok, 1)
            e.wait_ge(dl_ok, 1)
            done(e.tensor_scalar(oh[:, :, :], dl[:, :, :], 0.0, None, ALU.is_equal))
            done(e.tensor_tensor(oh[:, :, :], oh[:, :, :], K("rank").unsqueeze(1).broadcast_to([P, NT, E]), ALU.mult))
            done(e.tensor_reduce(mx8[:, 1, :], oh[:, :, :], AX.X, ALU.max))
            done(e.tensor_tensor(oh[:, :, :], oh[:, :, :], mx8[:, 1, :].unsqueeze(2).broadcast_to([P, NT, E]), ALU.is_equal))
            e.nop().then_inc(oh_ok, 1)
            e.wait_ge(ex_ok, 1)
            done(e.tensor_reduce(mx8[:, 0, :], bN[:, 0, 0:NT * E].rearrange("p (n e) -> p n e", e=E), AX.X, ALU.add))
            done(e.reciprocal(mx8[:, 2, :], mx8[:, 0, :]))
            e.wait_ge(ohT_ok, 1)
            e.tensor_copy(ohTb[:, :], ohT[:, :]).then_inc(ohT_ok, 1)
            for k in range(E):
                e.wait_ge(mk_ps, k + 1)
                if k >= 2:
                    e.wait_ge(l1_ps, k - 1)
                e.tensor_tensor(xm[:, k % 2, :], ps[:, 4 + 2 * (k % 2):6 + 2 * (k % 2), :].rearrange("p b c -> p (b c)"),
                                xT[:, :], ALU.mult).then_inc(xm_ok, 1)
            e.wait_ge(b2_ps, 1)
            e.tensor_copy(aN[:, :, :], ps[:, 4:6, :].rearrange("p b (n d) -> p (b n) d", d=D)).then_inc(b2_ok, 1)
            e.wait_ge(b2_ok, 1)
            i = 0
            for a, b in EG:
                for n in range(NT):
                    e.wait_ge(l2_ps, i + 1)
                    for k in range(a, b):
                        m = e.scalar_tensor_tensor(aN[:, n, :], ps[:, i % 8, (k - a) * D:(k - a + 1) * D], oh[:, n, k:k + 1],
                                                   aN[:, n, :], ALU.mult, ALU.add)
                        if k < b - 1:
                            done(m)
                        else:
                            m.then_inc(l2_used, 1)
                    i += 1
            e.wait_ge(l2_used, i)
            for n in range(NT):
                done(e.scalar_tensor_tensor(zN[:, n, :], aN[:, n, :], mx8[:, 2, n:n + 1], xN[:, n, :], ALU.mult, ALU.add),
                     wait=(n == NT - 1))
            layer_norm(zN, xN, ln_out)

        phases["act"].append(act_moe)
        phases["dve"].append(dve_moe)
        phases["pe"].append(pe_moe)
        turn(2)


        KTs = work[:, 0:T]
        Qs = work[:, T:2 * T]
        oT = work[:, 2 * T:3 * T]
        Vl = arena[:, 8 * T:10 * T].rearrange("p (n h k) -> p n h k", n=NT, h=LH)
        lq_ps = sem("lq_ps")
        lv_ps = sem("lv_ps")
        lq_sb = sem("lq_sb")
        lk_sb = sem("lk_sb")
        lv_sb = sem("lv_sb")
        vl_one = sem("vl_one")
        lz_ok = sem("lz_ok")
        ls_ps = sem("ls_ps")
        lc_sb = sem("lc_sb")
        lo_ps = sem("lo_ps")
        lo_sb = sem("lo_sb")
        lt_ps = sem("lt_ps")
        lh_sb = sem("lh_sb")
        lm_ok = sem("linear_heads_mixed")
        ly_ps = sem("ly_ps")
        NLH = NB * LH

        def pool_linear(e):
            e.wait_ge(pv_ps, NXH)
            e.memset(Vl[:, :, :, LD:], 1.0).then_inc(vl_one, 1)

        def pe_linear(e):
            e.wait_ge(xt_sb, 6)
            e.wait_ge(ld_l1, 16 * 12)
            e.wait_ge(l2_used, 4 * NT)
            for i in range(2):
                for b in range(2):
                    e.matmul(ps[:, 2 * i + b, :], l1w[:, i, :], xT[:, b * 512:(b + 1) * 512], start=True, stop=True).then_inc(lq_ps, 1)
            for n in range(NT):
                m = e.matmul(ps[:, 4 + n // 4, (n % 4) * P:(n % 4 + 1) * P], xT[:, n * P:(n + 1) * P], l1w[:, 2, :],
                             start=True, stop=True)
            m.then_inc(lv_ps, 1)
            e.wait_ge(lz_ok, LH)
            e.wait_ge(lk_sb, 1)
            e.wait_ge(lv_sb, 1)

            def scores(k):
                b, h = divmod(k, LH)
                if k >= 4:
                    e.wait_ge(lc_sb, k - 3)
                c0 = b * S
                e.matmul(ps[:, k % 4, 0:S], KTs[:, c0:c0 + P], Qz[:, h, c0:c0 + S], start=True, stop=True)
                e.matmul(ps[:, k % 4, S:384], KTs[:, c0 + P:c0 + S], Qz[:, h, c0 + P:c0 + S],
                         start=True, stop=True).then_inc(ls_ps, 1)

            def mix(k):
                b, h = divmod(k, LH)
                if h == 0 and b >= 2:
                    e.wait_ge(lo_sb, b - 1)
                e.wait_ge(lc_sb, k + 1)
                q, g = slice(32 * (h % 4), 32 * (h % 4) + 32), h // 4
                e.matmul(ps[q, 4 + b % 2, g * S:(g + 1) * S], Vl[:, 2 * b, h, :], CT[:, k % 2, 0:S], start=True, stop=True)
                e.matmul(ps[q, 4 + b % 2, g * S + P:(g + 1) * S], Vl[:, 2 * b + 1, h, :], CT[:, k % 2, S:384],
                         start=False, stop=True, skip_group_check=True).then_inc(lo_ps, 1)

            def to_tokens(b):
                e.wait_ge(lo_sb, b + 1)
                if b >= 2:
                    e.wait_ge(lh_sb, b - 1)
                for i in range(4):
                    f, g = divmod(i, 2)
                    m = e.transpose(ps[:, 6 + b % 2, i * P:(i + 1) * P], Osb[:, (b % 2) * 512 + g * S + f * P:(b % 2) * 512 + g * S + (f + 1) * P],
                                    K("ident"))
                m.then_inc(lt_ps, 1)

            for k in range(NLH):
                scores(k)
                if k:
                    mix(k - 1)
                if k % LH == 2 and k > LH:
                    to_tokens(k // LH - 1)
            mix(NLH - 1)
            to_tokens(NB - 1)

        def pe_linear_out(e):
            e.wait_ge(xt_sb, 8)
            for n in range(NT):
                m = e.matmul(ps[:, 4 + n // 4, (n % 4) * P:(n % 4 + 1) * P], oT[:, n * P:(n + 1) * P], l1w[:, 3, :],
                             start=True, stop=True)
            m.then_inc(ly_ps, 1)

        def act_linear(e):
            e.wait_ge(lq_ps, 2)
            e.copy(Qs[:, :], ps[:, 0:2, :].rearrange("p b c -> p (b c)")).then_inc(lq_sb, 1)
            e.wait_ge(lq_ps, 4)
            e.copy(KTs[:, :], ps[:, 2:4, :].rearrange("p b c -> p (b c)")).then_inc(lk_sb, 1)
            e.wait_ge(lv_ps, 1)
            e.wait_ge(vl_one, 1)
            e.copy(Vl[:, :, :, 0:LD], ps[:, 4:6, :].rearrange("p b (n h k) -> p (b n) h k", h=LH, k=LD)).then_inc(lv_sb, 1)
            for b in range(NB):
                e.wait_ge(lo_ps, LH * (b + 1))
                if b >= 2:
                    e.wait_ge(lt_ps, b - 1)
                e.copy(Osb[:, (b % 2) * 512:(b % 2) * 512 + 512], ps[:, 4 + b % 2, :]).then_inc(lo_sb, 1)

        def dve_linear(e):
            e.wait_ge(lq_sb, 1)
            for h in range(LH):
                e.tensor_scalar(Qz[:, h, :], Qs[:, :], K("hm8")[:, h:h + 1], None, ALU.mult).then_inc(lz_ok, 1)

            def normalise(b):
                e.wait_ge(lt_ps, b + 1)
                tt = ps[:, 6 + b % 2, :].rearrange("p (f h k) -> p f h k", f=HALVES, h=LH)
                su, ab = nrm_s[:, :, 0:LH], nrm_a[:, :, 0:LH]
                done(e.tensor_copy(su, tt[:, :, :, LD]))
                done(e.scalar_tensor_tensor(ab, su, -1.0, su, ALU.mult, ALU.max))
                done(e.tensor_scalar(ab, ab, 1.0, None, ALU.max))
                done(e.reciprocal(su, ab))
                e.tensor_tensor(aN[:, 2 * b:2 * b + 2, :].rearrange("p f (h k) -> p f h k", k=LD), tt[:, :, :, 0:LD],
                                su.unsqueeze(3).broadcast_to([P, HALVES, LH, LD]), ALU.mult).then_inc(lh_sb, 1)

            for k in range(NLH):
                e.wait_ge(ls_ps, k + 1)
                if k >= 2:
                    e.wait_ge(lo_ps, k - 1)
                e.tensor_tensor(CT[:, k % 2, :], ps[:, k % 4, 0:384], K("causal"), ALU.mult).then_inc(lc_sb, 1)
                if k % LH == 3 and k > LH:
                    normalise(k // LH - 1)
            normalise(NB - 1)
            e.wait_ge(lh_sb, NB)
            g16 = aN[:, :, :].rearrange("p n (h k) -> p (n h) k", k=LD)
            b16 = bN[:, :, :].rearrange("p n (h k) -> p (n h) k", k=LD)
            G = NT * LH
            done(e.tensor_tensor(b16, g16, g16, ALU.mult))
            done(e.tensor_reduce(hs1[:, 0:G], b16, AX.X, ALU.add))
            done(e.tensor_scalar(rs_v[:, 0:G], hs1[:, 0:G], 1.0 / LD, LN_EPS, ALU.mult, ALU.add))
            rsqrt(rs_v[:, 0:G], G)
            done(e.tensor_tensor(g16, g16, rs_y[:, 0:G].unsqueeze(2).broadcast_to([P, G, LD]), ALU.mult))
            done(e.tensor_tensor(g16, g16, nrm[:, :].unsqueeze(1).broadcast_to([P, G, LD]), ALU.mult))
            e.nop().then_inc(lm_ok, NT)
            e.wait_ge(ly_ps, 1)
            done(e.tensor_tensor(zN[:, :, :], ps[:, 4:6, :].rearrange("p b (n d) -> p (b n) d", d=D), xN[:, :, :], ALU.add))
            layer_norm(zN, xN, ln_out)

        def turn_heads(ready):
            phases["pe"].append(lambda e: pe_turn(aN, ready, 0))
            phases["act"].append(lambda e: act_turn(oT))

        phases["pool"].append(pool_linear)
        phases["act"].append(act_linear)
        phases["dve"].append(dve_linear)
        phases["pe"].append(pe_linear)
        turn_heads(lm_ok)
        phases["pe"].append(pe_linear_out)
        turn(3)


        NR = 9 * AD
        qf = work[:, 0:T]
        kf = work[:, T:2 * T]
        qp = work[:, 3 * T:4 * T + T // 2].bitcast(BF16).rearrange("p (c t) -> p c t", c=3)
        kp = work[:, 4 * T + T // 2:6 * T].bitcast(BF16).rearrange("p (c t) -> p c t", c=3)
        qr = work[:, 6 * T:7 * T]
        kr = work[:, 7 * T:8 * T]
        Qt = [arena[:, (4 + 2 * i) * T:(6 + 2 * i) * T].bitcast(BF16).rearrange("p (h t) -> p h t", h=AH) for i in range(2)]
        Kt = [arena[:, 8 * T:10 * T].bitcast(BF16).rearrange("p (h t) -> p h t", h=AH),
              work[:, 9 * T:11 * T].bitcast(BF16).rearrange("p (h t) -> p h t", h=AH)]
        Vx = arena[:, 0:4 * T].rearrange("p (n h k) -> p n h k", n=NT, h=AH)
        Pb = work[:, 6 * T:8 * T].rearrange("p (s c) -> p s c", s=4)
        Ox = work[:, 8 * T:9 * T]
        mS = sb("mS", [P, 2, 32])
        mt = sb("mt", [32, 2, P])
        mb = sb("mb", [32, 2, 3, P], BF16)
        xb = sb("xb", [P, NT, D])
        bq8 = sb("bq8", [P, 1])
        aq_ps = sem("aq_ps")
        av_ps = sem("av_ps")
        bq_ok = sem("bq_ok")
        aq_sb = sem("aq_sb")
        slot_clear = sem("slot_clear")
        av_sb = sem("av_sb")
        vx_one = sem("vx_one")
        qp_ok = sem("qp_ok")
        kp_ok = sem("kp_ok")
        qp_out = sem("qp_out")
        slot_ld = [sem("slot_ld0"), sem("slot_ld1")]
        as_ps = sem("as_ps")
        as_used = sem("as_used")
        am_ps = sem("am_ps")
        am_parts = sem("am_parts")
        am_row = [sem("am_row0"), sem("am_row1")]
        at_ps = sem("at_ps")
        ap_sb = sem("ap_sb")
        ao_ps = sem("ao_ps")
        ao_sb = sem("ao_sb")
        ac_ps = sem("ac_ps")
        ah_sb = sem("ah_sb")
        ax_ok = sem("ax_ok")
        ay_ps = sem("ay_ps")
        NSJ = 2 * AH // 2

        def pool_softmax(e):
            e.wait_ge(lv_sb, 1)
            e.wait_ge(lo_ps, NLH)
            e.memset(Qt[0][:, :, :], 0.0).then_inc(slot_clear, 1)
            e.memset(Kt[0][:, :, :], 1.0).then_inc(slot_clear, 1)
            e.memset(Qt[1][:, :, :], 0.0).then_inc(slot_clear, 1)
            e.memset(Kt[1][:, :, :], 1.0).then_inc(slot_clear, 1)
            e.memset(Vx[:, :, :, AD:], 1.0).then_inc(vx_one, 1)

        def pe_softmax(e):
            e.wait_ge(xt_sb, 10)
            for i, src in enumerate((xT, ctxT)):
                for b in range(2):
                    e.matmul(ps[:, 2 * i + b, :], axw[:, i, :], src[:, b * 512:(b + 1) * 512], start=True, stop=True).then_inc(aq_ps, 1)
            for n in range(NT):
                m = e.matmul(ps[:, 4 + n // 4, (n % 4) * P:(n % 4 + 1) * P], ctxT[:, n * P:(n + 1) * P], axw[:, 2, :],
                             start=True, stop=True)
            m.then_inc(av_ps, 1)
            e.wait_ge(av_sb, 1)
            e.wait_ge(aq_sb, 2)

            def score(s):
                b, r = divmod(s, NSJ)
                f, hp = divmod(r, AH // 2)
                if s >= 2:
                    e.wait_ge(as_used, s - 1)
                for h in range(2):
                    m = e.matmul(ps[:, s % 2, h * S:(h + 1) * S], Qt[b % 2][0:NR, 2 * hp + h, f * P:(f + 1) * P],
                                 Kt[b % 2][0:NR, 2 * hp + h, :], start=True, stop=True)
                m.then_inc(as_ps, 1)

            def turn_max(b):
                e.wait_ge(as_used, NSJ * (b + 1))
                if b >= 2:
                    e.wait_ge(ah_sb, b - 1)
                e.transpose(ps[0:32, 6, 0:P], mS[:, b % 2, :], K("ident")).then_inc(am_ps, 1)

            def logits(t):
                b, h = divmod(t, AH)
                if t >= 2:
                    e.wait_ge(ap_sb, t - 1)
                if h == 0:
                    e.wait_ge(am_row[b % 2], 48 * (b // 2 + 1))
                for f in range(HALVES):
                    m = e.matmul(ps[:, 2 + t % 2, f * S:(f + 1) * S], Kt[b % 2][:, h, f * P:(f + 1) * P], Qt[b % 2][:, h, :],
                                 start=True, stop=True)
                m.then_inc(at_ps, 1)

            def mix(t):
                b, h = divmod(t, AH)
                e.wait_ge(ap_sb, t + 1)
                if h == 0 and b:
                    e.wait_ge(ao_sb, b)
                q, g = slice(32 * (h % 4), 32 * (h % 4) + 32), h // 4
                for f in range(HALVES):
                    m = e.matmul(ps[q, 4 + g // 2, (g % 2) * S:(g % 2 + 1) * S], Vx[:, 2 * b + f, h, :],
                                 Pb[:, t % 4, f * S:(f + 1) * S], start=(f == 0), stop=(f == 1))
                m.then_inc(ao_ps, 1)

            def to_tokens(b):
                e.wait_ge(ao_sb, b + 1)
                if b:
                    e.wait_ge(ah_sb, b)
                e.wait_ge(am_parts, 3 * min(b + 2, NB))
                for i in range(8):
                    f, g = divmod(i, 4)
                    m = e.transpose(ps[:, 6 + f, g * P:(g + 1) * P], Ox[:, g * S + f * P:g * S + (f + 1) * P], K("ident"))
                m.then_inc(ac_ps, 1)

            for b in range(-1, NB):
                if b + 1 < NB:
                    e.wait_ge(slot_ld[(b + 1) % 2], 16 * 4 * ((b + 1) // 2 + 1))
                for r in range(AH):
                    if b + 1 < NB and r < NSJ // 2:
                        score((b + 1) * NSJ + 2 * r)
                        score((b + 1) * NSJ + 2 * r + 1)
                    if r == AH // 2 + 1 and b + 1 < NB:
                        turn_max(b + 1)
                    if b >= 0:
                        logits(b * AH + r)
                        if r:
                            mix(b * AH + r - 1)
                        if r == 3 and b:
                            to_tokens(b - 1)
                if b >= 0:
                    mix(b * AH + AH - 1)
            to_tokens(NB - 1)

        def pe_softmax_out(e):
            e.wait_ge(xt_sb, 12)
            for n in range(NT):
                m = e.matmul(ps[:, 4 + n // 4, (n % 4) * P:(n % 4 + 1) * P], oT[:, n * P:(n + 1) * P], axw[:, 3, :],
                             start=True, stop=True)
            m.then_inc(ay_ps, 1)

        def act_softmax(e):
            e.wait_ge(bq_ok, 1)
            e.wait_ge(aq_ps, 2)
            e.activation(qf, ps[:, 0:2, :].rearrange("p b c -> p (b c)"), ACT.Identity, bias=bq8[:, :],
                         scale=float(AD) ** -0.5).then_inc(aq_sb, 1)
            e.wait_ge(aq_ps, 4)
            e.activation(kf, ps[:, 2:4, :].rearrange("p b c -> p (b c)"), ACT.Identity, bias=abq[:, 1:2]).then_inc(aq_sb, 1)
            for t in range(NB * AH):
                e.wait_ge(at_ps, t + 1)
                if t >= 4:
                    e.wait_ge(ao_ps, t - 3)
                e.activation(Pb[:, t % 4, :], ps[:, 2 + t % 2, :], ACT.Exp).then_inc(ap_sb, 1)
                if t % AH == 1 and t > AH:
                    take(e, t // AH - 1)
            take(e, NB - 1)

        def take(e, b):
            e.wait_ge(ao_ps, AH * (b + 1))
            if b:
                e.wait_ge(ac_ps, b)
            e.copy(Ox[:, :], ps[:, 4:6, :].rearrange("p b c -> p (b c)")).then_inc(ao_sb, 1)

        def dve_softmax(e):
            e.wait_ge(ld_l1, 16 * 12)
            e.tensor_scalar(bq8[:, :], abq[:, 0:1], float(AD) ** -0.5, None, ALU.mult).then_inc(bq_ok, 1)
            e.wait_ge(vx_one, 1)
            e.wait_ge(av_ps, 1)
            for f in range(2):
                i = e.tensor_tensor(Vx[:, 4 * f:4 * f + 4, :, 0:AD], ps[:, 4 + f, :].rearrange("p (n h k) -> p n h k", h=AH, k=AD),
                                    abr[:, 0, :].rearrange("p (h k) -> p h k", k=AD).unsqueeze(1).broadcast_to([P, 4, AH, AD]), ALU.add)
                if f:
                    i.then_inc(av_sb, 1)
            for i, (src, parts, rest, ok) in enumerate(((qf, qp, qr, qp_ok), (kf, kp, kr, kp_ok))):
                e.wait_ge(aq_sb, i + 1)
                done(e.tensor_copy(parts[:, 0, :], src))
                done(e.tensor_tensor(rest, src, parts[:, 0, :], ALU.subtract))
                done(e.tensor_copy(parts[:, 1, :], rest))
                done(e.tensor_tensor(rest, rest, parts[:, 1, :], ALU.subtract))
                e.tensor_copy(parts[:, 2, :], rest).then_inc(ok, 1)
            done(e.tensor_tensor(xb[:, :, :], xN[:, :, :], abr[:, 1:2, :].broadcast_to([P, NT, D]), ALU.add))

            def maxima(s):
                b, r = divmod(s, NSJ)
                f, hp = divmod(r, AH // 2)
                e.wait_ge(as_ps, s + 1)
                if r == 0 and b >= 2:
                    e.wait_ge(am_ps, b - 1)
                e.tensor_reduce(mS[:, b % 2, 4 * hp + f:4 * hp + f + 3:2], ps[:, s % 2, :].rearrange("p (h k) -> p h k", h=2),
                                AX.X, ALU.max, negate=True).then_inc(as_used, 1)

            def parts_of_max(b):
                e.wait_ge(am_ps, b + 1)
                if b >= 2:
                    e.wait_ge(am_row[b % 2], 48 * (b // 2))
                o = mb[:, b % 2]
                done(e.tensor_copy(mt[:, 0, :], ps[0:32, 6, 0:P]))
                for i in range(3):
                    e.tensor_copy(o[:, i, :], mt[:, min(i, 1), :]).then_inc(am_parts, 1)
                    if i < 2:
                        e.wait_ge(am_parts, 3 * b + i + 1)
                        done(e.tensor_tensor(mt[:, 1, :], mt[:, i, :], o[:, i, :], ALU.subtract))

            def normalise(b):
                e.wait_ge(ac_ps, b + 1)
                tt = ps[:, 6:8, :].rearrange("p f (h k) -> p f h k", h=AH)
                done(e.reciprocal(nrm_s[:, :, :], tt[:, :, :, AD]))
                e.tensor_tensor(aN[:, 2 * b:2 * b + 2, :].rearrange("p f (h k) -> p f h k", k=AD), tt[:, :, :, 0:AD],
                                nrm_s[:, :, :].unsqueeze(3).broadcast_to([P, HALVES, AH, AD]), ALU.mult).then_inc(ah_sb, 1)

            for b in range(NB + 1):
                if b < NB:
                    for r in range(NSJ):
                        maxima(b * NSJ + r)
                        if r == AH // 2 + 1 and b >= 2:
                            normalise(b - 2)
                    parts_of_max(b)
            normalise(NB - 2)
            normalise(NB - 1)
            e.wait_ge(ah_sb, NB)
            e.nop().then_inc(ax_ok, NT)
            e.wait_ge(ay_ps, 1)
            done(e.tensor_tensor(zN[:, :, :], ps[:, 4:6, :].rearrange("p b (n d) -> p (b n) d", d=D), xb[:, :, :], ALU.add))
            layer_norm(zN, xN, ln_out)

        def sync_softmax(e):
            for i, (parts, ok) in enumerate(((qp, qp_ok), (kp, kp_ok))):
                e.wait_ge(ok, 1)
                for b in range(NB):
                    e.dma_start(q_scr[i, b].rearrange("c d (h t) -> (d h) c t", t=S),
                                parts[:, :, b * S:(b + 1) * S]).then_inc(qp_out, 16)
            e.wait_ge(qp_out, 16 * 2 * NB)
            e.wait_ge(slot_clear, 4)

            def load_slot(b):
                if b >= 2:
                    e.wait_ge(at_ps, AH * (b - 1))
                q2, k2 = (a[b % 2].rearrange("p h t -> p (h t)") for a in (Qt, Kt))
                for c in range(3):
                    e.dma_start(q2[24 * c:24 * c + 24, :],
                                q_scr[0, b, c].unsqueeze(0).broadcast_to([3, AD, AH * S])).then_inc(slot_ld[b % 2], 16)
                e.dma_start(k2[0:NR, :], q_scr[1, b].rearrange("c d n -> (c d) n").unsqueeze(0)
                            .broadcast_to([3, 3 * AD, AH * S])).then_inc(slot_ld[b % 2], 16)

            def load_max(b):
                for i in range(3):
                    e.wait_ge(am_parts, 3 * b + i + 1)
                    e.dma_start(Qt[b % 2][NR + i:NR + i + 1, :, :].rearrange("o h (f t) -> o (h f) t", f=2),
                                mb[:, b % 2, i, :]).then_inc(am_row[b % 2], 16)

            load_slot(0)
            load_slot(1)
            for b in range(NB):
                load_max(b)
                if b + 2 < NB:
                    load_slot(b + 2)

        phases["sync"].append(sync_softmax)
        phases["pool"].append(pool_softmax)
        phases["act"].append(act_softmax)
        phases["dve"].append(dve_softmax)
        phases["pe"].append(pe_softmax)
        turn_heads(ax_ok)
        phases["pe"].append(pe_softmax_out)
        turn(4)

        fa = work[:, 0:4 * T].rearrange("p (b k t) -> p b k t", b=2, k=4)
        fb = work[:, 4 * T:8 * T].rearrange("p (b k t) -> p b k t", b=2, k=4)
        sg = work[:, 8 * T:10 * T].rearrange("p (s t) -> p s t", s=4)
        g_ps = sem("g_ps")
        u_ps = sem("u_ps")
        sg_ok = sem("sg_ok")
        h1_ok = sem("h1_ok")
        gel_ps = sem("gel_ps")
        gel_ok = sem("gel_ok")
        fy_ps = sem("fy_ps")

        def pe_ffn(e):
            e.wait_ge(xt_sb, 14)
            e.wait_ge(ld_ffn, 16 * 7)
            for j in range(8):
                blk, m = divmod(j, 4)
                if j >= 4:
                    e.wait_ge(h1_ok, j - 3)
                t = slice(blk * 512, (blk + 1) * 512)
                e.matmul(ps[:, 2 * (j % 4), :], fw1[:, m * P:(m + 1) * P], xT[:, t], start=True, stop=True).then_inc(g_ps, 1)
                e.matmul(ps[:, 2 * (j % 4) + 1, :], fw2[:, m * P:(m + 1) * P], xT[:, t], start=True, stop=True).then_inc(u_ps, 1)
            for j in range(16):
                layer, blk, m = j // 8, (j // 4) % 2, j % 4
                if j < 8:
                    e.wait_ge(h1_ok, max(4 * (blk + 1), j // 2 + 5))
                else:
                    e.wait_ge(gel_ok, max(4 * (blk + 1), j - 7))
                wt, src = ((fh1, fa), (fh2, fb))[layer]
                for k in range(4):
                    i = e.matmul(ps[:, j % 8, :], wt[:, k, m * P:(m + 1) * P], src[:, blk, k, :], start=(k == 0), stop=(k == 3))
                i.then_inc(gel_ps, 1)
            for n in range(NT):
                blk = n // 4
                if n % 4 == 0:
                    e.wait_ge(gel_ok, 12 + 4 * blk)
                for k in range(4):
                    i = e.matmul(ps[:, blk, (n % 4) * P:(n % 4 + 1) * P], fa[:, blk, k, (n % 4) * P:(n % 4 + 1) * P], fw3[:, k, :],
                                 start=(k == 0), stop=(k == 3))
                if n % 4 == 3:
                    i.then_inc(fy_ps, 1)

        def act_ffn(e):
            for j in range(8):
                e.wait_ge(g_ps, j + 1)
                if j >= 4:
                    e.wait_ge(h1_ok, j - 3)
                e.activation(sg[:, j % 4, :], ps[:, 2 * (j % 4), :], ACT.Silu, scale=fsc[:, 0, j % 4:j % 4 + 1]).then_inc(sg_ok, 1)
            for j in range(16):
                layer, blk, m = j // 8, (j // 4) % 2, j % 4
                e.wait_ge(gel_ps, j + 1)
                if j >= 8:
                    e.wait_ge(gel_ps, 12 if blk == 0 else 16)
                dst = (fb, fa)[layer]
                e.activation(dst[:, blk, m, :], ps[:, j % 8, :], ACT.Gelu, scale=fsc[:, 2 + layer, m:m + 1]).then_inc(gel_ok, 1)

        def dve_ffn(e):
            for j in range(8):
                e.wait_ge(u_ps, j + 1)
                e.wait_ge(sg_ok, j + 1)
                e.scalar_tensor_tensor(fa[:, j // 4, j % 4, :], ps[:, 2 * (j % 4) + 1, :], fsc[:, 1, j % 4:j % 4 + 1],
                                       sg[:, j % 4, :], ALU.mult, ALU.mult).then_inc(h1_ok, 1)
            for b in range(2):
                e.wait_ge(fy_ps, b + 1)
                q = slice(4 * b, 4 * b + 4)
                done(e.tensor_tensor(aN[:, q, :], ps[:, b, :].rearrange("p (n d) -> p n d", d=D),
                                     fs3[:, :].unsqueeze(1).broadcast_to([P, 4, D]), ALU.mult))
                done(e.tensor_tensor(zN[:, q, :], aN[:, q, :], xN[:, q, :], ALU.add))
            layer_norm(zN, xN, ln_out)

        phases["act"].append(act_ffn)
        phases["dve"].append(dve_ffn)
        phases["pe"].append(pe_ffn)

        def sync_tail(e):
            e.wait_ge(ln_out, NT * N_NORMS[0])
            e.dma_start(out.rearrange("(n p) d -> p n d", p=P), xN[:, :, :]).then_inc(fin, 16)
            e.wait_ge(fin, 16)
            for q, n in final_loads:
                e.wait_ge(q, n)

        final_loads = [(ld_ctx, 48), (ld_w1, 80), (ld_moe, 96), (ld_l1, 16 * 12), (ld_ffn, 16 * 7)]
        N_NORMS = [6]

        @block.sync
        def _(e):
            sync_program(e)

        @block.gpsimd
        def _(e):
            for f in phases["pool"]:
                f(e)

        @block.scalar
        def _(e):
            for f in phases["act"]:
                f(e)

        @block.vector
        def _(e):
            for f in phases["dve"]:
                f(e)

        @block.tensor
        def _(e):
            for f in phases["pe"]:
                f(e)



def _arrays(inputs):

    def by_width(a):
        return np.swapaxes(a.reshape(a.shape[:-1] + (AH, AD)), -1, -2).reshape(a.shape)

    g = {k: np.asarray(a) for k, a in inputs.items()}
    p = np.arange(P)
    c = np.ascontiguousarray
    table = const_table()
    bf = np.zeros((P, 2 * P + 16 * P), np.float32)
    bf[:, 0:P] = np.eye(P)
    bf[:, P:2 * P] = np.where(p[:, None] <= p[None, :], 0, MASKED)
    sel = (p[:, None] % 32 == np.arange(16)[None, :]) & (p[:, None] < 96)
    bf[:, 2 * P:] = np.repeat(sel, P, 1)
    bf = (bf.view(np.uint32) >> 16).astype(np.uint16)
    return {
        "x": c(g["x"].reshape(T, D)), "ctx": c(g["ctx_1024"].reshape(T, D)),
        "xT": c(g["x"].reshape(T, D).T), "ctxT": c(g["ctx_1024"].reshape(T, D).T),
        "consts": table, "cbf": bf,
        "W0T": c(g["L0_attn_W"].T), "ln_gamma": g["L0_attn_ln_gamma"], "ln_beta": g["L0_attn_ln_beta"],
        "lam_logit": g["L0_attn_lam_logit"].reshape(1), "eta": g["L0_attn_eta"].reshape(1),
        "igate_kernel": g["L0_xattn_igate_kernel"], "fgate_kernel": g["L0_xattn_fgate_kernel"],
        "igate_bias": g["L0_xattn_igate_bias"], "fgate_bias": g["L0_xattn_fgate_bias"],
        "outnorm_scale": g["L0_xattn_outnorm_scale"],
        "router_w": g["L0_ffn_router_w"], "w1": g["L0_ffn_w1"], "b1": g["L0_ffn_b1"],
        "w2": g["L0_ffn_w2"], "b2": g["L0_ffn_b2"],
        "lqT": c(g["L1_attn_Wq"].T), "lkT": c(g["L1_attn_Wk"].T), "lvT": c(g["L1_attn_Wv"].T),
        "loT": c(g["L1_attn_Wo"].T), "norm_w": g["L1_attn_norm_w"],
        "aWq": c(by_width(g["L1_xattn_Wq"])), "aWk": c(by_width(g["L1_xattn_Wk"])), "aWv": g["L1_xattn_Wv"], "aWo": g["L1_xattn_Wo"],
        "abqk": c(np.stack([by_width(g["L1_xattn_bq"]), by_width(g["L1_xattn_bk"])], 1)), "abv": g["L1_xattn_bv"], "abo": g["L1_xattn_bo"],
        "w1T": c(g["L1_ffn_w1_w"].T), "w2T": c(g["L1_ffn_w2_w"].T), "h1T": c(g["L1_ffn_h1_w"].T),
        "h2T": c(g["L1_ffn_h2_w"].T), "w3T": c(g["L1_ffn_w3_w"].T),
        "hidden_scales": c(np.concatenate([g["L1_ffn_" + n].reshape(4, P).T for n in ("w1_s", "w2_s", "h1_s", "h2_s")], 1)),
        "w3_s": g["L1_ffn_w3_s"],
    }


def _program(nc, arrays, mybir_):
    a = {n: nc.dram_tensor("in_" + n, v.shape, mybir_.dt.from_np(v.dtype), kind="ExternalInput").ap()
         for n, v in arrays.items()}
    out = nc.dram_tensor("out_y", (T, D), F32, kind="ExternalOutput").ap()
    fixed = ("x", "ctx", "xT", "ctxT", "consts", "cbf")
    decoder(nc, a["x"], a["ctx"], a["xT"], a["ctxT"], a["consts"], a["cbf"],
            {n: v for n, v in a.items() if n not in fixed}, out)


def kernel(**inputs):
    import concourse.bacc as _bacc
    from concourse import mybir as _mybir
    from concourse.bass_utils import run_bass_kernel_spmd as _run

    arrays = _arrays(inputs)
    nc = _bacc.Bacc("TRN2", target_bir_lowering=False, num_devices=1)
    _program(nc, arrays, _mybir)
    r = _run(nc, [{"in_" + n: v for n, v in arrays.items()}], core_ids=[0])
    return np.asarray(r.results[0]["out_y"]).reshape(NB, S, D)
```

```python
from contextlib import ExitStack

import numpy as np

import concourse.bass as bass
import concourse.mybir as mybir

F32 = mybir.dt.float32
BF16 = mybir.dt.bfloat16
I32 = mybir.dt.int32
U32 = mybir.dt.uint32
ALU = mybir.AluOpType
ACT = mybir.ActivationFunctionType
AX = mybir.AxisListType

P = 128
D = 128
NB = 4
S = 256
T = NB * S
NT = T // P
HALVES = S // P
DH = 8
C = 16
NJ = S // C
XH, XD = 4, 32
E, FF = 14, 256
NSEG = (T + E * (P - 1)) // P
LH, LD = 8, 16
AH, AD = 16, 8
HID = 512
LN_EPS = 1e-5
MASKED = -float(2 ** 15)

CONST = {}


def const_table():
    p = np.arange(P)[:, None]
    q = np.arange(P)[None, :]
    t = np.arange(C)
    parts = {
        "ident": (p == q),
        "bones": (p // DH == q // DH),
        "causal": np.concatenate([p <= q, np.ones((P, P)), p <= q], 1),
        "hm32": (p % 32 // DH == np.arange(32)[None, :] // DH),
        "pw": np.broadcast_to(t[None, :] + 1, (P, C)),
        "lag": np.broadcast_to(t[None, 1:], (P, C - 1)),
        "age": np.where(p % 32 < C, C - 1 - p % 32, 0),
        "hm4": (p // XD == np.arange(XH)[None, :]),
        "hm8": (p // LD == np.arange(LH)[None, :]),
        "first": np.broadcast_to(np.arange(E * NT)[None, :] % NT > 0, (P, E * NT)),
        "full": np.broadcast_to(P * np.arange(NT)[None, :], (P, NT)),
        "seg": np.broadcast_to(np.arange(NSEG)[None, :], (P, NSEG)),
        "rank": np.broadcast_to(E - np.arange(E)[None, :], (P, E)),
    }
    cols, at = [], 0
    for name, a in parts.items():
        a = np.asarray(a, np.float32)
        CONST[name] = (at, at + a.shape[1])
        at += a.shape[1]
        cols.append(a)
    return np.concatenate(cols, 1)


const_table()
NCONST = max(b for _, b in CONST.values())


def decoder(nc, x, ctx, xT_d, ctxT_d, consts, cbf, w, out):
    es = ExitStack()
    with es:
        def sb(name, shape, dt=F32):
            return es.enter_context(nc.sbuf_tensor(name, shape, dt))

        def sem(name):
            return es.enter_context(nc.semaphore(name))

        cst = sb("cst", [P, NCONST])

        def K(name):
            a, b = CONST[name]
            return cst[:, a:b]

        cb = sb("cb", [P, 2 * P + 16 * P], BF16)
        ident_bf = cb[:, 0:P]
        neg_bf = cb[:, P:2 * P]
        sel_bf = cb[:, 2 * P:].rearrange("p (k m) -> p k m", m=P)

        xT = sb("xT", [P, T])
        xN = sb("xN", [P, NT, D])
        zN = sb("zN", [P, NT, D])
        aN = sb("aN", [P, NT, D])
        bN = sb("bN", [P, NT, D])
        ctxT = sb("ctxT", [P, T])
        ctxN = sb("ctxN", [P, NT, D])
        arena = sb("arena", [P, (C - 1) * T])
        ps = es.enter_context(nc.psum_tensor("ps", [P, 8, 512], F32))

        stats = sb("stats", [P, NT, 6])
        mv = sb("mv", [P, NT, 2])
        rs_v = sb("rs_v", [P, 64])
        rs_t = sb("rs_t", [P, 64])
        rs_y = sb("rs_y", [P, 64])
        rs_h = sb("rs_h", [P, 64])

        ld_c = sem("ld_consts")
        ld_k = sem("ld_k")
        ld_lam = sem("ld_lam")
        ld_x = sem("ld_x")
        ld_w0 = sem("ld_w0")
        ld_g0 = sem("ld_gamma_beta")
        ld_ctx = sem("ld_ctx")
        ld_w1 = sem("ld_w1")
        ld_moe = sem("ld_moe")
        ld_l1 = sem("ld_l1")
        ld_ffn = sem("ld_ffn")
        pool_init = sem("pool_init")
        v = sem("dve_step")
        ln_out = sem("ln_out")
        xt_ps = sem("xt_ps")
        xt_sb = sem("xt_sb")
        fin = sem("stored")
        zero_ok = sem("zero_ok")
        steps = {"n": 0}

        W0 = sb("W0", [P, D])
        lamb = sb("lamb", [P, 2])
        g0 = sb("g0", [P, 2, D])
        wg = sb("wg", [P, 3, 2 * XH])
        wgb = sb("wgb", [P, 2 * XH])
        ons = sb("ons", [P, D])
        wr = sb("wr", [P, E])
        w1 = sb("w1", [P, E, FF + 2])
        w2 = sb("w2", [P, 2, E, D])
        l1w = sb("l1w", [P, 4, D])
        nrm = sb("nrm", [P, LD])
        axw = sb("axw", [P, 4, D])
        abq = sb("abq", [P, 2])
        abr = sb("abr", [P, 2, D])
        fw1 = sb("fw1", [P, HID])
        fw2 = sb("fw2", [P, HID])
        fh1 = arena[:, 10 * T:12 * T].rearrange("p (k f) -> p k f", f=HID)
        fh2 = arena[:, 12 * T:14 * T].rearrange("p (k f) -> p k f", f=HID)
        fw3 = sb("fw3", [P, 4, D])
        fsc = sb("fsc", [P, 4, 4])
        fs3 = sb("fs3", [P, D])

        zero = sb("zero", [P, D])
        xs_scr = nc.dram_tensor("xs_scr", [NSEG * P, D], F32, kind="Internal").ap()
        ys_scr = nc.dram_tensor("ys_scr", [NSEG * P, D], F32, kind="Internal").ap()
        u_scr = nc.dram_tensor("u_scr", [NB, S, D], F32, kind="Internal").ap()
        q_scr = nc.dram_tensor("q_scr", [2, NB, 3, AD, AH * S], BF16, kind="Internal").ap()

        block = es.enter_context(nc.Block())

        NPR = NB * NJ * (C - 1)
        work = sb("work", [P, 8 * T + 4 * NPR])
        kT = work[:, 0:T]
        kN = work[:, T:2 * T].rearrange("p (n d) -> p n d", d=D)
        kd = work[:, 2 * T:4 * T].rearrange("p (j d) -> p j d", d=D)
        X = work[:, 4 * T:6 * T].rearrange("p (v t) -> p v t", v=2)
        Uall = work[:, 6 * T:8 * T].rearrange("p (j d) -> p j d", d=D)
        prod = work[:, 8 * T:8 * T + 2 * NPR].rearrange("p (s c) -> p s c", s=2)
        tmp = work[:, 8 * T + 2 * NPR:]
        S4 = sb("S4", [P, NB, 32])
        pwt = sb("pwt", [P, 2 * C])
        sc = sb("sc", [P, 12])
        nbl = sb("nbl", [P, C - 1])
        npw = sb("npw", [P, C])
        kap = sb("kap", [P, NT * 16])
        Nn = arena[:, :].rearrange("p (l t) -> p l t", t=T)

        lam_e = sem("lam_e")
        lam_ln = sem("lam_ln")
        lam_dve = sem("lam_dve")
        lam_pw = sem("lam_pw")
        tanh_k = sem("tanh_k")
        kd_tanh = sem("kd_tanh")
        kd_ok = sem("kd_ok")
        kap_ok = sem("kap_ok")
        v_ps = sem("v_ps")
        v_sb = sem("v_sb")
        scal_ok = sem("scal_ok")
        pr_ok = sem("pair_products")
        n_ps = sem("n_ps")
        n_sb = sem("n_sb")
        x_ok = sem("x_ok")
        fs_ok = sem("early_substituted")
        fs_sb = sem("early_in_sbuf")
        fs_late = sem("late_substituted")
        pool_step = sem("pool_step")
        J_DVE = 7
        ch_u = sem("chain_u_ps")
        ch_us = sem("chain_u_sb")
        ch_s = sem("chain_s_ps")
        ch_ss = sem("chain_s_sb")
        u_out = sem("u_out")
        u_in = sem("u_in")
        vn_ps = sem("vn_ps")
        y_done = sem("y_done")

        N_LAGS = C - 1
        n_of = [NJ * NB // 2 * (C - d) for d in range(1, C)]

        def sync_program(e):
            e.dma_start(kT[:, :], xT_d).then_inc(ld_k, 16)
            e.dma_start(lamb[:, 0:1], w["lam_logit"].partition_broadcast(P)).then_inc(ld_lam, 16)
            e.dma_start(lamb[:, 1:2], w["eta"].partition_broadcast(P)).then_inc(ld_lam, 16)
            e.dma_start(cst[:, :], consts).then_inc(ld_c, 16)
            e.dma_start(W0[:, :], w["W0T"]).then_inc(ld_w0, 16)
            for b in range(NB):
                e.dma_start(kd[32 * b:32 * b + C, :, :],
                            x[b * S:(b + 1) * S, :].rearrange("(j t) d -> t j d", t=C)).then_inc(ld_x, 16)
            e.dma_start(xN[:, :, :], x.rearrange("(n p) d -> p n d", p=P)).then_inc(ld_x, 16)
            e.dma_start(g0[:, 0, :], w["ln_gamma"].partition_broadcast(P)).then_inc(ld_g0, 16)
            e.dma_start(g0[:, 1, :], w["ln_beta"].partition_broadcast(P)).then_inc(ld_g0, 16)
            e.dma_start(cb[:, :], cbf.bitcast(BF16)).then_inc(ld_ctx, 16)
            e.dma_start(ctxT[:, :], ctxT_d).then_inc(ld_ctx, 16)
            e.dma_start(ctxN[:, :, :], ctx.rearrange("(n p) d -> p n d", p=P)).then_inc(ld_ctx, 16)
            e.dma_start(wg[:, :, 0:XH], w["igate_kernel"].rearrange("(g p) h -> p g h", p=P)).then_inc(ld_w1, 16)
            e.dma_start(wg[:, :, XH:], w["fgate_kernel"].rearrange("(g p) h -> p g h", p=P)).then_inc(ld_w1, 16)
            e.dma_start(wgb[:, 0:XH], w["igate_bias"].partition_broadcast(P)).then_inc(ld_w1, 16)
            e.dma_start(wgb[:, XH:], w["fgate_bias"].partition_broadcast(P)).then_inc(ld_w1, 16)
            e.dma_start(ons[:, :], w["outnorm_scale"].partition_broadcast(P)).then_inc(ld_w1, 16)
            e.dma_start(wr[:, :], w["router_w"]).then_inc(ld_moe, 16)
            e.wait_ge(zero_ok, 1)
            e.dma_start(xs_scr.rearrange("(s p) d -> p s d", p=P),
                        zero[:, :].unsqueeze(1).broadcast_to([P, NSEG, D])).then_inc(ld_moe, 16)
            e.dma_start(w1[:, :, 0:FF], w["w1"].rearrange("e d f -> d e f")).then_inc(ld_moe, 16)
            e.dma_start(w1[:, :, FF:], w["b1"].rearrange("p (e f) -> p e f", f=2)).then_inc(ld_moe, 16)
            for half in range(2):
                e.dma_start(w2[:, half, :, :],
                            w["w2"].rearrange("e (c p) d -> c p e d", p=P)[half]).then_inc(ld_moe, 16)
            for i, n in enumerate(("lqT", "lkT", "lvT", "loT")):
                e.dma_start(l1w[:, i, :], w[n]).then_inc(ld_l1, 16)
            e.dma_start(nrm[:, :], w["norm_w"].partition_broadcast(P)).then_inc(ld_l1, 16)
            for i, n in enumerate(("aWq", "aWk", "aWv", "aWo")):
                e.dma_start(axw[:, i, :], w[n]).then_inc(ld_l1, 16)
            e.dma_start(abq[:, :], w["abqk"]).then_inc(ld_l1, 16)
            for i, n in enumerate(("abv", "abo")):
                e.dma_start(abr[:, i, :], w[n].partition_broadcast(P)).then_inc(ld_l1, 16)
            e.dma_start(fw1[:, :], w["w1T"]).then_inc(ld_ffn, 16)
            e.dma_start(fw2[:, :], w["w2T"]).then_inc(ld_ffn, 16)
            e.wait_ge(fs_ok, 1)
            e.wait_ge(fs_late, 1)
            e.dma_start(fh1[:, :, :], w["h1T"].rearrange("(k p) f -> p k f", p=P)).then_inc(ld_ffn, 16)
            e.dma_start(fh2[:, :, :], w["h2T"].rearrange("(k p) f -> p k f", p=P)).then_inc(ld_ffn, 16)
            e.dma_start(fw3[:, :, :], w["w3T"].rearrange("(k p) d -> p k d", p=P)).then_inc(ld_ffn, 16)
            e.dma_start(fsc[:, :, :], w["hidden_scales"].rearrange("p (i k) -> p i k", i=4)).then_inc(ld_ffn, 16)
            e.dma_start(fs3[:, :], w["w3_s"].partition_broadcast(P)).then_inc(ld_ffn, 16)
            e.wait_ge(ch_us, NJ)
            for b in range(NB):
                e.dma_start(u_scr[b].rearrange("(j t) d -> t j d", t=C),
                            Uall[32 * b:32 * b + C, :, :]).then_inc(u_out, 16)
            e.wait_ge(u_out, 16 * NB)
            e.dma_start(aN[:, :, :], u_scr.rearrange("b (n p) d -> p (b n) d", p=P)).then_inc(u_in, 16)
            for f in phases["sync"]:
                f(e)
            sync_tail(e)

        def done(ins, wait=True):
            steps["n"] += 1
            ins.then_inc(v, 1)
            if wait:
                nc.vector.wait_ge(v, steps["n"])

        def rsqrt(src, n):
            e = nc.vector
            done(e.tensor_scalar(rs_t[:, 0:n].bitcast(I32), src.bitcast(I32), 1, None, ALU.logical_shift_right))
            done(e.tensor_scalar(rs_y[:, 0:n].bitcast(I32), rs_t[:, 0:n].bitcast(I32), -1.0, 1597463007.0,
                                 ALU.mult, ALU.add))
            y, h, u = rs_y[:, 0:n], rs_h[:, 0:n], rs_t[:, 0:n]
            done(e.scalar_tensor_tensor(h, src, -0.5, y, ALU.mult, ALU.mult))
            for i in range(3):
                done(e.tensor_tensor(u, h, y, ALU.mult))
                if i < 2:
                    done(e.scalar_tensor_tensor(h, u, 1.5, h, ALU.add, ALU.mult), wait=False)
                done(e.scalar_tensor_tensor(y, u, 1.5, y, ALU.add, ALU.mult))

        def norm_stats(src):
            e = nc.vector
            for n in range(NT):
                done(e.bn_stats(stats[:, n, :], src[:, n, :]), wait=(n == NT - 1))
            for n in range(NT):
                done(e.bn_aggr(mv[:, n, :], stats[:, n, :]), wait=(n == NT - 1))
            done(e.tensor_scalar(rs_v[:, 0:NT], mv[:, :, 1], LN_EPS, None, ALU.add))
            rsqrt(rs_v[:, 0:NT], NT)

        def layer_norm(src, dst, last_sem=None):
            norm_stats(src)
            for n in range(NT):
                i = nc.vector.tensor_scalar(dst[:, n, :], src[:, n, :], mv[:, n, 0:1], rs_y[:, n:n + 1],
                                            ALU.subtract, ALU.mult)
                if last_sem is None:
                    done(i, wait=(n == NT - 1))
                else:
                    i.then_inc(last_sem, 1)

        turns = {"pe": 0, "act": 0}

        def pe_turn(src, ready, base):
            k = turns["pe"]
            turns["pe"] += 1
            for n in range(NT):
                nc.tensor.wait_ge(ready, base + n + 1)
                if k and n == 0:
                    nc.tensor.wait_ge(xt_sb, 2 * k)
                nc.tensor.transpose(ps[:, 6 + n // 4, (n % 4) * P:(n % 4 + 1) * P], src[:, n, :],
                                    K("ident")).then_inc(xt_ps, 1)

        def act_turn(dst):
            k = turns["act"]
            turns["act"] += 1
            for h in range(2):
                nc.scalar.wait_ge(xt_ps, NT * k + 4 * (h + 1))
                nc.scalar.copy(dst[:, h * 512:(h + 1) * 512], ps[:, 6 + h, :]).then_inc(xt_sb, 1)

        X_ps = [ps[:, 2 * a:2 * a + 2, :].rearrange("p b c -> p (b c)") for a in (0, 3)]

        def chunks(a, j0, j1):
            return a.rearrange("p (b j t) -> p b j t", b=NB, t=C)[:, :, j0:j1, :]

        def substitute(e, count, base, rhs, scratch, j0, j1):
            nj = j1 - j0
            Xc = [a.rearrange("p (b j t) -> p b j t", b=NB, t=C) for a in rhs]
            n_done = base
            for s in range(C - 1):
                n = C - 1 - s
                pairs = bass.AP(arena, j0 * C + s + 1, [[(C - 1) * T, P], [S, NB], [C, nj], [T + 1, n]])
                for a in range(2):
                    t4 = scratch[:, a * NB * nj * n:(a + 1) * NB * nj * n].rearrange("p (b j t) -> p b j t", b=NB, j=nj)
                    if s:
                        e.wait_ge(count, n_done - 1)
                    e.tensor_tensor(t4, pairs, Xc[a][:, :, j0:j1, s:s + 1].broadcast_to([P, NB, nj, n]),
                                    ALU.mult).then_inc(count, 1)
                    n_done += 1
                for a in range(2):
                    t4 = scratch[:, a * NB * nj * n:(a + 1) * NB * nj * n].rearrange("p (b j t) -> p b j t", b=NB, j=nj)
                    e.wait_ge(count, n_done - 1)
                    row = Xc[a][:, :, j0:j1, s + 1:]
                    i = e.tensor_tensor(row, row, t4, ALU.add)
                    if s == C - 2 and a:
                        e_last = i
                    else:
                        i.then_inc(count, 1)
                        n_done += 1
            return e_last

        def pool_delta(e):
            e.memset(zero[:, :], 0.0).then_inc(zero_ok, 1)
            e.memset(S4[:, :, :], 0.0).then_inc(pool_init, 1)
            e.wait_ge(v_sb, 1)
            e.wait_ge(x_ok, 1)
            e.wait_ge(n_sb, 2 * N_LAGS)
            substitute(e, pool_step, 0, (X[:, 0, :], X[:, 1, :]), prod.rearrange("p s c -> p (s c)"), J_DVE, NJ).then_inc(fs_late, 1)
            e.wait_ge(tanh_k, 2)
            e.tensor_tensor(bN[:, :, :], kN[:, :, :], kN[:, :, :], ALU.mult).then_inc(kap_ok, 1)
            e.wait_ge(kap_ok, 1)
            k8 = bN[:, :, :].rearrange("p n (h k) -> p (n h) k", k=DH)
            for i, n in enumerate((4, 2)):
                e.tensor_tensor(k8[:, :, 0:n], k8[:, :, 0:n], k8[:, :, n:2 * n], ALU.add).then_inc(kap_ok, 1)
                e.wait_ge(kap_ok, 2 + i)
            e.tensor_tensor(kap[:, :], k8[:, :, 0], k8[:, :, 1], ALU.add).then_inc(kap_ok, 1)
            e.wait_ge(kap_ok, 4)
            e.tensor_scalar(kap[:, :], kap[:, :], sc[:, 10:11], 1.0, ALU.mult, ALU.add).then_inc(kap_ok, 1)
            e.wait_ge(ld_g0, 32)
            e.tensor_tensor(bN[:, :, :], xN[:, :, :], g0[:, 1:2, :].broadcast_to([P, NT, D]), ALU.add).then_inc(kap_ok, 1)

        def act_delta(e):
            e.wait_ge(ld_k, 16)
            e.activation(kT[:, :], kT[:, :], ACT.Tanh).then_inc(tanh_k, 1)
            e.wait_ge(lam_dve, 1)
            e.activation(sc[:, 3:4], sc[:, 0:1], ACT.Exp, scale=-1.0).then_inc(lam_e, 1)
            e.activation(sc[:, 4:5], lamb[:, 0:1], ACT.Exp, scale=-1.0).then_inc(lam_e, 1)
            e.wait_ge(lam_e, 1)
            e.activation(sc[:, 5:6], sc[:, 3:4], ACT.Ln, bias=1.0).then_inc(lam_ln, 1)
            e.wait_ge(lam_dve, 2)
            e.wait_ge(ld_c, 16)
            e.activation(pwt[:, :], cst[:, CONST["pw"][0]:CONST["age"][1]], ACT.Exp,
                         scale=sc[:, 6:7]).then_inc(lam_pw, 1)
            e.wait_ge(v_ps, 2)
            e.copy(chunks(X[:, 0, :], J_DVE, NJ), chunks(X_ps[0], J_DVE, NJ)).then_inc(v_sb, 1)
            e.wait_ge(scal_ok, 1)
            i = 0
            for lag in range(1, C):
                for h in range(2):
                    e.wait_ge(n_ps, i + 1)
                    dst = Nn[:, lag - 1, :].rearrange("p (c t) -> p c t", t=C)[:, 32 * h:32 * h + 32, lag:]
                    e.activation(dst, ps[:, 2 + i % 4, 0:n_of[lag - 1]].rearrange("p (c t) -> p c t", c=32),
                                 ACT.Copy, scale=nbl[:, lag - 1:lag]).then_inc(n_sb, 1)
                    i += 1
            e.wait_ge(ld_x, 16 * 5)
            for b in range(NB):
                q = slice(32 * b, 32 * b + C)
                e.activation(kd[q, :, :], kd[q, :, :], ACT.Tanh).then_inc(kd_tanh, 1)
            e.activation(kN[:, :, :], xN[:, :, :], ACT.Tanh).then_inc(tanh_k, 1)
            for b in range(NB):
                q = slice(32 * b, 32 * b + C)
                e.wait_ge(kd_tanh, b + 1)
                e.activation(kd[q, :, :], kd[q, :, :], ACT.Copy, scale=sc[q, 11:12]).then_inc(kd_ok, 1)
            e.wait_ge(fs_ok, 1)
            for a in range(2):
                e.copy(chunks(X[:, a, :], 0, J_DVE), chunks(X_ps[a], 0, J_DVE)).then_inc(fs_sb, 1)

        def dve_delta(e):
            e.wait_ge(ld_lam, 32)
            done(e.scalar_tensor_tensor(sc[:, 0:1], lamb[:, 0:1], -1.0, lamb[:, 0:1], ALU.mult, ALU.max), wait=False)
            done(e.tensor_scalar(sc[:, 1:2], lamb[:, 0:1], 0.0, None, ALU.min))
            e.nop().then_inc(lam_dve, 1)
            e.wait_ge(tanh_k, 1)

            def k3(a, b):
                return kT[:, :].rearrange("p (c t) -> p c t", t=C)[:, :, a:b]

            def products(lag):
                if lag > 2:
                    e.wait_ge(n_ps, 2 * (lag - 2))
                e.tensor_tensor(prod[:, lag % 2, 0:2 * n_of[lag - 1]].rearrange("p (c t) -> p c t", c=NB * NJ),
                                k3(lag, C), k3(0, C - lag), ALU.mult).then_inc(pr_ok, 1)

            products(1)
            e.wait_ge(lam_e, 2)
            done(e.tensor_scalar(sc[:, 7:8], sc[:, 4:5], 1.0, None, ALU.add))
            done(e.reciprocal(sc[:, 8:9], sc[:, 7:8]))
            done(e.tensor_scalar(sc[:, 9:10], sc[:, 8:9], -1.0, 1.0, ALU.mult, ALU.add))
            done(e.tensor_scalar(sc[:, 9:10], sc[:, 9:10], lamb[:, 1:2], 1.0 / DH, ALU.mult, ALU.mult))
            done(e.tensor_scalar(sc[:, 10:11], sc[:, 9:10], -1.0, None, ALU.mult))
            e.wait_ge(lam_ln, 1)
            e.tensor_tensor(sc[:, 6:7], sc[:, 1:2], sc[:, 5:6], ALU.subtract).then_inc(lam_dve, 1)
            products(2)
            e.wait_ge(lam_pw, 1)
            done(e.tensor_scalar(nbl[:, :], pwt[:, C:2 * C - 1], sc[:, 10:11], None, ALU.mult))
            done(e.tensor_scalar(npw[:, :], pwt[:, 0:C], -1.0, None, ALU.mult))
            done(e.tensor_scalar(sc[:, 11:12], pwt[:, 2 * C - 1:2 * C], sc[:, 9:10], None, ALU.mult))
            e.nop().then_inc(scal_ok, 1)
            for lag in range(3, C):
                products(lag)
            for dst, j0, j1 in ((X[:, 1, :], J_DVE, NJ), (X_ps[1], 0, J_DVE)):
                done(e.tensor_tensor(chunks(dst, j0, j1), chunks(kT, j0, j1),
                                     npw[:, :].unsqueeze(1).unsqueeze(1).broadcast_to([P, NB, j1 - j0, C]), ALU.mult))
            e.nop().then_inc(x_ok, 1)
            e.wait_ge(v_sb, 1)
            e.wait_ge(n_sb, 2 * N_LAGS)
            substitute(e, v, steps["n"], X_ps, tmp, 0, J_DVE).then_inc(fs_ok, 1)
            steps["n"] += 4 * (C - 1) - 1
            for j in range(NJ):
                e.wait_ge(ch_u, j + 1)
                e.tensor_copy(Uall[:, j, :].rearrange("p (g c) -> p g c", g=4), ps[:, 0:4, 0:32]).then_inc(ch_us, 1)
                if j == NJ - 1:
                    break
                e.wait_ge(ch_s, j + 1)
                t3 = tmp[:, 0:NB * 32].rearrange("p (b c) -> p b c", b=NB)
                done(e.tensor_tensor(t3, ps[:, 4:8, 0:32], K("hm32").unsqueeze(1).broadcast_to([P, NB, 32]), ALU.mult))
                e.scalar_tensor_tensor(S4[:, :, :], S4[:, :, :], pwt[:, C - 1:C], t3, ALU.mult, ALU.add).then_inc(ch_ss, 1)

        def pe_delta(e):
            e.wait_ge(tanh_k, 1)
            e.wait_ge(ld_w0, 16)
            e.wait_ge(ld_c, 16)
            e.wait_ge(pool_init, 1)
            for h in range(2):
                e.matmul(ps[:, h, :], W0[:, :], kT[:, h * 512:(h + 1) * 512], start=True, stop=True).then_inc(v_ps, 1)
            i = 0
            for lag in range(1, C):
                e.wait_ge(pr_ok, lag)
                for h in range(2):
                    if i >= 4:
                        e.wait_ge(n_sb, i - 3)
                    n = n_of[lag - 1]
                    e.matmul(ps[:, 2 + i % 4, 0:n], K("bones"), prod[:, lag % 2, h * n:(h + 1) * n],
                             start=True, stop=True).then_inc(n_ps, 1)
                    i += 1
            e.wait_ge(fs_sb, 2)
            for j in range(NJ):
                if j == J_DVE:
                    e.wait_ge(fs_late, 1)
                if j:
                    e.wait_ge(ch_us, j)
                for b in range(NB):
                    for g in range(4):
                        q = slice(32 * g, 32 * g + 32)
                        c0 = b * S + j * C
                        m = e.matmul(ps[32 * b:32 * b + C, g, 0:32], X[q, 0, c0:c0 + C], cst[q, CONST["ident"][0] + 32 * g:CONST["ident"][0] + 32 * g + 32],
                                     start=True, stop=(j == 0))
                if j:
                    e.wait_ge(ch_ss, j)
                    for g in range(4):
                        for b in range(NB):
                            q = slice(32 * g, 32 * g + 32)
                            c0 = b * S + j * C
                            m = e.matmul(ps[32 * b:32 * b + C, g, 0:32], X[q, 1, c0:c0 + C], S4[q, b, :],
                                         start=False, stop=True)
                m.then_inc(ch_u, 1)
                if j == NJ - 1:
                    break
                e.wait_ge(ch_us, j + 1)
                if j == 0:
                    e.wait_ge(kd_ok, NB)
                for b in range(NB):
                    q = slice(32 * b, 32 * b + C)
                    for g in range(4):
                        m = e.matmul(ps[32 * g:32 * g + 32, 4 + b, 0:32], kd[q, j, 32 * g:32 * g + 32],
                                     Uall[q, j, 32 * g:32 * g + 32], start=True, stop=True)
                m.then_inc(ch_s, 1)
            e.wait_ge(ch_us, NJ)
            for n in range(NT):
                m = e.matmul(ps[:, n // 4, (n % 4) * P:(n % 4 + 1) * P], kT[:, n * P:(n + 1) * P], W0[:, :],
                             start=True, stop=True)
            m.then_inc(vn_ps, 1)

        def dve_delta_out(e):
            e.wait_ge(u_in, 16)
            e.wait_ge(kap_ok, 6)
            done(e.tensor_tensor(aN[:, :, :].rearrange("p n (h k) -> p (n h) k", k=DH),
                                 aN[:, :, :].rearrange("p n (h k) -> p (n h) k", k=DH),
                                 kap[:, :].unsqueeze(2).broadcast_to([P, NT * 16, DH]), ALU.mult))
            e.wait_ge(vn_ps, 1)
            done(e.scalar_tensor_tensor(zN[:, :, :].rearrange("p n d -> p (n d)"),
                                        ps[:, 0:2, :].rearrange("p b c -> p (b c)"), 2.0,
                                        aN[:, :, :].rearrange("p n d -> p (n d)"), ALU.mult, ALU.subtract))
            layer_norm(zN, aN)
            e.wait_ge(ld_g0, 32)
            done(e.tensor_tensor(aN[:, :, :], aN[:, :, :], g0[:, 0:1, :].broadcast_to([P, NT, D]), ALU.mult))
            done(e.tensor_tensor(zN[:, :, :], aN[:, :, :], bN[:, :, :], ALU.add))
            layer_norm(zN, xN, ln_out)

        phases = {"sync": [], "pool": [pool_delta], "act": [act_delta], "dve": [dve_delta, dve_delta_out], "pe": [pe_delta]}

        LATE = {}

        def turn(n_before):
            def pe(e):
                pe_turn(xN, ln_out, NT * n_before)

            def act(e):
                act_turn(xT)
            phases["pe"].append(pe)
            phases["act"].append(act)

        turn(0)


        wgc = sb("wgc", [P, 2 * XH])
        gc = sb("gc", [P, NT, 2 * XH])
        gt = sb("gt", [P, NT, 2 * XH])
        nf = sb("nf", [P, NT, XH])
        af = sb("af", [P, NT, XH])
        lf = sb("lf", [P, HALVES, 16])
        gg = sb("gg", [P, HALVES, 16])
        cs = sb("cs", [P, HALVES, 16])
        enm = sb("enm", [P, HALVES, 16])
        gT = sb("gT", [16, S])
        mT = sb("mT", [16, 2, S])
        m3 = sb("m3", [96, S], BF16)
        mp = sb("mp", [16, 2, S], BF16)
        Qz = arena[:, 0:8 * T].rearrange("p (h t) -> p h t", t=T)
        Va = arena[:, 8 * T:10 * T].rearrange("p (n h k) -> p n h k", n=NT, h=XH)
        Dm = work[:, 6 * T:6 * T + 768].rearrange("p (s c) -> p s c", s=2)
        CT = work[:, 6 * T + 768:6 * T + 768 + 4 * 384].rearrange("p (s c) -> p s c", s=4)
        Oxs = work[:, 9 * T:9 * T + 512]
        nrm_s = sb("nrm_s", [P, HALVES, 16])
        nrm_a = sb("nrm_a", [P, HALVES, 16])
        hs1 = sb("hs1", [P, 64])
        gate_c = sem("gate_ctx_ps")
        gate_x = sem("gate_x_ps")
        gate_w = sem("gate_w")
        gf_ok = sem("gate_f_split")
        gl_ok = sem("gate_log")
        lf_ok = sem("log_f")
        cs_ps = sem("cs_ps")
        gg_ok = sem("g_ok")
        gT_ps = sem("gT_ps")
        m_ok = sem("m_ok")
        m3_ok = sem("m3_ok")
        mN_ps = sem("mN_ps")
        em_in = sem("em_in")
        em_ok = sem("em_ok")
        va_ok = sem("va_ok")
        qz_ok = sem("qz_ok")
        e_ps = sem("e_ps")
        s_ps = sem("s_ps")
        d_sb = sem("d_sb")
        ct_sb = sem("ct_sb")
        pv_ps = sem("pv_ps")
        o_sb = sem("o_sb")
        t_ps = sem("t_ps")
        h_sb = sem("h_sb")
        NXH = NB * XH

        def pool_mlstm(e):
            e.wait_ge(fs_ok, 1)
            e.wait_ge(fs_late, 1)
            e.memset(Va[:, :, :, XD:], 1.0).then_inc(va_ok, 1)
            e.memset(m3[:, :], 0.0).then_inc(va_ok, 1)
            e.wait_ge(ld_ctx, 48)
            e.tensor_copy(Va[:, :, :, 0:XD], ctxN[:, :, :].rearrange("p n (h k) -> p n h k", k=XD)).then_inc(va_ok, 1)

        def dve_mlstm_gates(e):
            e.wait_ge(ld_w1, 80)
            e.tensor_tensor(wgc[:, :], wg[:, 1, :], wg[:, 2, :], ALU.add).then_inc(gate_w, 1)
            e.wait_ge(gate_c, 1)
            done(e.tensor_tensor(gc[:, :, :], ps[:, 5, 0:64].rearrange("p (n g) -> p n g", n=NT),
                                 wgb[:, :].unsqueeze(1).broadcast_to([P, NT, 2 * XH]), ALU.add))

        def dve_mlstm(e):
            e.wait_ge(xt_sb, 2)
            for h in range(XH):
                e.tensor_scalar(Qz[:, h, :], xT[:, :], K("hm4")[:, h:h + 1], None, ALU.mult).then_inc(qz_ok, 1)
            e.wait_ge(gate_x, 1)
            done(e.tensor_tensor(gt[:, :, :], ps[:, 4, 0:64].rearrange("p (n g) -> p n g", n=NT), gc[:, :, :], ALU.add))
            f = gt[:, :, XH:]
            done(e.tensor_scalar(nf[:, :, :], f, 0.0, None, ALU.min), wait=False)
            done(e.scalar_tensor_tensor(af[:, :, :], f, -1.0, f, ALU.mult, ALU.max))
            e.nop().then_inc(gf_ok, 1)
            e.wait_ge(gl_ok, 2)
            e.tensor_tensor(lf[:, :, :].rearrange("p f (b h) -> p b f h", h=XH),
                            nf[:, :, :].rearrange("p (b f) h -> p b f h", f=HALVES),
                            af[:, :, :].rearrange("p (b f) h -> p b f h", f=HALVES), ALU.subtract).then_inc(lf_ok, 1)
            e.wait_ge(cs_ps, 1)
            done(e.tensor_copy(cs[:, :, :], ps[:, 4, 64:96].rearrange("p (f k) -> p f k", f=HALVES)))
            e.tensor_tensor(gg[:, :, :].rearrange("p f (b h) -> p b f h", h=XH),
                            gt[:, :, 0:XH].rearrange("p (b f) h -> p b f h", f=HALVES),
                            cs[:, :, :].rearrange("p f (b h) -> p b f h", h=XH), ALU.subtract).then_inc(gg_ok, 1)
            e.wait_ge(gT_ps, 1)
            done(e.tensor_copy(gT[:, :], ps[0:16, 5, 0:S]))
            e.tensor_tensor_scan(mT[:, 0, :], gT[:, :], gT[:, :], -3.0e38, ALU.max, ALU.max).then_inc(m_ok, 1)
            e.wait_ge(va_ok, 3)
            e.wait_ge(m_ok, 1)
            done(e.tensor_scalar(mT[:, 1, :], mT[:, 0, :], -1.0, None, ALU.mult))
            done(e.tensor_copy(m3[0:16, :], mT[:, 1, :]))
            done(e.tensor_tensor(mT[:, 1, :], mT[:, 1, :], m3[0:16, :], ALU.subtract))
            done(e.tensor_copy(mp[:, 0, :], mT[:, 1, :]))
            done(e.tensor_tensor(mT[:, 1, :], mT[:, 1, :], mp[:, 0, :], ALU.subtract), wait=False)
            done(e.tensor_copy(m3[32:48, :], mp[:, 0, :]))
            e.tensor_copy(m3[64:80, :], mT[:, 1, :]).then_inc(m3_ok, 1)
            e.wait_ge(mN_ps, 1)
            e.tensor_tensor(enm[:, :, :], ps[:, 5, 256:288].rearrange("p (f k) -> p f k", f=HALVES), cs[:, :, :],
                            ALU.add).then_inc(em_in, 1)

            def weigh(k):
                e.wait_ge(s_ps, k + 1)
                e.wait_ge(d_sb, k + 1)
                if k >= 4 and k % 2 == 0:
                    e.wait_ge(pv_ps, k // 2 - 1)
                e.scalar_tensor_tensor(CT[:, k % 4, :], ps[:, 2 + k % 2, 0:384], float(XD) ** -0.5, Dm[:, k % 2, :],
                                       ALU.mult, ALU.mult).then_inc(ct_sb, 1)

            def normalise(b):
                e.wait_ge(t_ps, b + 1)
                tt = ps[:, 5, :].rearrange("p (f h k) -> p f h k", f=HALVES, h=XH)
                done(e.tensor_copy(nrm_s[:, :, 0:XH], tt[:, :, :, XD]))
                done(e.scalar_tensor_tensor(nrm_a[:, :, 0:XH], nrm_s[:, :, 0:XH], -1.0, nrm_s[:, :, 0:XH], ALU.mult, ALU.max))
                done(e.tensor_tensor(nrm_a[:, :, 0:XH], nrm_a[:, :, 0:XH], enm[:, :, XH * b:XH * b + XH], ALU.max))
                done(e.tensor_scalar(nrm_a[:, :, 0:XH], nrm_a[:, :, 0:XH], 1e-6, None, ALU.add))
                done(e.reciprocal(nrm_s[:, :, 0:XH], nrm_a[:, :, 0:XH]))
                e.tensor_tensor(aN[:, 2 * b:2 * b + 2, :].rearrange("p f (h k) -> p f h k", k=XD), tt[:, :, :, 0:XD],
                                nrm_s[:, :, 0:XH].unsqueeze(3).broadcast_to([P, HALVES, XH, XD]), ALU.mult).then_inc(h_sb, 1)

            e.wait_ge(em_ok, 1)
            for k in range(NXH):
                weigh(k)
                if k % 4 == 3 and k > 4:
                    normalise(k // 4 - 1)
            normalise(NB - 1)
            e.wait_ge(h_sb, NB)
            g32 = aN[:, :, :].rearrange("p n (h k) -> p (n h) k", k=XD)
            b32 = bN[:, :, :].rearrange("p n (h k) -> p (n h) k", k=XD)
            G = NT * XH
            done(e.tensor_reduce(hs1[:, 0:G], g32, AX.X, ALU.add))
            done(e.tensor_scalar(hs1[:, 0:G], hs1[:, 0:G], 1.0 / XD, None, ALU.mult))
            done(e.tensor_tensor(g32, g32, hs1[:, 0:G].unsqueeze(2).broadcast_to([P, G, XD]), ALU.subtract))
            done(e.tensor_tensor(b32, g32, g32, ALU.mult))
            done(e.tensor_reduce(hs1[:, 0:G], b32, AX.X, ALU.add))
            done(e.tensor_scalar(rs_v[:, 0:G], hs1[:, 0:G], 1.0 / XD, LN_EPS, ALU.mult, ALU.add))
            rsqrt(rs_v[:, 0:G], G)
            done(e.tensor_tensor(g32, g32, rs_y[:, 0:G].unsqueeze(2).broadcast_to([P, G, XD]), ALU.mult))
            done(e.tensor_tensor(aN[:, :, :], aN[:, :, :], ons[:, :].unsqueeze(1).broadcast_to([P, NT, D]), ALU.mult))
            done(e.tensor_tensor(zN[:, :, :], aN[:, :, :], xN[:, :, :], ALU.add))
            layer_norm(zN, xN, ln_out)

        def act_mlstm(e):
            e.wait_ge(gf_ok, 1)
            e.activation(af[:, :, :], af[:, :, :], ACT.Exp, scale=-1.0).then_inc(gl_ok, 1)
            e.wait_ge(gl_ok, 1)
            e.activation(af[:, :, :], af[:, :, :], ACT.Ln, bias=1.0).then_inc(gl_ok, 1)
            e.wait_ge(em_in, 1)
            e.activation(enm[:, :, :], enm[:, :, :], ACT.Exp, scale=-1.0).then_inc(em_ok, 1)

            def decays(k):
                b, h = divmod(k, XH)
                e.wait_ge(e_ps, k + 1)
                if k >= 2:
                    e.wait_ge(ct_sb, k - 1)
                e.activation(Dm[:, k % 2, 0:S], ps[:, k % 2, 0:S], ACT.Exp, bias=gg[:, 0, k:k + 1])
                e.activation(Dm[:, k % 2, S:], ps[:, k % 2, S:384], ACT.Exp, bias=gg[:, 1, k:k + 1]).then_inc(d_sb, 1)

            def take_out(b):
                e.wait_ge(pv_ps, XH // 2 * (b + 1))
                if b:
                    e.wait_ge(t_ps, b)
                e.copy(Oxs[:, :], ps[:, 4, :]).then_inc(o_sb, 1)

            for k in range(NXH):
                decays(k)
                if k % 4 == 1 and k > 4:
                    take_out(k // 4 - 1)
            take_out(NB - 1)

        def pe_mlstm_gates(e):
            e.wait_ge(gate_w, 1)
            e.wait_ge(ld_ctx, 48)
            for n in range(NT):
                m = e.matmul(ps[:, 5, 8 * n:8 * n + 8], ctxT[:, n * P:(n + 1) * P], wgc[:, :], start=True, stop=True)
            m.then_inc(gate_c, 1)

        def pe_mlstm(e):
            e.wait_ge(xt_sb, 2)
            for n in range(NT):
                m = e.matmul(ps[:, 4, 8 * n:8 * n + 8], xT[:, n * P:(n + 1) * P], wg[:, 0, :], start=True, stop=True)
            m.then_inc(gate_x, 1)
            e.wait_ge(lf_ok, 1)
            e.matmul(ps[:, 4, 64:80], K("causal")[:, 0:P], lf[:, 0, :], start=True, stop=True)
            e.matmul(ps[:, 4, 80:96], K("causal")[:, P:2 * P], lf[:, 0, :], start=True, stop=False)
            e.matmul(ps[:, 4, 80:96], K("causal")[:, 0:P], lf[:, 1, :], start=False, stop=True).then_inc(cs_ps, 1)
            e.wait_ge(gg_ok, 1)
            e.transpose(ps[0:16, 5, 0:P], gg[:, 0, :], K("ident"))
            e.transpose(ps[0:16, 5, P:S], gg[:, 1, :], K("ident")).then_inc(gT_ps, 1)
            e.wait_ge(m_ok, 1)
            e.transpose(ps[:, 5, 256:272], mT[:, 0, 0:P], K("ident")[0:16, 0:16])
            e.transpose(ps[:, 5, 272:288], mT[:, 0, P:S], K("ident")[0:16, 0:16]).then_inc(mN_ps, 1)
            e.wait_ge(m3_ok, 1)
            e.wait_ge(qz_ok, XH)

            def logits(k):
                b, h = divmod(k, XH)
                if k >= 2:
                    e.wait_ge(d_sb, k - 1)
                E_ = ps[:, k % 2, :]
                e.matmul(E_[:, 0:S], sel_bf[0:96, k, :], m3[:, :], start=True, stop=False, skip_group_check=True)
                e.matmul(E_[:, S:384], sel_bf[0:96, k, :], m3[:, P:S], start=False, stop=False, skip_group_check=True)
                e.matmul(E_[:, 0:P], ident_bf, neg_bf, start=False, stop=False, skip_group_check=True)
                e.matmul(E_[:, S:384], ident_bf, neg_bf, start=False, stop=True, skip_group_check=True).then_inc(e_ps, 1)
                if k >= 2:
                    e.wait_ge(ct_sb, k - 1)
                c0 = b * S
                e.matmul(ps[:, 2 + k % 2, 0:S], ctxT[:, c0:c0 + P], Qz[:, h, c0:c0 + S], start=True, stop=True)
                e.matmul(ps[:, 2 + k % 2, S:384], ctxT[:, c0 + P:c0 + S], Qz[:, h, c0 + P:c0 + S],
                         start=True, stop=True).then_inc(s_ps, 1)

            def mix(u):
                b, g = divmod(u, XH // 2)
                if g == 0 and b:
                    e.wait_ge(o_sb, b)
                e.wait_ge(ct_sb, 2 * (u + 1))
                for i in range(2):
                    e.matmul(ps[64 * i:64 * i + 64, 4, g * S:(g + 1) * S], Va[:, 2 * b, 2 * g + i, :],
                             CT[:, (2 * u + i) % 4, 0:S], start=True, stop=True)
                for i in range(2):
                    m = e.matmul(ps[64 * i:64 * i + 64, 4, g * S + P:(g + 1) * S], Va[:, 2 * b + 1, 2 * g + i, :],
                                 CT[:, (2 * u + i) % 4, S:384], start=False, stop=True, skip_group_check=True)
                m.then_inc(pv_ps, 1)

            def to_tokens(b):
                e.wait_ge(o_sb, b + 1)
                if b:
                    e.wait_ge(h_sb, b)
                else:
                    e.wait_ge(em_in, 1)
                for f in range(HALVES):
                    for g in range(2):
                        i = 2 * f + g
                        m = e.transpose(ps[:, 5, i * P:(i + 1) * P], Oxs[:, g * S + f * P:g * S + (f + 1) * P], K("ident"))
                m.then_inc(t_ps, 1)

            for k in range(NXH):
                logits(k)
                if k % 2 and k > 2:
                    mix((k - 3) // 2)
                if k % 4 == 2 and k > 4:
                    to_tokens(k // 4 - 1)
            mix(NXH // 2 - 1)
            to_tokens(NB - 1)

        phases["pool"].append(pool_mlstm)
        phases["act"].append(act_mlstm)
        phases["dve"] += [dve_mlstm_gates, dve_mlstm]
        phases["pe"] += [pe_mlstm_gates, pe_mlstm]
        turn(1)


        dl = sb("dl", [P, NT, E])
        oh = sb("oh", [P, NT, E])
        mx8 = sb("mx8", [P, 3, NT])
        cnt = sb("cnt", [P, 4, E, NT])
        ne = sb("ne", [P, 3, E])
        posf = sb("posf", [P, NT])
        pos = sb("pos", [P, NT], I32)
        eidf = sb("eidf", [P, NSEG])
        eid = sb("eid", [P, NSEG], I32)
        big = arena[:, NSEG * D:NSEG * (D + E)].rearrange("p (s e) -> p s e", e=E)
        xs = arena[:, 0:NSEG * D].rearrange("p (s d) -> p s d", d=D)
        ys = xs
        xsT = arena[:, NSEG * D:2 * NSEG * D].rearrange("p (s d) -> p s d", d=D)
        w1c = arena[:, 2 * NSEG * D:2 * NSEG * D + 4 * (FF + 2)].rearrange("p (s f) -> p s f", s=4)
        b2r = work[:, 0:E * D].rearrange("p (e d) -> p e d", d=D)
        hT = work[:, 4 * T:5 * T].rearrange("p (s f) -> p s f", f=FF)
        kf_ok = sem("kf_ok")
        kp_out = sem("kp_out")
        ld_bias = sem("ld_bias")
        lg_ps = sem("lg_ps")
        dl_ok = sem("dl_ok")
        ex_ok = sem("ex_ok")
        oh_ok = sem("oh_ok")
        rk_ps = sem("rank_ps")
        pos_ok = sem("pos_ok")
        eid_ok = sem("eid_ok")
        sorted_out = sem("sorted_out")
        xs_in = [sem(f"xs_in{i}") for i in range(3)]
        xt2_ps = sem("segment_turned")
        xt2_sb = sem("segment_turned_sb")
        h_ps = sem("h_ps")
        w1_ok = sem("w1_ok")
        hT_ok = sem("hT_ok")
        y_ps = sem("y_ps")
        ys_ok = sem("ys_ok")
        ys_out = sem("ys_out")
        y_in = [sem(f"y_in{i}") for i in range(2)]
        G3 = NSEG // 3

        def sync_moe(e):
            e.wait_ge(pv_ps, NXH // 2)
            e.wait_ge(h_sb, NB)
            e.dma_start(b2r.rearrange("p e d -> p (e d)"), w["b2"].rearrange("e d -> (e d)").partition_broadcast(P)).then_inc(ld_bias, 16)
            e.wait_ge(sorted_out, 16 * NT)
            for i in range(3):
                e.dma_start(xs[:, i * G3:(i + 1) * G3, :],
                            xs_scr[i * G3 * P:(i + 1) * G3 * P, :].rearrange("(s p) d -> p s d", p=P)).then_inc(xs_in[i], 16)
            LATE["sync_keys"](e)
            for i in range(3):
                e.wait_ge(ys_ok, (i + 1) * G3)
                e.dma_start(ys_scr[i * G3 * P:(i + 1) * G3 * P, :].rearrange("(s p) d -> p s d", p=P),
                            ys[:, i * G3:(i + 1) * G3, :]).then_inc(ys_out, 16)

        def pool_moe(e):
            e.wait_ge(pos_ok, 1)
            e.wait_ge(ld_moe, 16 * 6)
            for n in range(NT):
                e.indirect_dma_start(xs_scr, bass.IndirectOffsetOnAxis(ap=pos[:, n:n + 1].bitcast(U32), axis=0),
                                     xN[:, n, :], None).then_inc(sorted_out, 16)
            LATE["pool_keys"](e)
            e.wait_ge(ys_out, 48)
            for n in range(NT):
                e.indirect_dma_start(aN[:, n, :], None, ys_scr,
                                     bass.IndirectOffsetOnAxis(ap=pos[:, n:n + 1].bitcast(U32), axis=0)).then_inc(y_in[n // 4], 16)

        def pe_moe(e):
            e.wait_ge(xt_sb, 4)
            e.wait_ge(ld_moe, 16 * 6)
            for n in range(NT):
                m = e.matmul(ps[:, 4, E * n:E * (n + 1)], xT[:, n * P:(n + 1) * P], wr[:, :], start=True, stop=True)
            m.then_inc(lg_ps, 1)
            LATE["pe_keys"](e)
            e.wait_ge(oh_ok, 1)
            for c in range(2):
                m = e.matmul(ps[:, 5, c * NT * E:(c + 1) * NT * E], K("causal")[:, c * P:(c + 1) * P],
                             oh[:, :, :].rearrange("p n e -> p (n e)"), start=True, stop=True)
            m.then_inc(rk_ps, 1)
            e.wait_ge(kf_ok, 1)
            e.wait_ge(eid_ok, 1)

            def turn_in(s):
                if s % G3 == 0:
                    e.wait_ge(xs_in[s // G3], 16)
                if s >= 2:
                    e.wait_ge(xt2_sb, s - 1)
                e.transpose(ps[:, s % 2, 0:P], xs[:, s, :], K("ident")).then_inc(xt2_ps, 1)

            def layer1(s):
                e.wait_ge(xt2_sb, s + 1)
                e.wait_ge(w1_ok, s + 1)
                if s >= 2:
                    e.wait_ge(hT_ok, s - 1)
                for f in range(2):
                    m = e.matmul(ps[:, 2 + s % 2, f * P:(f + 1) * P], w1c[:, s % 4, f * P:(f + 1) * P], xsT[:, s, :],
                                 start=True, stop=True)
                m.then_inc(h_ps, 1)

            def layer2(s):
                e.wait_ge(hT_ok, s + 1)
                if s >= 2:
                    e.wait_ge(ys_ok, s - 1)
                k = e.value_load(eid[0:1, s:s + 1], min_val=0, max_val=E - 1)
                for f in range(2):
                    m = e.matmul(ps[:, 6 + s % 2, 0:D], hT[:, s % 4, f * P:(f + 1) * P],
                                 w2[:, f, bass.ds(k, 1), :].rearrange("p o d -> p (o d)"), start=(f == 0), stop=(f == 1))
                m.then_inc(y_ps, 1)

            for i in range(-1, NSEG + 2):
                if i + 1 < NSEG:
                    turn_in(i + 1)
                if 0 <= i < NSEG:
                    layer1(i)
                if 0 <= i - 2 < NSEG:
                    layer2(i - 2)

        def act_moe(e):
            e.wait_ge(dl_ok, 1)
            e.activation(bN[:, 0, 0:NT * E].rearrange("p (n e) -> p n e", e=E), dl[:, :, :], ACT.Exp).then_inc(ex_ok, 1)
            LATE["act_keys"](e)
            for s in range(NSEG):
                e.wait_ge(h_ps, s + 1)
                if s >= 4:
                    e.wait_ge(y_ps, s - 3)
                for f in range(2):
                    i = e.activation(hT[:, s % 4, f * P:(f + 1) * P], ps[:, 2 + s % 2, f * P:(f + 1) * P], ACT.Gelu,
                                     bias=w1c[:, s % 4, FF + f:FF + f + 1])
                i.then_inc(hT_ok, 1)

        def dve_moe(e):
            e.wait_ge(lg_ps, 1)
            lg = ps[:, 4, 0:NT * E].rearrange("p (n e) -> p n e", e=E)
            done(e.tensor_reduce(mx8[:, 0, :], lg, AX.X, ALU.max))
            e.tensor_tensor(dl[:, :, :], lg, mx8[:, 0, :].unsqueeze(2).broadcast_to([P, NT, E]), ALU.subtract).then_inc(dl_ok, 1)
            e.wait_ge(dl_ok, 1)
            done(e.tensor_scalar(oh[:, :, :], dl[:, :, :], 0.0, None, ALU.is_equal))
            done(e.tensor_tensor(oh[:, :, :], oh[:, :, :], K("rank").unsqueeze(1).broadcast_to([P, NT, E]), ALU.mult))
            done(e.tensor_reduce(mx8[:, 1, :], oh[:, :, :], AX.X, ALU.max))
            e.tensor_tensor(oh[:, :, :], oh[:, :, :], mx8[:, 1, :].unsqueeze(2).broadcast_to([P, NT, E]), ALU.is_equal).then_inc(oh_ok, 1)
            e.wait_ge(ex_ok, 1)
            done(e.tensor_reduce(mx8[:, 0, :], bN[:, 0, 0:NT * E].rearrange("p (n e) -> p n e", e=E), AX.X, ALU.add))
            done(e.reciprocal(mx8[:, 2, :], mx8[:, 0, :]))
            e.wait_ge(rk_ps, 1)
            rank = ps[:, 5, 0:NT * E].rearrange("p (n e) -> p e n", e=E)
            done(e.tensor_copy(cnt[:, 0], ps[:, 5, NT * E:2 * NT * E].rearrange("p (n e) -> p e n", e=E)))
            done(e.tensor_tensor_scan(cnt[:, 1].rearrange("p e n -> p (e n)"), K("first"), cnt[:, 0].rearrange("p e n -> p (e n)"),
                                      0.0, ALU.mult, ALU.add))
            g8 = big[:, 0:NT, :].rearrange("p n e -> p e n")
            done(e.tensor_tensor(g8, cnt[:, 1, :, NT - 1:NT].broadcast_to([P, E, NT]),
                                 K("full").unsqueeze(1).broadcast_to([P, E, NT]), ALU.is_gt))
            done(e.tensor_reduce(ne[:, 0, :], g8, AX.X, ALU.add))
            done(e.tensor_tensor_scan(ne[:, 1, :], K("causal")[:, P:P + E], ne[:, 0, :], 0.0, ALU.mult, ALU.add))
            done(e.tensor_tensor(ne[:, 2, :], ne[:, 1, :], ne[:, 0, :], ALU.subtract), wait=False)
            done(e.tensor_tensor(cnt[:, 2], cnt[:, 1], cnt[:, 0], ALU.subtract))
            done(e.scalar_tensor_tensor(cnt[:, 2], ne[:, 2, :].unsqueeze(2).broadcast_to([P, E, NT]), float(P), cnt[:, 2],
                                        ALU.mult, ALU.add))
            done(e.tensor_tensor(cnt[:, 3], rank, cnt[:, 2], ALU.add))
            done(e.tensor_tensor(cnt[:, 3], cnt[:, 3], oh[:, :, :].rearrange("p n e -> p e n"), ALU.mult))
            done(e.tensor_reduce(posf[:, :], cnt[:, 3].rearrange("p e n -> p n e"), AX.X, ALU.add))
            e.tensor_scalar(pos[:, :], posf[:, :], -1.0, None, ALU.add).then_inc(pos_ok, 1)
            done(e.tensor_tensor(big, ne[:, 1:2, :].broadcast_to([P, NSEG, E]), K("seg").unsqueeze(2).broadcast_to([P, NSEG, E]),
                                 ALU.is_le))
            done(e.tensor_reduce(eidf[:, :], big, AX.X, ALU.add))
            e.tensor_scalar(eid[:, :], eidf[:, :], float(E - 1), None, ALU.min).then_inc(eid_ok, 1)
            e.wait_ge(eid_ok, 1)
            e.wait_ge(ld_bias, 16)
            experts = {}

            def take_weights(s):
                if s >= 4:
                    e.wait_ge(hT_ok, s - 3)
                experts[s] = e.value_load(eid[0:1, s:s + 1], min_val=0, max_val=E - 1)
                e.tensor_copy(w1c[:, s % 4, :], w1[:, bass.ds(experts[s], 1), :].rearrange("p o f -> p (o f)")).then_inc(w1_ok, 1)

            take_weights(0)
            take_weights(1)
            for i in range(-1, NSEG + 2):
                if i + 1 < NSEG:
                    e.wait_ge(xt2_ps, i + 2)
                    e.tensor_copy(xsT[:, i + 1, :], ps[:, (i + 1) % 2, 0:P]).then_inc(xt2_sb, 1)
                if 2 <= i + 2 < NSEG:
                    take_weights(i + 2)
                if 0 <= i - 2 < NSEG:
                    s = i - 2
                    e.wait_ge(y_ps, s + 1)
                    e.tensor_tensor(ys[:, s, :], ps[:, 6 + s % 2, 0:D],
                                    b2r[:, bass.ds(experts.pop(s), 1), :].rearrange("p o d -> p (o d)"), ALU.add).then_inc(ys_ok, 1)
            for n in range(NT):
                if n % 4 == 0:
                    e.wait_ge(y_in[n // 4], 64)
                done(e.scalar_tensor_tensor(zN[:, n, :], aN[:, n, :], mx8[:, 2, n:n + 1], xN[:, n, :], ALU.mult, ALU.add),
                     wait=(n == NT - 1))
            layer_norm(zN, xN, ln_out)

        phases["sync"].append(sync_moe)
        phases["pool"].append(pool_moe)
        phases["act"].append(act_moe)
        phases["dve"].append(dve_moe)
        phases["pe"].append(pe_moe)
        turn(2)


        KTs = work[:, 0:T]
        Qs = work[:, T:2 * T]
        oT = work[:, 2 * T:3 * T]
        Vl = arena[:, 8 * T:10 * T].rearrange("p (n h k) -> p n h k", n=NT, h=LH)
        Osb = work[:, 8 * T:9 * T]
        CL = work[:, 3 * T:6 * T].rearrange("p (s c) -> p s c", s=8)
        lq_ps = sem("lq_ps")
        lv_ps = sem("lv_ps")
        lq_sb = sem("lq_sb")
        lk_sb = sem("lk_sb")
        lv_sb = sem("lv_sb")
        vl_one = sem("vl_one")
        lz_ok = sem("lz_ok")
        ls_ps = sem("ls_ps")
        lc_sb = sem("lc_sb")
        lo_ps = sem("lo_ps")
        lo_sb = sem("lo_sb")
        lt_ps = sem("lt_ps")
        lh_sb = sem("lh_sb")
        lm_ok = sem("linear_heads_mixed")
        ly_ps = sem("ly_ps")
        NLH = NB * LH

        def pool_linear(e):
            e.wait_ge(pv_ps, NXH // 2)
            e.memset(Vl[:, :, :, LD:], 1.0).then_inc(vl_one, 1)

        def pe_linear(e):
            e.wait_ge(xt_sb, 5)
            e.wait_ge(ld_l1, 16 * 12)
            e.wait_ge(ys_ok, NSEG)

            def project(b, bank):
                for i in range(2):
                    e.matmul(ps[:, bank + i, :], l1w[:, i, :], xT[:, b * 512:(b + 1) * 512], start=True, stop=True).then_inc(lq_ps, 1)

            project(0, 0)
            e.wait_ge(xt_sb, 6)
            for n in range(NT):
                m = e.matmul(ps[:, 4 + n // 4, (n % 4) * P:(n % 4 + 1) * P], xT[:, n * P:(n + 1) * P], l1w[:, 2, :],
                             start=True, stop=True)
            m.then_inc(lv_ps, 1)

            def scores(k):
                b, h = divmod(k, LH)
                if k >= 4:
                    e.wait_ge(lc_sb, k - 3)
                if k % (2 * LH) == 0:
                    e.wait_ge(lk_sb, k // (2 * LH) + 1)
                e.wait_ge(lz_ok, k + 1)
                c0 = b * S
                e.matmul(ps[:, k % 4, 0:S], KTs[:, c0:c0 + P], Qz[:, h, c0:c0 + S], start=True, stop=True)
                e.matmul(ps[:, k % 4, S:384], KTs[:, c0 + P:c0 + S], Qz[:, h, c0 + P:c0 + S],
                         start=True, stop=True).then_inc(ls_ps, 1)

            def mix(u):
                b, g = divmod(u, LH // 4)
                if g == 0 and b >= 2:
                    e.wait_ge(lo_sb, b - 1)
                e.wait_ge(lc_sb, 4 * (u + 1))
                if u == 0:
                    e.wait_ge(lv_sb, 1)
                for i in range(4):
                    e.matmul(ps[32 * i:32 * i + 32, 4 + b % 2, g * S:(g + 1) * S], Vl[:, 2 * b, 4 * g + i, :],
                             CL[:, (4 * u + i) % 8, 0:S], start=True, stop=True)
                for i in range(4):
                    m = e.matmul(ps[32 * i:32 * i + 32, 4 + b % 2, g * S + P:(g + 1) * S], Vl[:, 2 * b + 1, 4 * g + i, :],
                                 CL[:, (4 * u + i) % 8, S:384], start=False, stop=True, skip_group_check=True)
                m.then_inc(lo_ps, 1)

            def to_tokens(b):
                e.wait_ge(lo_sb, b + 1)
                e.wait_ge(lk_sb, 2)
                if b >= 2:
                    e.wait_ge(lh_sb, b - 1)
                for i in range(4):
                    f, g = divmod(i, 2)
                    m = e.transpose(ps[:, 6 + b % 2, i * P:(i + 1) * P], Osb[:, (b % 2) * 512 + g * S + f * P:(b % 2) * 512 + g * S + (f + 1) * P],
                                    K("ident"))
                m.then_inc(lt_ps, 1)

            for k in range(NLH):
                scores(k)
                if k == 3:
                    project(1, 6)
                if k % 4 == 1 and k > 4:
                    mix((k - 5) // 4)
                if k % LH == 4 and k > LH:
                    to_tokens(k // LH - 1)
            mix(NLH // 4 - 1)
            to_tokens(NB - 1)

        def pe_linear_out(e):
            e.wait_ge(xt_sb, 8)
            for n in range(NT):
                m = e.matmul(ps[:, 4 + n // 4, (n % 4) * P:(n % 4 + 1) * P], oT[:, n * P:(n + 1) * P], l1w[:, 3, :],
                             start=True, stop=True)
            m.then_inc(ly_ps, 1)

        def act_linear(e):
            e.wait_ge(lq_ps, 1)
            e.copy(Qs[:, 0:512], ps[:, 0, :]).then_inc(lq_sb, 1)
            e.wait_ge(lq_ps, 2)
            e.copy(KTs[:, 0:512], ps[:, 1, :]).then_inc(lk_sb, 1)
            e.wait_ge(lv_ps, 1)
            e.wait_ge(vl_one, 1)
            e.copy(Vl[:, :, :, 0:LD], ps[:, 4:6, :].rearrange("p b (n h k) -> p (b n) h k", h=LH, k=LD)).then_inc(lv_sb, 1)
            e.wait_ge(lq_ps, 3)
            e.copy(Qs[:, 512:], ps[:, 6, :]).then_inc(lq_sb, 1)
            e.wait_ge(lq_ps, 4)
            e.copy(KTs[:, 512:], ps[:, 7, :]).then_inc(lk_sb, 1)
            e.wait_ge(kp_out, 16 * NB)
            for b in range(NB):
                e.wait_ge(lo_ps, LH // 4 * (b + 1))
                if b >= 2:
                    e.wait_ge(lt_ps, b - 1)
                e.copy(Osb[:, (b % 2) * 512:(b % 2) * 512 + 512], ps[:, 4 + b % 2, :]).then_inc(lo_sb, 1)

        def dve_linear(e):
            def one_head(k):
                b, h = divmod(k, LH)
                if h == 0:
                    e.wait_ge(lq_sb, b // 2 + 1)
                e.tensor_scalar(Qz[:, h, b * S:(b + 1) * S], Qs[:, b * S:(b + 1) * S], K("hm8")[:, h:h + 1], None,
                                ALU.mult).then_inc(lz_ok, 1)

            for k in range(LH):
                one_head(k)

            def normalise(b):
                e.wait_ge(lt_ps, b + 1)
                tt = ps[:, 6 + b % 2, :].rearrange("p (f h k) -> p f h k", f=HALVES, h=LH)
                su, ab = nrm_s[:, :, 0:LH], nrm_a[:, :, 0:LH]
                done(e.tensor_copy(su, tt[:, :, :, LD]))
                done(e.scalar_tensor_tensor(ab, su, -1.0, su, ALU.mult, ALU.max))
                done(e.tensor_scalar(ab, ab, 1.0, None, ALU.max))
                done(e.reciprocal(su, ab))
                e.tensor_tensor(aN[:, 2 * b:2 * b + 2, :].rearrange("p f (h k) -> p f h k", k=LD), tt[:, :, :, 0:LD],
                                su.unsqueeze(3).broadcast_to([P, HALVES, LH, LD]), ALU.mult).then_inc(lh_sb, 1)

            for k in range(NLH):
                e.wait_ge(ls_ps, k + 1)
                if k >= 8 and k % 4 == 0:
                    e.wait_ge(lo_ps, k // 4 - 1)
                e.tensor_tensor(CL[:, k % 8, :], ps[:, k % 4, 0:384], K("causal"), ALU.mult).then_inc(lc_sb, 1)
                if k + LH < NLH:
                    one_head(k + LH)
                if k % LH == 6 and k > LH:
                    normalise(k // LH - 1)
            normalise(NB - 1)
            e.wait_ge(lh_sb, NB)
            g16 = aN[:, :, :].rearrange("p n (h k) -> p (n h) k", k=LD)
            b16 = bN[:, :, :].rearrange("p n (h k) -> p (n h) k", k=LD)
            G = NT * LH
            done(e.tensor_tensor(b16, g16, g16, ALU.mult))
            done(e.tensor_reduce(hs1[:, 0:G], b16, AX.X, ALU.add))
            done(e.tensor_scalar(rs_v[:, 0:G], hs1[:, 0:G], 1.0 / LD, LN_EPS, ALU.mult, ALU.add))
            rsqrt(rs_v[:, 0:G], G)
            done(e.tensor_tensor(g16, g16, rs_y[:, 0:G].unsqueeze(2).broadcast_to([P, G, LD]), ALU.mult))
            done(e.tensor_tensor(g16, g16, nrm[:, :].unsqueeze(1).broadcast_to([P, G, LD]), ALU.mult))
            e.nop().then_inc(lm_ok, NT)
            e.wait_ge(ly_ps, 1)
            done(e.tensor_tensor(zN[:, :, :], ps[:, 4:6, :].rearrange("p b (n d) -> p (b n) d", d=D), xN[:, :, :], ALU.add))
            layer_norm(zN, xN, ln_out)

        def turn_heads(ready):
            phases["pe"].append(lambda e: pe_turn(aN, ready, 0))
            phases["act"].append(lambda e: act_turn(oT))

        phases["pool"].append(pool_linear)
        phases["act"].append(act_linear)
        phases["dve"].append(dve_linear)
        phases["pe"].append(pe_linear)
        turn_heads(lm_ok)
        phases["pe"] += [pe_linear_out, lambda e: LATE["values"](e)]
        turn(3)


        NR = 96
        ONES = float(np.array(0x3F803F80, np.uint32).view(np.float32))
        qf = work[:, 0:T]
        qr = work[:, T:2 * T]
        qp = work[:, 2 * T:3 * T + T // 2].bitcast(BF16).rearrange("p (c t) -> p c t", c=3)
        kf = work[:, 6 * T:7 * T]
        kr = work[:, 7 * T:8 * T]
        kp = work[:, 8 * T:9 * T + T // 2].bitcast(BF16).rearrange("p (c t) -> p c t", c=3)
        Qs_raw = [arena[:, 4 * T:6 * T], arena[:, 6 * T:8 * T], work[:, 6 * T:8 * T]]
        Ks_raw = [arena[:, 8 * T:10 * T], work[:, 9 * T:11 * T], work[:, 4 * T:6 * T]]
        NSLOT = 3
        Qt, Kt = ([a.bitcast(BF16).rearrange("p (h t) -> p h t", h=AH) for a in raw] for raw in (Qs_raw, Ks_raw))
        Vx = arena[:, 0:4 * T].rearrange("p (n h k) -> p n h k", n=NT, h=AH)
        Pb = work[:, 0:4 * T].rearrange("p (s c) -> p s c", s=8)
        Ox = work[:, 8 * T:9 * T]
        mS = sb("mS", [P, 2, 32])
        mt = sb("mt", [32, 2, P])
        mb = sb("mb", [32, 2, 3, P], BF16)
        xb = sb("xb", [P, NT, D])
        bq8 = sb("bq8", [P, 1])
        aq_ps = sem("aq_ps")
        av_ps = sem("av_ps")
        bq_ok = sem("bq_ok")
        aq_sb = sem("aq_sb")
        slot_clear = sem("slot_clear")
        av_sb = sem("av_sb")
        vx_one = sem("vx_one")
        qp_ok = sem("qp_ok")
        kp_ok = sem("kp_ok")
        qp_out = sem("qp_out")
        kf_ps = sem("kf_ps")
        kstep = sem("k_split_step")
        slot_ld = [sem(f"slot_ld{i}") for i in range(NSLOT)]
        as_ps = sem("as_ps")
        as_used = sem("as_used")
        am_ps = sem("am_ps")
        am_parts = sem("am_parts")
        am_row = [sem("am_row0"), sem("am_row1")]
        at_ps = sem("at_ps")
        ap_sb = sem("ap_sb")
        ao_ps = sem("ao_ps")
        ao_sb = sem("ao_sb")
        ac_ps = sem("ac_ps")
        ah_sb = sem("ah_sb")
        ax_ok = sem("ax_ok")
        ay_ps = sem("ay_ps")
        NSJ = 2 * AH // 2
        AHEAD = 3 * AH // 2
        SBANK = (0, 1, 7)
        WIDE = NB * AH - AHEAD + 4

        def lbank(t):
            return 2 + t % 2 if t < WIDE else (2, 3, 0, 1)[t % 4]


        def pe_keys(e):
            e.wait_ge(ld_l1, 16 * 12)
            for b in range(2):
                m = e.matmul(ps[:, 6 + b, :], axw[:, 1, :], ctxT[:, b * 512:(b + 1) * 512], start=True, stop=True)
            m.then_inc(kf_ps, 1)

        def act_keys(e):
            e.wait_ge(kf_ps, 1)
            e.activation(kf, ps[:, 6:8, :].rearrange("p b c -> p (b c)"), ACT.Identity, bias=abq[:, 1:2]).then_inc(kf_ok, 1)

        def pool_keys(e):
            e.wait_ge(kf_ok, 1)
            n = 0
            for i in range(3):
                j = e.tensor_copy(kp[:, i, :], kf if i == 0 else kr)
                if i == 2:
                    j.then_inc(kp_ok, 1)
                    break
                j.then_inc(kstep, 1)
                e.wait_ge(kstep, n + 1)
                e.tensor_tensor(kr, kf if i == 0 else kr, kp[:, i, :], ALU.subtract).then_inc(kstep, 1)
                e.wait_ge(kstep, n + 2)
                n += 2
            e.wait_ge(kp_out, 16 * NB)
            e.memset(Qs_raw[2], 0.0).then_inc(slot_clear, 1)
            e.memset(Ks_raw[1], ONES).then_inc(slot_clear, 1)

        def sync_keys(e):
            e.wait_ge(kp_ok, 1)
            for b in range(NB):
                e.dma_start(q_scr[1, b].rearrange("c d (h t) -> (d h) c t", t=S),
                            kp[:, :, b * S:(b + 1) * S]).then_inc(kp_out, 16)

        def pool_softmax(e):
            e.wait_ge(lo_ps, NLH // 4)
            e.memset(Ks_raw[0], ONES).then_inc(slot_clear, 1)
            e.memset(Qs_raw[0], 0.0).then_inc(slot_clear, 1)
            e.memset(Vx[:, :, :, AD:], 1.0).then_inc(vx_one, 1)
            e.memset(Qs_raw[1], 0.0).then_inc(slot_clear, 1)
            e.memset(Ks_raw[2], ONES).then_inc(slot_clear, 1)

        def pe_values(e):
            for n in range(NT):
                m = e.matmul(ps[:, 2 + n // 4, (n % 4) * P:(n % 4 + 1) * P], ctxT[:, n * P:(n + 1) * P], axw[:, 2, :],
                             start=True, stop=True)
            m.then_inc(av_ps, 1)

        def pe_softmax(e):
            for b in range(2):
                e.wait_ge(xt_sb, 9 + b)
                e.matmul(ps[:, b, :], axw[:, 0, :], xT[:, b * 512:(b + 1) * 512], start=True, stop=True).then_inc(aq_ps, 1)
            e.wait_ge(av_sb, 1)
            e.wait_ge(aq_sb, 2)

            def score(s):
                b, r = divmod(s, NSJ)
                f, hp = divmod(r, AH // 2)
                if s >= 3:
                    e.wait_ge(as_used, s - 2)
                for h in range(2):
                    m = e.matmul(ps[:, SBANK[s % 3], h * S:(h + 1) * S], Qt[b % NSLOT][0:NR, 2 * hp + h, f * P:(f + 1) * P],
                                 Kt[b % NSLOT][0:NR, 2 * hp + h, :], start=True, stop=True)
                m.then_inc(as_ps, 1)

            def turn_max(b):
                e.wait_ge(as_used, NSJ * (b + 1))
                if b >= 2:
                    e.wait_ge(ah_sb, 2 * (b - 2) + 1)
                e.transpose(ps[0:32, 6, 0:P], mS[:, b % 2, :], K("ident")).then_inc(am_ps, 1)

            def logits(t):
                b, h = divmod(t, AH)
                if t < WIDE + 2:
                    if t >= 2:
                        e.wait_ge(ap_sb, t - 1)
                elif t < WIDE + 4:
                    e.wait_ge(as_used, NB * NSJ)
                else:
                    e.wait_ge(ap_sb, t - 3)
                if h == 0:
                    e.wait_ge(am_row[b % 2], 48 * (b // 2 + 1))
                for f in range(HALVES):
                    m = e.matmul(ps[:, lbank(t), f * S:(f + 1) * S], Kt[b % NSLOT][:, h, f * P:(f + 1) * P], Qt[b % NSLOT][:, h, :],
                                 start=True, stop=True)
                m.then_inc(at_ps, 1)

            def mix(u, f):
                b, g = divmod(u, AH // 4)
                if f == 0:
                    e.wait_ge(ap_sb, 4 * (u + 1))
                    if g == 0 and b:
                        e.wait_ge(ao_sb, b)
                for i in range(4):
                    m = e.matmul(ps[32 * i:32 * i + 32, 4 + g // 2, (g % 2) * S:(g % 2 + 1) * S], Vx[:, 2 * b + f, 4 * g + i, :],
                                 Pb[:, (4 * u + i) % 8, f * S:(f + 1) * S], start=(f == 0), stop=(f == 1))
                if f == 1:
                    m.then_inc(ao_ps, 1)

            def to_tokens(b, f):
                e.wait_ge(ao_sb, b + 1)
                if b or f:
                    e.wait_ge(ah_sb, 2 * b + f)
                e.wait_ge(am_parts, 3 * min(b + 2 + f, NB))
                for g in range(4):
                    m = e.transpose(ps[:, 6, g * P:(g + 1) * P], Ox[:, g * S + f * P:g * S + (f + 1) * P], K("ident"))
                m.then_inc(ac_ps, 1)

            for t in range(-AHEAD, NB * AH):
                s = t + AHEAD
                if s < NB * NSJ:
                    if s % NSJ == 0:
                        b = s // NSJ
                        e.wait_ge(slot_ld[b % NSLOT], 16 * 6 * (b // NSLOT + 1))
                    score(s)
                if s % NSJ == 1 and 0 < s // NSJ <= NB:
                    turn_max(s // NSJ - 1)
                if t >= 0:
                    logits(t)
                    if t % 4 in (1, 2) and t > 4:
                        mix((t - 5) // 4, t % 4 - 1)
                    if t % AH in (6, 10) and t > AH:
                        to_tokens(t // AH - 1, (t % AH - 6) // 4)
            mix(NB * AH // 4 - 1, 0)
            mix(NB * AH // 4 - 1, 1)
            to_tokens(NB - 1, 0)
            to_tokens(NB - 1, 1)

        def pe_softmax_out(e):
            e.wait_ge(xt_sb, 12)
            for n in range(NT):
                m = e.matmul(ps[:, 4 + n // 4, (n % 4) * P:(n % 4 + 1) * P], oT[:, n * P:(n + 1) * P], axw[:, 3, :],
                             start=True, stop=True)
            m.then_inc(ay_ps, 1)

        def act_softmax(e):
            e.wait_ge(bq_ok, 1)
            for i in range(2):
                e.wait_ge(aq_ps, i + 1)
                e.activation(qf[:, i * 512:(i + 1) * 512], ps[:, i, :], ACT.Identity, bias=bq8[:, :],
                             scale=float(AD) ** -0.5).then_inc(aq_sb, 1)
            for t in range(NB * AH):
                e.wait_ge(at_ps, t + 1)
                if t >= 8 and t % 4 == 0:
                    e.wait_ge(ao_ps, t // 4 - 1)
                e.activation(Pb[:, t % 8, :], ps[:, lbank(t), :], ACT.Exp).then_inc(ap_sb, 1)
                if t % AH == 2 and t > AH:
                    take(e, t // AH - 1)
            take(e, NB - 1)

        def take(e, b):
            e.wait_ge(ao_ps, AH // 4 * (b + 1))
            if b:
                e.wait_ge(ac_ps, 2 * b)
            e.copy(Ox[:, :], ps[:, 4:6, :].rearrange("p b c -> p (b c)")).then_inc(ao_sb, 1)

        def dve_softmax(e):
            e.wait_ge(ld_l1, 16 * 12)
            e.tensor_scalar(bq8[:, :], abq[:, 0:1], float(AD) ** -0.5, None, ALU.mult).then_inc(bq_ok, 1)
            for b in range(NB):
                t = slice(b * S, (b + 1) * S)
                e.wait_ge(aq_sb, b // 2 + 1)
                done(e.tensor_copy(qp[:, 0, t], qf[:, t]))
                done(e.tensor_tensor(qr[:, t], qf[:, t], qp[:, 0, t], ALU.subtract))
                done(e.tensor_copy(qp[:, 1, t], qr[:, t]))
                done(e.tensor_tensor(qr[:, t], qr[:, t], qp[:, 1, t], ALU.subtract))
                e.tensor_copy(qp[:, 2, t], qr[:, t]).then_inc(qp_ok, 1)
                if b == 0:
                    e.wait_ge(vx_one, 1)
                    e.wait_ge(av_ps, 1)
                    for f in range(2):
                        i = e.tensor_tensor(Vx[:, 4 * f:4 * f + 4, :, 0:AD],
                                            ps[:, 2 + f, :].rearrange("p (n h k) -> p n h k", h=AH, k=AD),
                                            abr[:, 0, :].rearrange("p (h k) -> p h k", k=AD).unsqueeze(1).broadcast_to([P, 4, AH, AD]),
                                            ALU.add)
                    i.then_inc(av_sb, 1)
            done(e.tensor_tensor(xb[:, :, :], xN[:, :, :], abr[:, 1:2, :].broadcast_to([P, NT, D]), ALU.add))

            def maxima(s):
                b, r = divmod(s, NSJ)
                f, hp = divmod(r, AH // 2)
                e.wait_ge(as_ps, s + 1)
                if r == 0 and b >= 2:
                    e.wait_ge(am_ps, b - 1)
                e.tensor_reduce(mS[:, b % 2, 4 * hp + f:4 * hp + f + 3:2], ps[:, SBANK[s % 3], :].rearrange("p (h k) -> p h k", h=2),
                                AX.X, ALU.max, negate=True).then_inc(as_used, 1)

            def parts_of_max(b):
                e.wait_ge(am_ps, b + 1)
                if b >= 2:
                    e.wait_ge(am_row[b % 2], 48 * (b // 2))
                o = mb[:, b % 2]
                done(e.tensor_copy(mt[:, 0, :], ps[0:32, 6, 0:P]))
                for i in range(3):
                    e.tensor_copy(o[:, i, :], mt[:, min(i, 1), :]).then_inc(am_parts, 1)
                    if i < 2:
                        e.wait_ge(am_parts, 3 * b + i + 1)
                        done(e.tensor_tensor(mt[:, 1, :], mt[:, i, :], o[:, i, :], ALU.subtract))

            def normalise(b, f):
                e.wait_ge(ac_ps, 2 * b + f + 1)
                tt = ps[:, 6, :].rearrange("p (h k) -> p h k", h=AH)
                done(e.reciprocal(nrm_s[:, f, :], tt[:, :, AD]))
                e.tensor_tensor(aN[:, 2 * b + f, :].rearrange("p (h k) -> p h k", k=AD), tt[:, :, 0:AD],
                                nrm_s[:, f, :].unsqueeze(2).broadcast_to([P, AH, AD]), ALU.mult).then_inc(ah_sb, 1)

            for b in range(NB):
                for r in range(NSJ):
                    maxima(b * NSJ + r)
                    if r == 2 and b >= 3:
                        normalise(b - 3, 1)
                    if r == NSJ - 2 and b >= 2:
                        normalise(b - 2, 0)
                parts_of_max(b)
            for b, f in ((NB - 3, 1), (NB - 2, 0), (NB - 2, 1), (NB - 1, 0), (NB - 1, 1)):
                normalise(b, f)
            e.wait_ge(ah_sb, 2 * NB)
            e.nop().then_inc(ax_ok, NT)
            e.wait_ge(ay_ps, 1)
            done(e.tensor_tensor(zN[:, :, :], ps[:, 4:6, :].rearrange("p b (n d) -> p (b n) d", d=D), xb[:, :, :], ALU.add))
            layer_norm(zN, xN, ln_out)

        PAIRS_Q = ((0, 3), (1, 2), (2, 1))
        PAIRS_K = ((0, 3), (0, 2), (0, 1))

        def sync_softmax(e):
            def load_keys(b):
                row = 0
                for c, n in PAIRS_K:
                    e.dma_start(Kt[b % NSLOT][row:row + n * AD, :, :].rearrange("p h t -> p (h t)"),
                                q_scr[1, b, c:c + n].rearrange("c d n -> (c d) n")).then_inc(slot_ld[b % NSLOT], 16)
                    row += n * AD

            def load_queries(b):
                row = 0
                for c, n in PAIRS_Q:
                    e.dma_start(Qt[b % NSLOT][row:row + n * AD, :, :].rearrange("p h t -> p (h t)"),
                                q_scr[0, b, c].unsqueeze(0).broadcast_to([n, AD, AH * S])).then_inc(slot_ld[b % NSLOT], 16)
                    row += n * AD

            e.wait_ge(slot_clear, 3)
            load_keys(0)
            load_keys(1)
            e.wait_ge(slot_clear, 6)
            load_keys(2)
            for b in range(NB):
                e.wait_ge(qp_ok, b + 1)
                e.dma_start(q_scr[0, b].rearrange("c d (h t) -> (d h) c t", t=S),
                            qp[:, :, b * S:(b + 1) * S]).then_inc(qp_out, 16)
                e.wait_ge(qp_out, 16 * (b + 1))
                if b < NSLOT:
                    load_queries(b)

            def load_max(b):
                for i in range(3):
                    e.wait_ge(am_parts, 3 * b + i + 1)
                    e.dma_start(Qt[b % NSLOT][NR + i:NR + i + 1, :, :].rearrange("o h (f t) -> o (h f) t", f=2),
                                mb[:, b % 2, i, :]).then_inc(am_row[b % 2], 16)

            load_max(0)
            load_max(1)
            for b in range(NSLOT, NB):
                e.wait_ge(at_ps, AH * (b - NSLOT + 1))
                load_keys(b)
                load_queries(b)
            for b in range(2, NB):
                load_max(b)

        LATE.update(values=pe_values, pe_keys=pe_keys, act_keys=act_keys, pool_keys=pool_keys, sync_keys=sync_keys)
        phases["sync"].append(sync_softmax)
        phases["pool"].append(pool_softmax)
        phases["act"].append(act_softmax)
        phases["dve"].append(dve_softmax)
        phases["pe"].append(pe_softmax)
        turn_heads(ax_ok)
        phases["pe"].append(pe_softmax_out)
        turn(4)

        fa = work[:, 0:4 * T].rearrange("p (b k t) -> p b k t", b=2, k=4)
        fb = work[:, 4 * T:8 * T].rearrange("p (b k t) -> p b k t", b=2, k=4)
        sg = work[:, 8 * T:10 * T].rearrange("p (s t) -> p s t", s=4)
        g_ps = sem("g_ps")
        u_ps = sem("u_ps")
        sg_ok = sem("sg_ok")
        h1_ok = sem("h1_ok")
        gel_ps = sem("gel_ps")
        gel_ok = sem("gel_ok")
        fy_ps = sem("fy_ps")

        def pe_ffn(e):
            e.wait_ge(ld_ffn, 16 * 7)
            for j in range(8):
                blk, m = divmod(j, 4)
                if j == 0:
                    e.wait_ge(xt_sb, 13)
                if j == 3:
                    e.wait_ge(xt_sb, 14)
                if j >= 4:
                    e.wait_ge(h1_ok, j - 3)
                t = slice(blk * 512, (blk + 1) * 512)
                e.matmul(ps[:, 2 * (j % 4), :], fw1[:, m * P:(m + 1) * P], xT[:, t], start=True, stop=True).then_inc(g_ps, 1)
                e.matmul(ps[:, 2 * (j % 4) + 1, :], fw2[:, m * P:(m + 1) * P], xT[:, t], start=True, stop=True).then_inc(u_ps, 1)
            for j in range(16):
                layer, blk, m = j // 8, (j // 4) % 2, j % 4
                if j < 8:
                    e.wait_ge(h1_ok, max(4 * (blk + 1), j // 2 + 5))
                else:
                    e.wait_ge(gel_ok, max(4 * (blk + 1), j - 7))
                wt, src = ((fh1, fa), (fh2, fb))[layer]
                for k in range(4):
                    i = e.matmul(ps[:, j % 8, :], wt[:, k, m * P:(m + 1) * P], src[:, blk, k, :], start=(k == 0), stop=(k == 3))
                i.then_inc(gel_ps, 1)
            for n in range(NT):
                blk = n // 4
                if n % 4 == 0:
                    e.wait_ge(gel_ok, 12 + 4 * blk)
                for k in range(4):
                    i = e.matmul(ps[:, blk, (n % 4) * P:(n % 4 + 1) * P], fa[:, blk, k, (n % 4) * P:(n % 4 + 1) * P], fw3[:, k, :],
                                 start=(k == 0), stop=(k == 3))
                if n % 4 == 3:
                    i.then_inc(fy_ps, 1)

        def act_ffn(e):
            for j in range(8):
                e.wait_ge(g_ps, j + 1)
                if j >= 4:
                    e.wait_ge(h1_ok, j - 3)
                e.activation(sg[:, j % 4, :], ps[:, 2 * (j % 4), :], ACT.Silu, scale=fsc[:, 0, j % 4:j % 4 + 1]).then_inc(sg_ok, 1)
            for j in range(16):
                layer, blk, m = j // 8, (j // 4) % 2, j % 4
                e.wait_ge(gel_ps, j + 1)
                if j >= 8:
                    e.wait_ge(gel_ps, 12 if blk == 0 else 16)
                dst = (fb, fa)[layer]
                e.activation(dst[:, blk, m, :], ps[:, j % 8, :], ACT.Gelu, scale=fsc[:, 2 + layer, m:m + 1]).then_inc(gel_ok, 1)

        def dve_ffn(e):
            for j in range(8):
                e.wait_ge(u_ps, j + 1)
                e.wait_ge(sg_ok, j + 1)
                e.scalar_tensor_tensor(fa[:, j // 4, j % 4, :], ps[:, 2 * (j % 4) + 1, :], fsc[:, 1, j % 4:j % 4 + 1],
                                       sg[:, j % 4, :], ALU.mult, ALU.mult).then_inc(h1_ok, 1)
            for b in range(2):
                e.wait_ge(fy_ps, b + 1)
                q = slice(4 * b, 4 * b + 4)
                done(e.tensor_tensor(aN[:, q, :], ps[:, b, :].rearrange("p (n d) -> p n d", d=D),
                                     fs3[:, :].unsqueeze(1).broadcast_to([P, 4, D]), ALU.mult))
                done(e.tensor_tensor(zN[:, q, :], aN[:, q, :], xN[:, q, :], ALU.add))
            layer_norm(zN, xN, ln_out)

        phases["act"].append(act_ffn)
        phases["dve"].append(dve_ffn)
        phases["pe"].append(pe_ffn)

        def sync_tail(e):
            e.wait_ge(ln_out, NT * N_NORMS[0])
            e.dma_start(out.rearrange("(n p) d -> p n d", p=P), xN[:, :, :]).then_inc(fin, 16)
            e.wait_ge(fin, 16)
            for q, n in final_loads:
                e.wait_ge(q, n)

        final_loads = [(ld_ctx, 48), (ld_w1, 80), (ld_moe, 16 * 6), (ld_l1, 16 * 12), (ld_ffn, 16 * 7)]
        N_NORMS = [6]

        @block.sync
        def _(e):
            sync_program(e)

        @block.gpsimd
        def _(e):
            for f in phases["pool"]:
                f(e)

        @block.scalar
        def _(e):
            for f in phases["act"]:
                f(e)

        @block.vector
        def _(e):
            for f in phases["dve"]:
                f(e)

        @block.tensor
        def _(e):
            for f in phases["pe"]:
                f(e)



def _arrays(inputs):

    def by_width(a):
        return np.swapaxes(a.reshape(a.shape[:-1] + (AH, AD)), -1, -2).reshape(a.shape)

    g = {k: np.asarray(a) for k, a in inputs.items()}
    p = np.arange(P)
    c = np.ascontiguousarray
    table = const_table()
    bf = np.zeros((P, 2 * P + 16 * P), np.float32)
    bf[:, 0:P] = np.eye(P)
    bf[:, P:2 * P] = np.where(p[:, None] <= p[None, :], 0, MASKED)
    sel = (p[:, None] % 32 == np.arange(16)[None, :]) & (p[:, None] < 96)
    bf[:, 2 * P:] = np.repeat(sel, P, 1)
    bf = (bf.view(np.uint32) >> 16).astype(np.uint16)
    return {
        "x": c(g["x"].reshape(T, D)), "ctx": c(g["ctx_1024"].reshape(T, D)),
        "xT": c(g["x"].reshape(T, D).T), "ctxT": c(g["ctx_1024"].reshape(T, D).T),
        "consts": table, "cbf": bf,
        "W0T": c(g["L0_attn_W"].T), "ln_gamma": g["L0_attn_ln_gamma"], "ln_beta": g["L0_attn_ln_beta"],
        "lam_logit": g["L0_attn_lam_logit"].reshape(1), "eta": g["L0_attn_eta"].reshape(1),
        "igate_kernel": g["L0_xattn_igate_kernel"], "fgate_kernel": g["L0_xattn_fgate_kernel"],
        "igate_bias": g["L0_xattn_igate_bias"], "fgate_bias": g["L0_xattn_fgate_bias"],
        "outnorm_scale": g["L0_xattn_outnorm_scale"],
        "router_w": g["L0_ffn_router_w"], "w1": g["L0_ffn_w1"], "b1": c(g["L0_ffn_b1"].reshape(E, 2, P).transpose(2, 0, 1).reshape(P, 2 * E)),
        "w2": g["L0_ffn_w2"], "b2": g["L0_ffn_b2"],
        "lqT": c(g["L1_attn_Wq"].T), "lkT": c(g["L1_attn_Wk"].T), "lvT": c(g["L1_attn_Wv"].T),
        "loT": c(g["L1_attn_Wo"].T), "norm_w": g["L1_attn_norm_w"],
        "aWq": c(by_width(g["L1_xattn_Wq"])), "aWk": c(by_width(g["L1_xattn_Wk"])), "aWv": g["L1_xattn_Wv"], "aWo": g["L1_xattn_Wo"],
        "abqk": c(np.stack([by_width(g["L1_xattn_bq"]), by_width(g["L1_xattn_bk"])], 1)), "abv": g["L1_xattn_bv"], "abo": g["L1_xattn_bo"],
        "w1T": c(g["L1_ffn_w1_w"].T), "w2T": c(g["L1_ffn_w2_w"].T), "h1T": c(g["L1_ffn_h1_w"].T),
        "h2T": c(g["L1_ffn_h2_w"].T), "w3T": c(g["L1_ffn_w3_w"].T),
        "hidden_scales": c(np.concatenate([g["L1_ffn_" + n].reshape(4, P).T for n in ("w1_s", "w2_s", "h1_s", "h2_s")], 1)),
        "w3_s": g["L1_ffn_w3_s"],
    }


def _program(nc, arrays, mybir_):
    a = {n: nc.dram_tensor("in_" + n, v.shape, mybir_.dt.from_np(v.dtype), kind="ExternalInput").ap()
         for n, v in arrays.items()}
    out = nc.dram_tensor("out_y", (T, D), F32, kind="ExternalOutput").ap()
    fixed = ("x", "ctx", "xT", "ctxT", "consts", "cbf")
    decoder(nc, a["x"], a["ctx"], a["xT"], a["ctxT"], a["consts"], a["cbf"],
            {n: v for n, v in a.items() if n not in fixed}, out)


def kernel(**inputs):
    import concourse.bacc as _bacc
    from concourse import mybir as _mybir
    from concourse.bass_utils import run_bass_kernel_spmd as _run

    arrays = _arrays(inputs)
    nc = _bacc.Bacc("TRN2", target_bir_lowering=False, num_devices=1)
    _program(nc, arrays, _mybir)
    r = _run(nc, [{"in_" + n: v for n, v in arrays.items()}], core_ids=[0])
    return np.asarray(r.results[0]["out_y"]).reshape(NB, S, D)
```

```python
from contextlib import ExitStack

import numpy as np

import concourse.bass as bass
import concourse.mybir as mybir

F32 = mybir.dt.float32
BF16 = mybir.dt.bfloat16
I32 = mybir.dt.int32
U32 = mybir.dt.uint32
ALU = mybir.AluOpType
ACT = mybir.ActivationFunctionType
AX = mybir.AxisListType

P = 128
D = 128
NB = 4
S = 256
T = NB * S
NT = T // P
HALVES = S // P
DH = 8
C = 16
NJ = S // C
XH, XD = 4, 32
E, FF = 14, 256
NSEG = (T + E * (P - 1)) // P
LH, LD = 8, 16
AH, AD = 16, 8
HID = 512
LN_EPS = 1e-5
MASKED = -float(2 ** 15)

CONST = {}


def const_table():
    p = np.arange(P)[:, None]
    q = np.arange(P)[None, :]
    t = np.arange(C)
    parts = {
        "ident": (p == q),
        "bones": (p // DH == q // DH),
        "causal": np.concatenate([p <= q, np.ones((P, P)), p <= q], 1),
        "hm32": (p % 32 // DH == np.arange(32)[None, :] // DH),
        "pw": np.broadcast_to(t[None, :] + 1, (P, C)),
        "lag": np.broadcast_to(t[None, 1:], (P, C - 1)),
        "age": np.where(p % 32 < C, C - 1 - p % 32, 0),
        "hm4": (p // XD == np.arange(XH)[None, :]),
        "hm8": (p // LD == np.arange(LH)[None, :]),
        "first": np.broadcast_to(np.arange(E * NT)[None, :] % NT > 0, (P, E * NT)),
        "full": np.broadcast_to(P * np.arange(NT)[None, :], (P, NT)),
        "seg": np.broadcast_to(np.arange(NSEG)[None, :], (P, NSEG)),
        "rank": np.broadcast_to(E - np.arange(E)[None, :], (P, E)),
    }
    cols, at = [], 0
    for name, a in parts.items():
        a = np.asarray(a, np.float32)
        CONST[name] = (at, at + a.shape[1])
        at += a.shape[1]
        cols.append(a)
    return np.concatenate(cols, 1)


const_table()
NCONST = max(b for _, b in CONST.values())


def decoder(nc, x, ctx, xT_d, ctxT_d, consts, cbf, w, out):
    es = ExitStack()
    with es:
        def sb(name, shape, dt=F32):
            return es.enter_context(nc.sbuf_tensor(name, shape, dt))

        def sem(name):
            return es.enter_context(nc.semaphore(name))

        cst = sb("cst", [P, NCONST])

        def K(name):
            a, b = CONST[name]
            return cst[:, a:b]

        cb = sb("cb", [P, 2 * P + 16 * P], BF16)
        ident_bf = cb[:, 0:P]
        neg_bf = cb[:, P:2 * P]
        sel_bf = cb[:, 2 * P:].rearrange("p (k m) -> p k m", m=P)

        xT = sb("xT", [P, T])
        xN = sb("xN", [P, NT, D])
        zN = sb("zN", [P, NT, D])
        aN = sb("aN", [P, NT, D])
        bN = sb("bN", [P, NT, D])
        ctxT = sb("ctxT", [P, T])
        ctxN = sb("ctxN", [P, NT, D])
        arena = sb("arena", [P, (C - 1) * T])
        ps = es.enter_context(nc.psum_tensor("ps", [P, 8, 512], F32))

        stats = sb("stats", [P, NT, 6])
        mv = sb("mv", [P, NT, 2])
        rs_v = sb("rs_v", [P, 64])
        rs_t = sb("rs_t", [P, 64])
        rs_y = sb("rs_y", [P, 64])
        rs_h = sb("rs_h", [P, 64])

        ld_c = sem("ld_consts")
        ld_k = sem("ld_k")
        ld_lam = sem("ld_lam")
        ld_x = sem("ld_x")
        ld_w0 = sem("ld_w0")
        ld_g0 = sem("ld_gamma_beta")
        ld_ctx = sem("ld_ctx")
        ld_w1 = sem("ld_w1")
        ld_moe = sem("ld_moe")
        ld_l1 = sem("ld_l1")
        ld_ffn = sem("ld_ffn")
        pool_init = sem("pool_init")
        v = sem("dve_step")
        ln_out = sem("ln_out")
        xt_ps = sem("xt_ps")
        xt_sb = sem("xt_sb")
        fin = sem("stored")
        zero_ok = sem("zero_ok")
        steps = {"n": 0}

        W0 = sb("W0", [P, D])
        lamb = sb("lamb", [P, 2])
        g0 = sb("g0", [P, 2, D])
        wg = sb("wg", [P, 3, 2 * XH])
        wgb = sb("wgb", [P, 2 * XH])
        ons = sb("ons", [P, D])
        wr = sb("wr", [P, E])
        w1 = sb("w1", [P, E, FF + 2])
        w2 = sb("w2", [P, 2, E, D])
        l1w = sb("l1w", [P, 4, D])
        nrm = sb("nrm", [P, 1])
        axw = sb("axw", [P, 4, D])
        abq = sb("abq", [P, 2])
        abr = sb("abr", [P, 2, D])
        fw1 = sb("fw1", [P, HID])
        fw2 = sb("fw2", [P, HID])
        fh1 = arena[:, 10 * T:12 * T].rearrange("p (k f) -> p k f", f=HID)
        fh2 = arena[:, 12 * T:14 * T].rearrange("p (k f) -> p k f", f=HID)
        fw3 = sb("fw3", [P, 4, D])
        fsc = sb("fsc", [P, 4, 4])
        fs3 = sb("fs3", [P, D])

        zero = sb("zero", [P, D])
        xs_scr = nc.dram_tensor("xs_scr", [NSEG * P, D], F32, kind="Internal").ap()
        ys_scr = nc.dram_tensor("ys_scr", [NSEG * P, D], F32, kind="Internal").ap()
        u_scr = nc.dram_tensor("u_scr", [NB, S, D], F32, kind="Internal").ap()
        k_scr = nc.dram_tensor("k_scr", [NB, 3, AD, AH * S], BF16, kind="Internal").ap()

        block = es.enter_context(nc.Block())

        NPR = NB * NJ * (C - 1)
        work = sb("work", [P, 8 * T + 4 * NPR])
        kT = work[:, 0:T]
        kN = work[:, T:2 * T].rearrange("p (n d) -> p n d", d=D)
        kd = work[:, 2 * T:4 * T].rearrange("p (j d) -> p j d", d=D)
        X = work[:, 4 * T:6 * T].rearrange("p (v t) -> p v t", v=2)
        Uall = work[:, 6 * T:8 * T].rearrange("p (j d) -> p j d", d=D)
        prod = work[:, 8 * T:8 * T + 2 * NPR].rearrange("p (s c) -> p s c", s=2)
        tmp = work[:, 8 * T + 2 * NPR:]
        S4 = sb("S4", [P, NB, 32])
        pwt = sb("pwt", [P, 2 * C])
        sc = sb("sc", [P, 12])
        nbl = sb("nbl", [P, C - 1])
        npw = sb("npw", [P, C])
        kap = sb("kap", [P, NT * 16])
        Nn = arena[:, :].rearrange("p (l t) -> p l t", t=T)

        lam_e = sem("lam_e")
        lam_ln = sem("lam_ln")
        lam_dve = sem("lam_dve")
        lam_pw = sem("lam_pw")
        tanh_k = sem("tanh_k")
        kd_tanh = sem("kd_tanh")
        kd_ok = sem("kd_ok")
        kap_ok = sem("kap_ok")
        v_ps = sem("v_ps")
        v_sb = sem("v_sb")
        scal_ok = sem("scal_ok")
        pr_ok = sem("pair_products")
        n_ps = sem("n_ps")
        n_sb = sem("n_sb")
        x_ok = sem("x_ok")
        fs_ok = sem("early_substituted")
        fs_sb = sem("early_in_sbuf")
        fs_late = sem("late_substituted")
        pool_step = sem("pool_step")
        J_DVE = 8
        ch_u = sem("chain_u_ps")
        ch_us = sem("chain_u_sb")
        ch_s = sem("chain_s_ps")
        ch_ss = sem("chain_s_sb")
        u_out = [sem("u_out0"), sem("u_out1")]
        u_in = [sem("u_in0"), sem("u_in1")]
        vn_ps = sem("vn_ps")
        in_stats = sem("inner_stats")
        in_pool = sem("inner_norm_pool")

        N_LAGS = C - 1
        n_of = [NJ * NB // 2 * (C - d) for d in range(1, C)]

        def sync_program(e):
            e.dma_start(kT[:, :], xT_d).then_inc(ld_k, 16)
            e.dma_start(lamb[:, 0:1], w["lam_logit"].partition_broadcast(P)).then_inc(ld_lam, 16)
            e.dma_start(lamb[:, 1:2], w["eta"].partition_broadcast(P)).then_inc(ld_lam, 16)
            e.dma_start(cst[:, :], consts).then_inc(ld_c, 16)
            e.dma_start(W0[:, :], w["W0T"]).then_inc(ld_w0, 16)
            for b in range(NB):
                e.dma_start(kd[32 * b:32 * b + C, :, :],
                            x[b * S:(b + 1) * S, :].rearrange("(j t) d -> t j d", t=C)).then_inc(ld_x, 16)
            e.dma_start(xN[:, :, :], x.rearrange("(n p) d -> p n d", p=P)).then_inc(ld_x, 16)
            e.dma_start(g0[:, 0, :], w["ln_gamma"].partition_broadcast(P)).then_inc(ld_g0, 16)
            e.dma_start(g0[:, 1, :], w["ln_beta"].partition_broadcast(P)).then_inc(ld_g0, 16)
            e.dma_start(cb[:, :], cbf.bitcast(BF16)).then_inc(ld_ctx, 16)
            e.dma_start(ctxT[:, :], ctxT_d).then_inc(ld_ctx, 16)
            e.dma_start(ctxN[:, :, :], ctx.rearrange("(n p) d -> p n d", p=P)).then_inc(ld_ctx, 16)
            e.dma_start(wg[:, :, 0:XH], w["igate_kernel"].rearrange("(g p) h -> p g h", p=P)).then_inc(ld_w1, 16)
            e.dma_start(wg[:, :, XH:], w["fgate_kernel"].rearrange("(g p) h -> p g h", p=P)).then_inc(ld_w1, 16)
            e.dma_start(wgb[:, 0:XH], w["igate_bias"].partition_broadcast(P)).then_inc(ld_w1, 16)
            e.dma_start(wgb[:, XH:], w["fgate_bias"].partition_broadcast(P)).then_inc(ld_w1, 16)
            e.dma_start(ons[:, :], w["outnorm_scale"].partition_broadcast(P)).then_inc(ld_w1, 16)
            e.dma_start(wr[:, :], w["router_w"]).then_inc(ld_moe, 16)
            e.wait_ge(zero_ok, 1)
            e.dma_start(xs_scr.rearrange("(s p) d -> p s d", p=P),
                        zero[:, :].unsqueeze(1).broadcast_to([P, NSEG, D])).then_inc(ld_moe, 16)
            e.dma_start(w1[:, :, 0:FF], w["w1"].rearrange("e d f -> d e f")).then_inc(ld_moe, 16)
            e.dma_start(w1[:, :, FF:], w["b1"].rearrange("p (e f) -> p e f", f=2)).then_inc(ld_moe, 16)
            for half in range(2):
                e.dma_start(w2[:, half, :, :],
                            w["w2"].rearrange("e (c p) d -> c p e d", p=P)[half]).then_inc(ld_moe, 16)
            for i, n in enumerate(("lqT", "lkT", "lvT", "loT")):
                e.dma_start(l1w[:, i, :], w[n]).then_inc(ld_l1, 16)
            e.dma_start(nrm[:, :], w["norm_w"]).then_inc(ld_l1, 16)
            for i, n in enumerate(("aWq", "aWk", "aWv", "aWo")):
                e.dma_start(axw[:, i, :], w[n]).then_inc(ld_l1, 16)
            e.dma_start(abq[:, :], w["abqk"]).then_inc(ld_l1, 16)
            for i, n in enumerate(("abv", "abo")):
                e.dma_start(abr[:, i, :], w[n].partition_broadcast(P)).then_inc(ld_l1, 16)
            e.dma_start(fw1[:, :], w["w1T"]).then_inc(ld_ffn, 16)
            e.dma_start(fw2[:, :], w["w2T"]).then_inc(ld_ffn, 16)
            e.wait_ge(fs_ok, 1)
            e.wait_ge(fs_late, 1)
            e.dma_start(fh1[:, :, :], w["h1T"].rearrange("(k p) f -> p k f", p=P)).then_inc(ld_ffn, 16)
            e.dma_start(fh2[:, :, :], w["h2T"].rearrange("(k p) f -> p k f", p=P)).then_inc(ld_ffn, 16)
            e.dma_start(fw3[:, :, :], w["w3T"].rearrange("(k p) d -> p k d", p=P)).then_inc(ld_ffn, 16)
            e.dma_start(fsc[:, :, :], w["hidden_scales"].rearrange("p (i k) -> p i k", i=4)).then_inc(ld_ffn, 16)
            e.dma_start(fs3[:, :], w["w3_s"].partition_broadcast(P)).then_inc(ld_ffn, 16)
            e.wait_ge(ch_us, NJ)
            for b in range(NB):
                e.dma_start(u_scr[b].rearrange("(j t) d -> t j d", t=C),
                            Uall[32 * b:32 * b + C, :, :]).then_inc(u_out[b // 2], 16)
            for h in range(2):
                e.wait_ge(u_out[h], 32)
                e.dma_start(aN[:, 4 * h:4 * h + 4, :],
                            u_scr[2 * h:2 * h + 2].rearrange("b (n p) d -> p (b n) d", p=P)).then_inc(u_in[h], 16)
            for f in phases["sync"]:
                f(e)
            sync_tail(e)

        def done(ins, wait=True):
            steps["n"] += 1
            ins.then_inc(v, 1)
            if wait:
                nc.vector.wait_ge(v, steps["n"])

        def rsqrt(src, n, first=0):
            e = nc.vector
            y, h, u = (a[:, first:first + n] for a in (rs_y, rs_h, rs_t))
            done(e.tensor_scalar(u.bitcast(I32), src.bitcast(I32), 1, None, ALU.logical_shift_right))
            done(e.tensor_scalar(y.bitcast(I32), u.bitcast(I32), -1.0, 1597463007.0, ALU.mult, ALU.add))
            done(e.scalar_tensor_tensor(h, src, -0.5, y, ALU.mult, ALU.mult))
            for i in range(3):
                done(e.tensor_tensor(u, h, y, ALU.mult))
                if i < 2:
                    done(e.scalar_tensor_tensor(h, u, 1.5, h, ALU.add, ALU.mult), wait=False)
                done(e.scalar_tensor_tensor(y, u, 1.5, y, ALU.add, ALU.mult))

        def norm_stats(src, stats_taken, first, last):
            e = nc.vector
            if not stats_taken:
                for n in range(first, last):
                    done(e.bn_stats(stats[:, n, :], src[:, n, :]), wait=(n == last - 1))
            for n in range(first, last):
                done(e.bn_aggr(mv[:, n, :], stats[:, n, :]), wait=(n == last - 1))
            done(e.tensor_scalar(rs_v[:, first:last], mv[:, first:last, 1], LN_EPS, None, ALU.add))
            rsqrt(rs_v[:, first:last], last - first, first)

        def layer_norm(src, dst, last_sem=None, stats_taken=False, first=0, last=NT):
            norm_stats(src, stats_taken, first, last)
            for n in range(first, last):
                i = nc.vector.tensor_scalar(dst[:, n, :], src[:, n, :], mv[:, n, 0:1], rs_y[:, n:n + 1],
                                            ALU.subtract, ALU.mult)
                if last_sem is None:
                    done(i, wait=(n == last - 1))
                else:
                    i.then_inc(last_sem, 1)

        def add_half(h, bank, other):
            e = nc.vector
            q = slice(4 * h, 4 * h + 4)
            done(e.tensor_tensor(zN[:, q, :], ps[:, bank, :].rearrange("p (n d) -> p n d", d=D), other[:, q, :], ALU.add))
            for n in range(4 * h, 4 * h + 4):
                done(e.bn_stats(stats[:, n, :], zN[:, n, :]), wait=(n == NT - 1))

        turns = {"pe": 0, "act": 0}

        def pe_turn(src, ready, base, banks=(6, 7), halves=(0, 1)):
            if 0 in halves:
                if turns["pe"]:
                    nc.tensor.wait_ge(xt_sb, 2 * turns["pe"])
                turns["pe"] += 1
            for h in halves:
                for n in range(4 * h, 4 * h + 4):
                    nc.tensor.wait_ge(ready, base + n + 1)
                    nc.tensor.transpose(ps[:, banks[h], (n % 4) * P:(n % 4 + 1) * P], src[:, n, :],
                                        K("ident")).then_inc(xt_ps, 1)

        def act_turn(dst, banks=(6, 7), halves=(0, 1)):
            turns["act"] += 0 in halves
            k = turns["act"] - 1
            for h in halves:
                nc.scalar.wait_ge(xt_ps, NT * k + 4 * (h + 1))
                nc.scalar.copy(dst[:, h * 512:(h + 1) * 512], ps[:, banks[h], :]).then_inc(xt_sb, 1)

        X_ps = [ps[:, 2 * a:2 * a + 2, :].rearrange("p b c -> p (b c)") for a in (0, 3)]

        def chunks(a, j0, j1):
            return a.rearrange("p (b j t) -> p b j t", b=NB, t=C)[:, :, j0:j1, :]

        def substitute(e, count, base, rhs, scratch, j0, j1):
            nj = j1 - j0
            Xc = [a.rearrange("p (b j t) -> p b j t", b=NB, t=C) for a in rhs]
            n_done = base
            for s in range(C - 1):
                n = C - 1 - s
                pairs = bass.AP(arena, j0 * C + s + 1, [[(C - 1) * T, P], [S, NB], [C, nj], [T + 1, n]])
                for a in range(2):
                    t4 = scratch[:, a * NB * nj * n:(a + 1) * NB * nj * n].rearrange("p (b j t) -> p b j t", b=NB, j=nj)
                    if s:
                        e.wait_ge(count, n_done - 1)
                    e.tensor_tensor(t4, pairs, Xc[a][:, :, j0:j1, s:s + 1].broadcast_to([P, NB, nj, n]),
                                    ALU.mult).then_inc(count, 1)
                    n_done += 1
                for a in range(2):
                    t4 = scratch[:, a * NB * nj * n:(a + 1) * NB * nj * n].rearrange("p (b j t) -> p b j t", b=NB, j=nj)
                    e.wait_ge(count, n_done - 1)
                    row = Xc[a][:, :, j0:j1, s + 1:]
                    i = e.tensor_tensor(row, row, t4, ALU.add)
                    if s == C - 2 and a:
                        e_last = i
                    else:
                        i.then_inc(count, 1)
                        n_done += 1
            return e_last

        def pool_delta(e):
            e.memset(zero[:, :], 0.0).then_inc(zero_ok, 1)
            e.memset(S4[:, :, :], 0.0).then_inc(pool_init, 1)
            e.wait_ge(v_sb, 1)
            e.wait_ge(x_ok, 1)
            e.wait_ge(n_sb, 2 * N_LAGS)
            substitute(e, pool_step, 0, (X[:, 0, :], X[:, 1, :]), prod.rearrange("p s c -> p (s c)"), J_DVE, NJ).then_inc(fs_late, 1)
            e.wait_ge(tanh_k, 2)
            e.tensor_tensor(bN[:, :, :], kN[:, :, :], kN[:, :, :], ALU.mult).then_inc(kap_ok, 1)
            e.wait_ge(kap_ok, 1)
            k8 = bN[:, :, :].rearrange("p n (h k) -> p (n h) k", k=DH)
            for i, n in enumerate((4, 2)):
                e.tensor_tensor(k8[:, :, 0:n], k8[:, :, 0:n], k8[:, :, n:2 * n], ALU.add).then_inc(kap_ok, 1)
                e.wait_ge(kap_ok, 2 + i)
            e.tensor_tensor(kap[:, :], k8[:, :, 0], k8[:, :, 1], ALU.add).then_inc(kap_ok, 1)
            e.wait_ge(kap_ok, 4)
            e.tensor_scalar(kap[:, :], kap[:, :], sc[:, 10:11], 1.0, ALU.mult, ALU.add).then_inc(kap_ok, 1)
            e.wait_ge(ld_g0, 32)
            e.tensor_tensor(bN[:, :, :], xN[:, :, :], g0[:, 1:2, :].broadcast_to([P, NT, D]), ALU.add).then_inc(kap_ok, 1)

        def act_delta(e):
            e.wait_ge(ld_k, 16)
            e.activation(kT[:, :], kT[:, :], ACT.Tanh).then_inc(tanh_k, 1)
            e.wait_ge(lam_dve, 1)
            e.activation(sc[:, 3:4], sc[:, 0:1], ACT.Exp, scale=-1.0).then_inc(lam_e, 1)
            e.activation(sc[:, 4:5], lamb[:, 0:1], ACT.Exp, scale=-1.0).then_inc(lam_e, 1)
            e.wait_ge(lam_e, 1)
            e.activation(sc[:, 5:6], sc[:, 3:4], ACT.Ln, bias=1.0).then_inc(lam_ln, 1)
            e.wait_ge(lam_dve, 2)
            e.wait_ge(ld_c, 16)
            e.activation(pwt[:, :], cst[:, CONST["pw"][0]:CONST["age"][1]], ACT.Exp,
                         scale=sc[:, 6:7]).then_inc(lam_pw, 1)
            e.wait_ge(v_ps, 2)
            e.copy(chunks(X[:, 0, :], J_DVE, NJ), chunks(X_ps[0], J_DVE, NJ)).then_inc(v_sb, 1)
            e.wait_ge(scal_ok, 1)
            i = 0
            for lag in range(1, C):
                for h in range(2):
                    e.wait_ge(n_ps, i + 1)
                    dst = Nn[:, lag - 1, :].rearrange("p (c t) -> p c t", t=C)[:, 32 * h:32 * h + 32, lag:]
                    e.activation(dst, ps[:, 2 + i % 4, 0:n_of[lag - 1]].rearrange("p (c t) -> p c t", c=32),
                                 ACT.Copy, scale=nbl[:, lag - 1:lag]).then_inc(n_sb, 1)
                    i += 1
            e.wait_ge(ld_x, 16 * 5)
            for b in range(NB):
                q = slice(32 * b, 32 * b + C)
                e.activation(kd[q, :, :], kd[q, :, :], ACT.Tanh).then_inc(kd_tanh, 1)
            e.activation(kN[:, :, :], xN[:, :, :], ACT.Tanh).then_inc(tanh_k, 1)
            for b in range(NB):
                q = slice(32 * b, 32 * b + C)
                e.wait_ge(kd_tanh, b + 1)
                e.activation(kd[q, :, :], kd[q, :, :], ACT.Copy, scale=sc[q, 11:12]).then_inc(kd_ok, 1)
            e.wait_ge(fs_ok, 1)
            for a in range(2):
                e.copy(chunks(X[:, a, :], 0, J_DVE), chunks(X_ps[a], 0, J_DVE)).then_inc(fs_sb, 1)

        def dve_delta(e):
            e.wait_ge(ld_lam, 32)
            done(e.scalar_tensor_tensor(sc[:, 0:1], lamb[:, 0:1], -1.0, lamb[:, 0:1], ALU.mult, ALU.max), wait=False)
            done(e.tensor_scalar(sc[:, 1:2], lamb[:, 0:1], 0.0, None, ALU.min))
            e.nop().then_inc(lam_dve, 1)
            e.wait_ge(tanh_k, 1)

            def k3(a, b):
                return kT[:, :].rearrange("p (c t) -> p c t", t=C)[:, :, a:b]

            def products(lag):
                if lag > 2:
                    e.wait_ge(n_ps, 2 * (lag - 2))
                e.tensor_tensor(prod[:, lag % 2, 0:2 * n_of[lag - 1]].rearrange("p (c t) -> p c t", c=NB * NJ),
                                k3(lag, C), k3(0, C - lag), ALU.mult).then_inc(pr_ok, 1)

            products(1)
            e.wait_ge(lam_e, 2)
            done(e.tensor_scalar(sc[:, 7:8], sc[:, 4:5], 1.0, None, ALU.add))
            done(e.reciprocal(sc[:, 8:9], sc[:, 7:8]))
            done(e.tensor_scalar(sc[:, 9:10], sc[:, 8:9], -1.0, 1.0, ALU.mult, ALU.add))
            done(e.tensor_scalar(sc[:, 9:10], sc[:, 9:10], lamb[:, 1:2], 1.0 / DH, ALU.mult, ALU.mult))
            done(e.tensor_scalar(sc[:, 10:11], sc[:, 9:10], -1.0, None, ALU.mult))
            e.wait_ge(lam_ln, 1)
            e.tensor_tensor(sc[:, 6:7], sc[:, 1:2], sc[:, 5:6], ALU.subtract).then_inc(lam_dve, 1)
            products(2)
            e.wait_ge(lam_pw, 1)
            done(e.tensor_scalar(nbl[:, :], pwt[:, C:2 * C - 1], sc[:, 10:11], None, ALU.mult))
            done(e.tensor_scalar(npw[:, :], pwt[:, 0:C], -1.0, None, ALU.mult))
            done(e.tensor_scalar(sc[:, 11:12], pwt[:, 2 * C - 1:2 * C], sc[:, 9:10], None, ALU.mult))
            e.nop().then_inc(scal_ok, 1)
            for lag in range(3, C):
                products(lag)
            for dst, j0, j1 in ((X[:, 1, :], J_DVE, NJ), (X_ps[1], 0, J_DVE)):
                done(e.tensor_tensor(chunks(dst, j0, j1), chunks(kT, j0, j1),
                                     npw[:, :].unsqueeze(1).unsqueeze(1).broadcast_to([P, NB, j1 - j0, C]), ALU.mult))
            e.nop().then_inc(x_ok, 1)
            e.wait_ge(v_sb, 1)
            e.wait_ge(n_sb, 2 * N_LAGS)
            substitute(e, v, steps["n"], X_ps, tmp, 0, J_DVE).then_inc(fs_ok, 1)
            steps["n"] += 4 * (C - 1) - 1
            for j in range(NJ):
                e.wait_ge(ch_u, j + 1)
                e.tensor_copy(Uall[:, j, :].rearrange("p (g c) -> p g c", g=4), ps[:, 0:4, 0:32]).then_inc(ch_us, 1)
                if j == NJ - 1:
                    break
                e.wait_ge(ch_s, j + 1)
                t3 = tmp[:, 0:NB * 32].rearrange("p (b c) -> p b c", b=NB)
                done(e.tensor_tensor(t3, ps[:, 4:8, 0:32], K("hm32").unsqueeze(1).broadcast_to([P, NB, 32]), ALU.mult))
                e.scalar_tensor_tensor(S4[:, :, :], S4[:, :, :], pwt[:, C - 1:C], t3, ALU.mult, ALU.add).then_inc(ch_ss, 1)

        def pe_delta(e):
            e.wait_ge(tanh_k, 1)
            e.wait_ge(ld_w0, 16)
            e.wait_ge(ld_c, 16)
            e.wait_ge(pool_init, 1)
            for h in range(2):
                e.matmul(ps[:, h, :], W0[:, :], kT[:, h * 512:(h + 1) * 512], start=True, stop=True).then_inc(v_ps, 1)
            i = 0
            for lag in range(1, C):
                e.wait_ge(pr_ok, lag)
                for h in range(2):
                    if i >= 4:
                        e.wait_ge(n_sb, i - 3)
                    n = n_of[lag - 1]
                    e.matmul(ps[:, 2 + i % 4, 0:n], K("bones"), prod[:, lag % 2, h * n:(h + 1) * n],
                             start=True, stop=True).then_inc(n_ps, 1)
                    i += 1
            e.wait_ge(fs_sb, 2)
            for j in range(NJ):
                if j == J_DVE:
                    e.wait_ge(fs_late, 1)
                if j:
                    e.wait_ge(ch_us, j)
                for b in range(NB):
                    for g in range(4):
                        q = slice(32 * g, 32 * g + 32)
                        c0 = b * S + j * C
                        m = e.matmul(ps[32 * b:32 * b + C, g, 0:32], X[q, 0, c0:c0 + C], cst[q, CONST["ident"][0] + 32 * g:CONST["ident"][0] + 32 * g + 32],
                                     start=True, stop=(j == 0))
                if j:
                    e.wait_ge(ch_ss, j)
                    for g in range(4):
                        for b in range(NB):
                            q = slice(32 * g, 32 * g + 32)
                            c0 = b * S + j * C
                            m = e.matmul(ps[32 * b:32 * b + C, g, 0:32], X[q, 1, c0:c0 + C], S4[q, b, :],
                                         start=False, stop=True)
                m.then_inc(ch_u, 1)
                if j == NJ - 1:
                    break
                e.wait_ge(ch_us, j + 1)
                if j == 0:
                    e.wait_ge(kd_ok, NB)
                for b in range(NB):
                    q = slice(32 * b, 32 * b + C)
                    for g in range(4):
                        m = e.matmul(ps[32 * g:32 * g + 32, 4 + b, 0:32], kd[q, j, 32 * g:32 * g + 32],
                                     Uall[q, j, 32 * g:32 * g + 32], start=True, stop=True)
                m.then_inc(ch_s, 1)
            e.wait_ge(ch_us, NJ)
            for n in range(NT):
                m = e.matmul(ps[:, n // 4, (n % 4) * P:(n % 4 + 1) * P], kT[:, n * P:(n + 1) * P], W0[:, :],
                             start=True, stop=True)
            m.then_inc(vn_ps, 1)
            EARLY["pe_gates"](e)

        def dve_delta_out(e):
            e.wait_ge(kap_ok, 6)
            EARLY["dve_gates"](e)
            e.wait_ge(vn_ps, 1)
            for h in range(2):
                q = slice(4 * h, 4 * h + 4)
                e.wait_ge(u_in[h], 16)
                a8 = aN[:, q, :].rearrange("p n (h k) -> p (n h) k", k=DH)
                done(e.tensor_tensor(a8, a8, kap[:, 64 * h:64 * h + 64].unsqueeze(2).broadcast_to([P, NT * 8, DH]), ALU.mult))
                done(e.scalar_tensor_tensor(zN[:, q, :], ps[:, h, :].rearrange("p (n d) -> p n d", d=D), 2.0, aN[:, q, :],
                                            ALU.mult, ALU.subtract))
                for n in range(4 * h, 4 * h + 4):
                    done(e.bn_stats(stats[:, n, :], zN[:, n, :]), wait=(n == NT - 1))
            norm_stats(zN, True, 0, NT)
            e.nop().then_inc(in_stats, 1)
            inner_norm(e, 0, N_IN, done)
            for n in range(N_IN):
                done(e.bn_stats(stats[:, n, :], zN[:, n, :]), wait=False)
            e.wait_ge(in_pool, NT - N_IN + 2)
            for n in range(N_IN, NT):
                done(e.bn_stats(stats[:, n, :], zN[:, n, :]), wait=(n == NT - 1))
            layer_norm(zN, xN, ln_out, stats_taken=True)

        N_IN = 6

        def inner_norm(e, first, last, step):
            e.wait_ge(ld_g0, 32)
            for n in range(first, last):
                step(e.tensor_scalar(aN[:, n, :], zN[:, n, :], mv[:, n, 0:1], rs_y[:, n:n + 1], ALU.subtract, ALU.mult),
                     n == last - 1)
            q = slice(first, last)
            step(e.tensor_tensor(aN[:, q, :], aN[:, q, :], g0[:, 0:1, :].broadcast_to([P, last - first, D]), ALU.mult))
            step(e.tensor_tensor(zN[:, q, :], aN[:, q, :], bN[:, q, :], ALU.add))

        def pool_inner_norm(e):
            e.wait_ge(in_stats, 1)
            count = [0]

            def step(i, wait=True):
                count[0] += 1
                i.then_inc(in_pool, 1)
                if wait:
                    e.wait_ge(in_pool, count[0])
            inner_norm(e, N_IN, NT, step)

        phases = {"sync": [], "pool": [pool_delta, pool_inner_norm], "act": [act_delta], "dve": [dve_delta, dve_delta_out], "pe": [pe_delta]}

        EARLY = {}

        def turn(n_before):
            def pe(e):
                pe_turn(xN, ln_out, NT * n_before)

            def act(e):
                act_turn(xT)
            phases["pe"].append(pe)
            phases["act"].append(act)

        turn(0)


        wgc = sb("wgc", [P, 2 * XH])
        gc = sb("gc", [P, NT, 2 * XH])
        gt = sb("gt", [P, NT, 2 * XH])
        nf = sb("nf", [P, NT, XH])
        af = sb("af", [P, NT, XH])
        lf = sb("lf", [P, HALVES, 16])
        gg = sb("gg", [P, HALVES, 16])
        cs = sb("cs", [P, HALVES, 16])
        enm = sb("enm", [P, HALVES, 16])
        gT = sb("gT", [16, S])
        mT = sb("mT", [16, 2, S])
        m3 = sb("m3", [96, S], BF16)
        mp = sb("mp", [16, 2, S], BF16)
        Qz = arena[:, 0:8 * T].rearrange("p (h t) -> p h t", t=T)
        Va = arena[:, 8 * T:10 * T].rearrange("p (n h k) -> p n h k", n=NT, h=XH)
        Dm = work[:, 6 * T:6 * T + 768].rearrange("p (s c) -> p s c", s=2)
        CT = work[:, 6 * T + 768:6 * T + 768 + 4 * 384].rearrange("p (s c) -> p s c", s=4)
        Oxs = work[:, 9 * T:9 * T + 512]
        nrm_s = sb("nrm_s", [P, HALVES, 16])
        nrm_a = sb("nrm_a", [P, HALVES, 16])
        hs1 = sb("hs1", [P, 64])
        gate_c = sem("gate_ctx_ps")
        gate_x = sem("gate_x_ps")
        gate_w = sem("gate_w")
        gf_ok = sem("gate_f_split")
        gl_ok = sem("gate_log")
        lf_ok = sem("log_f")
        cs_ps = sem("cs_ps")
        gg_ok = sem("g_ok")
        gT_ps = sem("gT_ps")
        m_ok = sem("m_ok")
        m3_ok = sem("m3_ok")
        mN_ps = sem("mN_ps")
        em_in = sem("em_in")
        em_ok = sem("em_ok")
        va_ok = sem("va_ok")
        qz_ok = sem("qz_ok")
        e_ps = sem("e_ps")
        s_ps = sem("s_ps")
        d_sb = sem("d_sb")
        ct_sb = sem("ct_sb")
        pv_ps = sem("pv_ps")
        o_sb = sem("o_sb")
        t_ps = sem("t_ps")
        h_sb = sem("h_sb")
        NXH = NB * XH

        def pool_mlstm(e):
            e.wait_ge(fs_ok, 1)
            e.wait_ge(fs_late, 1)
            e.memset(Va[:, :, :, XD:], 1.0).then_inc(va_ok, 1)
            e.memset(m3[:, :], 0.0).then_inc(va_ok, 1)
            e.wait_ge(ld_ctx, 48)
            e.tensor_copy(Va[:, :, :, 0:XD], ctxN[:, :, :].rearrange("p n (h k) -> p n h k", k=XD)).then_inc(va_ok, 1)

        def dve_mlstm_gates(e):
            e.wait_ge(ld_w1, 80)
            e.tensor_tensor(wgc[:, :], wg[:, 1, :], wg[:, 2, :], ALU.add).then_inc(gate_w, 1)
            e.wait_ge(gate_c, 1)
            done(e.tensor_tensor(gc[:, :, :], ps[:, 5, 0:64].rearrange("p (n g) -> p n g", n=NT),
                                 wgb[:, :].unsqueeze(1).broadcast_to([P, NT, 2 * XH]), ALU.add))

        def dve_mlstm(e):
            def one_head(h):
                e.tensor_scalar(Qz[:, h, :], xT[:, :], K("hm4")[:, h:h + 1], None, ALU.mult).then_inc(qz_ok, 1)

            e.wait_ge(gate_x, 1)
            done(e.tensor_tensor(gt[:, :, :], ps[:, 4, 0:64].rearrange("p (n g) -> p n g", n=NT), gc[:, :, :], ALU.add))
            f = gt[:, :, XH:]
            done(e.tensor_scalar(nf[:, :, :], f, 0.0, None, ALU.min), wait=False)
            done(e.scalar_tensor_tensor(af[:, :, :], f, -1.0, f, ALU.mult, ALU.max))
            e.nop().then_inc(gf_ok, 1)
            one_head(0)
            one_head(1)
            e.wait_ge(gl_ok, 2)
            e.tensor_tensor(lf[:, :, :].rearrange("p f (b h) -> p b f h", h=XH),
                            nf[:, :, :].rearrange("p (b f) h -> p b f h", f=HALVES),
                            af[:, :, :].rearrange("p (b f) h -> p b f h", f=HALVES), ALU.subtract).then_inc(lf_ok, 1)
            one_head(2)
            one_head(3)
            e.wait_ge(cs_ps, 1)
            done(e.tensor_copy(cs[:, :, :], ps[:, 4, 64:96].rearrange("p (f k) -> p f k", f=HALVES)))
            e.tensor_tensor(gg[:, :, :].rearrange("p f (b h) -> p b f h", h=XH),
                            gt[:, :, 0:XH].rearrange("p (b f) h -> p b f h", f=HALVES),
                            cs[:, :, :].rearrange("p f (b h) -> p b f h", h=XH), ALU.subtract).then_inc(gg_ok, 1)
            e.wait_ge(gT_ps, 1)
            done(e.tensor_copy(gT[:, :], ps[0:16, 5, 0:S]))
            e.tensor_tensor_scan(mT[:, 0, :], gT[:, :], gT[:, :], -3.0e38, ALU.max, ALU.max).then_inc(m_ok, 1)
            e.wait_ge(va_ok, 3)
            e.wait_ge(m_ok, 1)
            done(e.tensor_scalar(mT[:, 1, :], mT[:, 0, :], -1.0, None, ALU.mult))
            done(e.tensor_copy(m3[0:16, :], mT[:, 1, :]))
            done(e.tensor_tensor(mT[:, 1, :], mT[:, 1, :], m3[0:16, :], ALU.subtract))
            done(e.tensor_copy(mp[:, 0, :], mT[:, 1, :]))
            done(e.tensor_tensor(mT[:, 1, :], mT[:, 1, :], mp[:, 0, :], ALU.subtract), wait=False)
            done(e.tensor_copy(m3[32:48, :], mp[:, 0, :]))
            e.tensor_copy(m3[64:80, :], mT[:, 1, :]).then_inc(m3_ok, 1)
            e.wait_ge(mN_ps, 1)
            e.tensor_tensor(enm[:, :, :], ps[:, 5, 256:288].rearrange("p (f k) -> p f k", f=HALVES), cs[:, :, :],
                            ALU.add).then_inc(em_in, 1)

            def weigh(k):
                e.wait_ge(s_ps, k + 1)
                e.wait_ge(d_sb, k + 1)
                if k >= 4 and k % 2 == 0:
                    e.wait_ge(pv_ps, k // 2 - 1)
                e.scalar_tensor_tensor(CT[:, k % 4, :], ps[:, 2 + k % 2, 0:384], float(XD) ** -0.5, Dm[:, k % 2, :],
                                       ALU.mult, ALU.mult).then_inc(ct_sb, 1)

            def normalise(b):
                e.wait_ge(t_ps, b + 1)
                tt = ps[:, 5, :].rearrange("p (f h k) -> p f h k", f=HALVES, h=XH)
                done(e.tensor_copy(nrm_s[:, :, 0:XH], tt[:, :, :, XD]))
                done(e.scalar_tensor_tensor(nrm_a[:, :, 0:XH], nrm_s[:, :, 0:XH], -1.0, nrm_s[:, :, 0:XH], ALU.mult, ALU.max))
                done(e.tensor_tensor(nrm_a[:, :, 0:XH], nrm_a[:, :, 0:XH], enm[:, :, XH * b:XH * b + XH], ALU.max))
                done(e.tensor_scalar(nrm_a[:, :, 0:XH], nrm_a[:, :, 0:XH], 1e-6, None, ALU.add))
                done(e.reciprocal(nrm_s[:, :, 0:XH], nrm_a[:, :, 0:XH]))
                e.tensor_tensor(aN[:, 2 * b:2 * b + 2, :].rearrange("p f (h k) -> p f h k", k=XD), tt[:, :, :, 0:XD],
                                nrm_s[:, :, 0:XH].unsqueeze(3).broadcast_to([P, HALVES, XH, XD]), ALU.mult).then_inc(h_sb, 1)

            g32 = aN[:, :, :].rearrange("p n (h k) -> p (n h) k", k=XD)
            b32 = bN[:, :, :].rearrange("p n (h k) -> p (n h) k", k=XD)
            G = NT * XH

            def head_norm(b, part):
                q = slice(b * G // NB, (b + 1) * G // NB)
                if part == 0:
                    e.wait_ge(h_sb, b + 1)
                    done(e.tensor_reduce(hs1[:, q], g32[:, q, :], AX.X, ALU.add))
                    done(e.tensor_scalar(hs1[:, q], hs1[:, q], 1.0 / XD, None, ALU.mult))
                    done(e.tensor_tensor(g32[:, q, :], g32[:, q, :], hs1[:, q].unsqueeze(2).broadcast_to([P, G // NB, XD]),
                                         ALU.subtract))
                else:
                    done(e.tensor_tensor(b32[:, q, :], g32[:, q, :], g32[:, q, :], ALU.mult))
                    done(e.tensor_reduce(hs1[:, q], b32[:, q, :], AX.X, ALU.add), wait=False)
                    n = slice(b * NT // NB, (b + 1) * NT // NB)
                    done(e.tensor_tensor(aN[:, n, :], aN[:, n, :], ons[:, :].unsqueeze(1).broadcast_to([P, NT // NB, D]), ALU.mult))

            e.wait_ge(em_ok, 1)
            for k in range(NXH):
                weigh(k)
                if k % XH == 3 and k > XH:
                    normalise(k // XH - 1)
                if k % XH < 2 and k >= 2 * XH:
                    head_norm(k // XH - 2, k % XH)
            for part in range(2):
                head_norm(NB - 2, part)
            normalise(NB - 1)
            for part in range(2):
                head_norm(NB - 1, part)
            done(e.tensor_scalar(rs_v[:, 0:G], hs1[:, 0:G], 1.0 / XD, LN_EPS, ALU.mult, ALU.add))
            rsqrt(rs_v[:, 0:G], G)
            done(e.tensor_tensor(g32, g32, rs_y[:, 0:G].unsqueeze(2).broadcast_to([P, G, XD]), ALU.mult))
            done(e.tensor_tensor(zN[:, :, :], aN[:, :, :], xN[:, :, :], ALU.add))
            layer_norm(zN, xN, ln_out)

        def act_mlstm(e):
            e.wait_ge(gf_ok, 1)
            e.activation(af[:, :, :], af[:, :, :], ACT.Exp, scale=-1.0).then_inc(gl_ok, 1)
            e.wait_ge(gl_ok, 1)
            e.activation(af[:, :, :], af[:, :, :], ACT.Ln, bias=1.0).then_inc(gl_ok, 1)
            e.wait_ge(em_in, 1)
            e.activation(enm[:, :, :], enm[:, :, :], ACT.Exp, scale=-1.0).then_inc(em_ok, 1)

            def decays(k):
                b, h = divmod(k, XH)
                e.wait_ge(e_ps, k + 1)
                if k >= 2:
                    e.wait_ge(ct_sb, k - 1)
                e.activation(Dm[:, k % 2, 0:S], ps[:, k % 2, 0:S], ACT.Exp, bias=gg[:, 0, k:k + 1])
                e.activation(Dm[:, k % 2, S:], ps[:, k % 2, S:384], ACT.Exp, bias=gg[:, 1, k:k + 1]).then_inc(d_sb, 1)

            def take_out(b):
                e.wait_ge(pv_ps, XH // 2 * (b + 1))
                if b:
                    e.wait_ge(t_ps, b)
                e.copy(Oxs[:, :], ps[:, 4, :]).then_inc(o_sb, 1)

            for k in range(NXH):
                decays(k)
                if k % 4 == 1 and k > 4:
                    take_out(k // 4 - 1)
            take_out(NB - 1)

        def pe_mlstm_gates(e):
            e.wait_ge(gate_w, 1)
            e.wait_ge(ld_ctx, 48)
            for n in range(NT):
                m = e.matmul(ps[:, 5, 8 * n:8 * n + 8], ctxT[:, n * P:(n + 1) * P], wgc[:, :], start=True, stop=True)
            m.then_inc(gate_c, 1)

        EARLY.update(dve_gates=dve_mlstm_gates, pe_gates=pe_mlstm_gates)

        def pe_mlstm(e):
            for n in range(NT):
                if n % 4 == 0:
                    e.wait_ge(xt_sb, 1 + n // 4)
                m = e.matmul(ps[:, 4, 8 * n:8 * n + 8], xT[:, n * P:(n + 1) * P], wg[:, 0, :], start=True, stop=True)
            m.then_inc(gate_x, 1)
            e.wait_ge(lf_ok, 1)
            e.matmul(ps[:, 4, 64:80], K("causal")[:, 0:P], lf[:, 0, :], start=True, stop=True)
            e.matmul(ps[:, 4, 80:96], K("causal")[:, P:2 * P], lf[:, 0, :], start=True, stop=False)
            e.matmul(ps[:, 4, 80:96], K("causal")[:, 0:P], lf[:, 1, :], start=False, stop=True).then_inc(cs_ps, 1)
            e.wait_ge(gg_ok, 1)
            e.transpose(ps[0:16, 5, 0:P], gg[:, 0, :], K("ident"))
            e.transpose(ps[0:16, 5, P:S], gg[:, 1, :], K("ident")).then_inc(gT_ps, 1)
            e.wait_ge(m_ok, 1)
            e.transpose(ps[:, 5, 256:272], mT[:, 0, 0:P], K("ident")[0:16, 0:16])
            e.transpose(ps[:, 5, 272:288], mT[:, 0, P:S], K("ident")[0:16, 0:16]).then_inc(mN_ps, 1)
            e.wait_ge(m3_ok, 1)
            e.wait_ge(qz_ok, XH)

            def logits(k):
                b, h = divmod(k, XH)
                if k >= 2:
                    e.wait_ge(d_sb, k - 1)
                E_ = ps[:, k % 2, :]
                e.matmul(E_[:, 0:S], sel_bf[0:96, k, :], m3[:, :], start=True, stop=False, skip_group_check=True)
                e.matmul(E_[:, S:384], sel_bf[0:96, k, :], m3[:, P:S], start=False, stop=False, skip_group_check=True)
                e.matmul(E_[:, 0:P], ident_bf, neg_bf, start=False, stop=False, skip_group_check=True)
                e.matmul(E_[:, S:384], ident_bf, neg_bf, start=False, stop=True, skip_group_check=True).then_inc(e_ps, 1)
                if k >= 2:
                    e.wait_ge(ct_sb, k - 1)
                c0 = b * S
                e.matmul(ps[:, 2 + k % 2, 0:S], ctxT[:, c0:c0 + P], Qz[:, h, c0:c0 + S], start=True, stop=True)
                e.matmul(ps[:, 2 + k % 2, S:384], ctxT[:, c0 + P:c0 + S], Qz[:, h, c0 + P:c0 + S],
                         start=True, stop=True).then_inc(s_ps, 1)

            def mix(u):
                b, g = divmod(u, XH // 2)
                if g == 0 and b:
                    e.wait_ge(o_sb, b)
                e.wait_ge(ct_sb, 2 * (u + 1))
                for i in range(2):
                    e.matmul(ps[64 * i:64 * i + 64, 4, g * S:(g + 1) * S], Va[:, 2 * b, 2 * g + i, :],
                             CT[:, (2 * u + i) % 4, 0:S], start=True, stop=True)
                for i in range(2):
                    m = e.matmul(ps[64 * i:64 * i + 64, 4, g * S + P:(g + 1) * S], Va[:, 2 * b + 1, 2 * g + i, :],
                                 CT[:, (2 * u + i) % 4, S:384], start=False, stop=True, skip_group_check=True)
                m.then_inc(pv_ps, 1)

            def to_tokens(b):
                e.wait_ge(o_sb, b + 1)
                if b:
                    e.wait_ge(h_sb, b)
                else:
                    e.wait_ge(em_in, 1)
                for f in range(HALVES):
                    for g in range(2):
                        i = 2 * f + g
                        m = e.transpose(ps[:, 5, i * P:(i + 1) * P], Oxs[:, g * S + f * P:g * S + (f + 1) * P], K("ident"))
                m.then_inc(t_ps, 1)

            for k in range(NXH):
                logits(k)
                if k % 2 and k > 2:
                    mix((k - 3) // 2)
                if k % 4 == 2 and k > 4:
                    to_tokens(k // 4 - 1)
            mix(NXH // 2 - 1)
            to_tokens(NB - 1)

        phases["pool"].append(pool_mlstm)
        phases["act"].append(act_mlstm)
        phases["dve"].append(dve_mlstm)
        phases["pe"].append(pe_mlstm)
        turn(1)


        dl = sb("dl", [P, NT, E])
        oh = sb("oh", [P, NT, E])
        mx8 = sb("mx8", [P, 3, NT])
        cnt = sb("cnt", [P, 4, E, NT])
        ne = sb("ne", [P, 3, E])
        posf = sb("posf", [P, NT])
        pos = sb("pos", [P, NT], I32)
        eidf = sb("eidf", [P, NSEG])
        eid = sb("eid", [P, NSEG], I32)
        big = arena[:, NSEG * D:NSEG * (D + E)].rearrange("p (s e) -> p s e", e=E)
        xs = arena[:, 0:NSEG * D].rearrange("p (s d) -> p s d", d=D)
        ys = xs
        xsT = arena[:, NSEG * D:2 * NSEG * D].rearrange("p (s d) -> p s d", d=D)
        w1c = arena[:, 2 * NSEG * D:2 * NSEG * D + 4 * (FF + 2)].rearrange("p (s f) -> p s f", s=4)
        b2r = work[:, 0:E * D].rearrange("p (e d) -> p e d", d=D)
        hT = work[:, 4 * T:5 * T].rearrange("p (s f) -> p s f", f=FF)
        kf_ok = sem("kf_ok")
        kp_out = sem("kp_out")
        ld_bias = sem("ld_bias")
        lg_ps = sem("lg_ps")
        dl_ok = sem("dl_ok")
        ex_ok = sem("ex_ok")
        oh_ok = sem("oh_ok")
        rk_ps = sem("rank_ps")
        pos_ok = sem("pos_ok")
        eid_ok = sem("eid_ok")
        sorted_out = sem("sorted_out")
        xs_in = [sem(f"xs_in{i}") for i in range(3)]
        xt2_ps = sem("segment_turned")
        xt2_sb = sem("segment_turned_sb")
        h_ps = sem("h_ps")
        w1_ok = sem("w1_ok")
        hT_ok = sem("hT_ok")
        y_ps = sem("y_ps")
        ys_ok = sem("ys_ok")
        ys_out = sem("ys_out")
        y_in = [sem(f"y_in{i}") for i in range(NT)]
        G3 = NSEG // 3

        def sync_moe(e):
            e.wait_ge(pv_ps, NXH // 2)
            e.wait_ge(h_sb, NB)
            e.dma_start(b2r.rearrange("p e d -> p (e d)"), w["b2"].rearrange("e d -> (e d)").partition_broadcast(P)).then_inc(ld_bias, 16)
            e.wait_ge(sorted_out, 16 * NT)
            for i in range(3):
                e.dma_start(xs[:, i * G3:(i + 1) * G3, :],
                            xs_scr[i * G3 * P:(i + 1) * G3 * P, :].rearrange("(s p) d -> p s d", p=P)).then_inc(xs_in[i], 16)
            EARLY["sync_keys"](e)
            for a, b in ((0, 9), (9, 18), (18, NSEG)):
                e.wait_ge(ys_ok, b)
                e.dma_start(ys_scr[a * P:b * P, :].rearrange("(s p) d -> p s d", p=P),
                            ys[:, a:b, :]).then_inc(ys_out, 16)

        def pool_moe(e):
            e.wait_ge(pos_ok, 1)
            e.wait_ge(ld_moe, 16 * 6)
            for n in range(NT):
                e.indirect_dma_start(xs_scr, bass.IndirectOffsetOnAxis(ap=pos[:, n:n + 1].bitcast(U32), axis=0),
                                     xN[:, n, :], None).then_inc(sorted_out, 16)
            EARLY["pool_keys"](e)
            e.wait_ge(ys_out, 48)
            for n in range(NT):
                e.indirect_dma_start(aN[:, n, :], None, ys_scr,
                                     bass.IndirectOffsetOnAxis(ap=pos[:, n:n + 1].bitcast(U32), axis=0)).then_inc(y_in[n], 16)

        def pe_moe(e):
            e.wait_ge(ld_moe, 16 * 6)
            for n in range(NT):
                if n % 4 == 0:
                    e.wait_ge(xt_sb, 3 + n // 4)
                m = e.matmul(ps[:, 4, E * n:E * (n + 1)], xT[:, n * P:(n + 1) * P], wr[:, :], start=True, stop=True)
            m.then_inc(lg_ps, 1)
            e.wait_ge(oh_ok, 1)
            for c in range(2):
                m = e.matmul(ps[:, 5, c * NT * E:(c + 1) * NT * E], K("causal")[:, c * P:(c + 1) * P],
                             oh[:, :, :].rearrange("p n e -> p (n e)"), start=True, stop=True)
            m.then_inc(rk_ps, 1)
            EARLY["pe_keys"](e)
            e.wait_ge(kf_ok, 1)
            e.wait_ge(eid_ok, 1)

            def turn_in(s):
                if s % G3 == 0:
                    e.wait_ge(xs_in[s // G3], 16)
                if s >= 2:
                    e.wait_ge(xt2_sb, s - 1)
                e.transpose(ps[:, s % 2, 0:P], xs[:, s, :], K("ident")).then_inc(xt2_ps, 1)

            def layer1(s):
                e.wait_ge(xt2_sb, s + 1)
                e.wait_ge(w1_ok, s + 1)
                if s >= 2:
                    e.wait_ge(hT_ok, s - 1)
                for f in range(2):
                    m = e.matmul(ps[:, 2 + s % 2, f * P:(f + 1) * P], w1c[:, s % 4, f * P:(f + 1) * P], xsT[:, s, :],
                                 start=True, stop=True)
                m.then_inc(h_ps, 1)

            def layer2(s):
                e.wait_ge(hT_ok, s + 1)
                if s >= 2:
                    e.wait_ge(ys_ok, s - 1)
                k = e.value_load(eid[0:1, s:s + 1], min_val=0, max_val=E - 1)
                for f in range(2):
                    m = e.matmul(ps[:, 6 + s % 2, 0:D], hT[:, s % 4, f * P:(f + 1) * P],
                                 w2[:, f, bass.ds(k, 1), :].rearrange("p o d -> p (o d)"), start=(f == 0), stop=(f == 1))
                m.then_inc(y_ps, 1)

            for i in range(-1, NSEG + 2):
                if i + 1 < NSEG:
                    turn_in(i + 1)
                if 0 <= i < NSEG:
                    layer1(i)
                if 0 <= i - 2 < NSEG:
                    layer2(i - 2)

        def act_moe(e):
            e.wait_ge(dl_ok, 1)
            e.activation(bN[:, 0, 0:NT * E].rearrange("p (n e) -> p n e", e=E), dl[:, :, :], ACT.Exp).then_inc(ex_ok, 1)
            EARLY["act_keys"](e)
            for s in range(NSEG):
                e.wait_ge(h_ps, s + 1)
                if s >= 4:
                    e.wait_ge(y_ps, s - 3)
                for f in range(2):
                    i = e.activation(hT[:, s % 4, f * P:(f + 1) * P], ps[:, 2 + s % 2, f * P:(f + 1) * P], ACT.Gelu,
                                     bias=w1c[:, s % 4, FF + f:FF + f + 1])
                i.then_inc(hT_ok, 1)

        def dve_moe(e):
            e.wait_ge(lg_ps, 1)
            lg = ps[:, 4, 0:NT * E].rearrange("p (n e) -> p n e", e=E)
            done(e.tensor_reduce(mx8[:, 0, :], lg, AX.X, ALU.max))
            e.tensor_tensor(dl[:, :, :], lg, mx8[:, 0, :].unsqueeze(2).broadcast_to([P, NT, E]), ALU.subtract).then_inc(dl_ok, 1)
            e.wait_ge(dl_ok, 1)
            done(e.tensor_scalar(oh[:, :, :], dl[:, :, :], 0.0, None, ALU.is_equal))
            done(e.tensor_tensor(oh[:, :, :], oh[:, :, :], K("rank").unsqueeze(1).broadcast_to([P, NT, E]), ALU.mult))
            done(e.tensor_reduce(mx8[:, 1, :], oh[:, :, :], AX.X, ALU.max))
            e.tensor_tensor(oh[:, :, :], oh[:, :, :], mx8[:, 1, :].unsqueeze(2).broadcast_to([P, NT, E]), ALU.is_equal).then_inc(oh_ok, 1)
            e.wait_ge(ex_ok, 1)
            done(e.tensor_reduce(mx8[:, 0, :], bN[:, 0, 0:NT * E].rearrange("p (n e) -> p n e", e=E), AX.X, ALU.add))
            done(e.reciprocal(mx8[:, 2, :], mx8[:, 0, :]))
            e.wait_ge(rk_ps, 1)
            rank = ps[:, 5, 0:NT * E].rearrange("p (n e) -> p e n", e=E)
            done(e.tensor_copy(cnt[:, 0], ps[:, 5, NT * E:2 * NT * E].rearrange("p (n e) -> p e n", e=E)))
            done(e.tensor_tensor_scan(cnt[:, 1].rearrange("p e n -> p (e n)"), K("first"), cnt[:, 0].rearrange("p e n -> p (e n)"),
                                      0.0, ALU.mult, ALU.add))
            g8 = big[:, 0:NT, :].rearrange("p n e -> p e n")
            done(e.tensor_tensor(g8, cnt[:, 1, :, NT - 1:NT].broadcast_to([P, E, NT]),
                                 K("full").unsqueeze(1).broadcast_to([P, E, NT]), ALU.is_gt))
            done(e.tensor_reduce(ne[:, 0, :], g8, AX.X, ALU.add))
            done(e.tensor_tensor_scan(ne[:, 1, :], K("causal")[:, P:P + E], ne[:, 0, :], 0.0, ALU.mult, ALU.add))
            done(e.tensor_tensor(ne[:, 2, :], ne[:, 1, :], ne[:, 0, :], ALU.subtract), wait=False)
            done(e.tensor_tensor(cnt[:, 2], cnt[:, 1], cnt[:, 0], ALU.subtract))
            done(e.scalar_tensor_tensor(cnt[:, 2], ne[:, 2, :].unsqueeze(2).broadcast_to([P, E, NT]), float(P), cnt[:, 2],
                                        ALU.mult, ALU.add))
            done(e.tensor_tensor(cnt[:, 3], rank, cnt[:, 2], ALU.add))
            done(e.tensor_tensor(cnt[:, 3], cnt[:, 3], oh[:, :, :].rearrange("p n e -> p e n"), ALU.mult))
            done(e.tensor_reduce(posf[:, :], cnt[:, 3].rearrange("p e n -> p n e"), AX.X, ALU.add))
            e.tensor_scalar(pos[:, :], posf[:, :], -1.0, None, ALU.add).then_inc(pos_ok, 1)
            done(e.tensor_tensor(big, ne[:, 1:2, :].broadcast_to([P, NSEG, E]), K("seg").unsqueeze(2).broadcast_to([P, NSEG, E]),
                                 ALU.is_le))
            done(e.tensor_reduce(eidf[:, :], big, AX.X, ALU.add))
            e.tensor_scalar(eid[:, :], eidf[:, :], float(E - 1), None, ALU.min).then_inc(eid_ok, 1)
            e.wait_ge(eid_ok, 1)
            e.wait_ge(ld_bias, 16)
            experts = {}

            def take_weights(s):
                if s >= 4:
                    e.wait_ge(hT_ok, s - 3)
                experts[s] = e.value_load(eid[0:1, s:s + 1], min_val=0, max_val=E - 1)
                e.tensor_copy(w1c[:, s % 4, :], w1[:, bass.ds(experts[s], 1), :].rearrange("p o f -> p (o f)")).then_inc(w1_ok, 1)

            take_weights(0)
            take_weights(1)
            for i in range(-1, NSEG + 2):
                if i + 1 < NSEG:
                    e.wait_ge(xt2_ps, i + 2)
                    e.tensor_copy(xsT[:, i + 1, :], ps[:, (i + 1) % 2, 0:P]).then_inc(xt2_sb, 1)
                if 2 <= i + 2 < NSEG:
                    take_weights(i + 2)
                if 0 <= i - 2 < NSEG:
                    s = i - 2
                    e.wait_ge(y_ps, s + 1)
                    e.tensor_tensor(ys[:, s, :], ps[:, 6 + s % 2, 0:D],
                                    b2r[:, bass.ds(experts.pop(s), 1), :].rearrange("p o d -> p (o d)"), ALU.add).then_inc(ys_ok, 1)
            for n in range(NT):
                e.wait_ge(y_in[n], 16)
                done(e.scalar_tensor_tensor(zN[:, n, :], aN[:, n, :], mx8[:, 2, n:n + 1], xN[:, n, :], ALU.mult, ALU.add))
                done(e.bn_stats(stats[:, n, :], zN[:, n, :]), wait=(n % 4 == 3))
                if n % 4 == 3:
                    layer_norm(zN, xN, ln_out, True, n - 3, n + 1)

        phases["sync"].append(sync_moe)
        phases["pool"].append(pool_moe)
        phases["act"].append(act_moe)
        phases["dve"].append(dve_moe)
        phases["pe"].append(pe_moe)


        KTs = work[:, 0:T]
        Qs = work[:, T:2 * T]
        oT = work[:, 2 * T:3 * T]
        Vl = arena[:, 8 * T:10 * T].rearrange("p (n h k) -> p n h k", n=NT, h=LH)
        Osb = work[:, 8 * T:9 * T]
        CL = work[:, 3 * T:6 * T].rearrange("p (s c) -> p s c", s=8)
        lq_ps = sem("lq_ps")
        lw_ok = sem("lw_ok")
        lv_ps = sem("lv_ps")
        lq_sb = sem("lq_sb")
        lk_sb = sem("lk_sb")
        lv_sb = sem("lv_sb")
        vl_one = sem("vl_one")
        lz_ok = sem("lz_ok")
        ls_ps = sem("ls_ps")
        lc_sb = sem("lc_sb")
        lo_ps = sem("lo_ps")
        lo_sb = sem("lo_sb")
        lt_ps = sem("lt_ps")
        lh_sb = sem("lh_sb")
        lm_ok = sem("linear_heads_mixed")
        ly_ps = sem("ly_ps")
        NLH = NB * LH

        def pool_linear(e):
            e.wait_ge(pv_ps, NXH // 2)
            e.memset(Vl[:, :, :, LD:], 1.0).then_inc(vl_one, 1)

        def pe_linear(e):
            pe_turn(xN, ln_out, NT * 2, halves=(0,))
            e.wait_ge(xt_sb, 5)
            e.wait_ge(ld_l1, 16 * 12)
            e.wait_ge(ys_ok, NSEG)

            def project(b, bank):
                for i in range(2):
                    e.matmul(ps[:, bank + i, :], l1w[:, i, :], xT[:, b * 512:(b + 1) * 512], start=True, stop=True).then_inc(lq_ps, 1)

            project(0, 0)
            for n in range(NT):
                if n == NT // 2:
                    pe_turn(xN, ln_out, NT * 2, halves=(1,))
                    e.wait_ge(xt_sb, 6)
                m = e.matmul(ps[:, 4 + n // 4, (n % 4) * P:(n % 4 + 1) * P], xT[:, n * P:(n + 1) * P], l1w[:, 2, :],
                             start=True, stop=True)
            m.then_inc(lv_ps, 1)

            def scores(k):
                b, h = divmod(k, LH)
                if k >= 4:
                    e.wait_ge(lc_sb, k - 3)
                if k % (2 * LH) == 0:
                    e.wait_ge(lk_sb, k // (2 * LH) + 1)
                e.wait_ge(lz_ok, k + 1)
                c0 = b * S
                e.matmul(ps[:, k % 4, 0:S], KTs[:, c0:c0 + P], Qz[:, h, c0:c0 + S], start=True, stop=True)
                e.matmul(ps[:, k % 4, S:384], KTs[:, c0 + P:c0 + S], Qz[:, h, c0 + P:c0 + S],
                         start=True, stop=True).then_inc(ls_ps, 1)

            def mix(u):
                b, g = divmod(u, LH // 4)
                if g == 0 and b >= 2:
                    e.wait_ge(lo_sb, b - 1)
                e.wait_ge(lc_sb, 4 * (u + 1))
                if u == 0:
                    e.wait_ge(lv_sb, 1)
                for i in range(4):
                    e.matmul(ps[32 * i:32 * i + 32, 4 + b % 2, g * S:(g + 1) * S], Vl[:, 2 * b, 4 * g + i, :],
                             CL[:, (4 * u + i) % 8, 0:S], start=True, stop=True)
                for i in range(4):
                    m = e.matmul(ps[32 * i:32 * i + 32, 4 + b % 2, g * S + P:(g + 1) * S], Vl[:, 2 * b + 1, 4 * g + i, :],
                                 CL[:, (4 * u + i) % 8, S:384], start=False, stop=True, skip_group_check=True)
                m.then_inc(lo_ps, 1)

            def to_tokens(b):
                e.wait_ge(lo_sb, b + 1)
                e.wait_ge(lk_sb, 2)
                if b >= 2:
                    e.wait_ge(lh_sb, b - 1)
                for i in range(4):
                    f, g = divmod(i, 2)
                    m = e.transpose(ps[:, 6 + b % 2, i * P:(i + 1) * P], Osb[:, (b % 2) * 512 + g * S + f * P:(b % 2) * 512 + g * S + (f + 1) * P],
                                    K("ident"))
                m.then_inc(lt_ps, 1)

            for k in range(NLH):
                scores(k)
                if k == 3:
                    project(1, 6)
                if k % 4 == 1 and k > 4:
                    mix((k - 5) // 4)
                if k % LH == 4 and k > LH:
                    to_tokens(k // LH - 1)
            mix(NLH // 4 - 1)
            to_tokens(NB - 1)

        def pe_linear_out(e):
            e.wait_ge(lw_ok, 1)
            for n in range(NT):
                if n % 4 == 0:
                    e.wait_ge(xt_sb, 7 + n // 4)
                m = e.matmul(ps[:, 4 + n // 4, (n % 4) * P:(n % 4 + 1) * P], oT[:, n * P:(n + 1) * P], l1w[:, 3, :],
                             start=True, stop=True)
                if n % 4 == 3:
                    m.then_inc(ly_ps, 1)

        def act_linear(e):
            act_turn(xT, halves=(0,))
            e.wait_ge(lq_ps, 1)
            e.copy(Qs[:, 0:512], ps[:, 0, :]).then_inc(lq_sb, 1)
            e.wait_ge(lq_ps, 2)
            e.copy(KTs[:, 0:512], ps[:, 1, :]).then_inc(lk_sb, 1)
            act_turn(xT, halves=(1,))
            e.wait_ge(lv_ps, 1)
            e.wait_ge(vl_one, 1)
            e.copy(Vl[:, :, :, 0:LD], ps[:, 4:6, :].rearrange("p b (n h k) -> p (b n) h k", h=LH, k=LD)).then_inc(lv_sb, 1)
            e.wait_ge(lq_ps, 3)
            e.copy(Qs[:, 512:], ps[:, 6, :]).then_inc(lq_sb, 1)
            e.wait_ge(lq_ps, 4)
            e.copy(KTs[:, 512:], ps[:, 7, :]).then_inc(lk_sb, 1)
            e.wait_ge(kp_out, 16 * NB)
            for b in range(NB):
                e.wait_ge(lo_ps, LH // 4 * (b + 1))
                if b >= 2:
                    e.wait_ge(lt_ps, b - 1)
                e.copy(Osb[:, (b % 2) * 512:(b % 2) * 512 + 512], ps[:, 4 + b % 2, :]).then_inc(lo_sb, 1)

        def dve_linear(e):
            e.wait_ge(ld_l1, 16 * 12)
            e.tensor_scalar(l1w[:, 3, :], l1w[:, 3, :], nrm[:, :], None, ALU.mult).then_inc(lw_ok, 1)

            def one_head(k):
                b, h = divmod(k, LH)
                if h == 0:
                    e.wait_ge(lq_sb, b // 2 + 1)
                e.tensor_scalar(Qz[:, h, b * S:(b + 1) * S], Qs[:, b * S:(b + 1) * S], K("hm8")[:, h:h + 1], None,
                                ALU.mult).then_inc(lz_ok, 1)

            for k in range(LH):
                one_head(k)

            def normalise(b):
                e.wait_ge(lt_ps, b + 1)
                tt = ps[:, 6 + b % 2, :].rearrange("p (f h k) -> p f h k", f=HALVES, h=LH)
                su, ab = nrm_s[:, :, 0:LH], nrm_a[:, :, 0:LH]
                done(e.tensor_copy(su, tt[:, :, :, LD]))
                done(e.scalar_tensor_tensor(ab, su, -1.0, su, ALU.mult, ALU.max))
                done(e.tensor_scalar(ab, ab, 1.0, None, ALU.max))
                done(e.reciprocal(su, ab))
                e.tensor_tensor(aN[:, 2 * b:2 * b + 2, :].rearrange("p f (h k) -> p f h k", k=LD), tt[:, :, :, 0:LD],
                                su.unsqueeze(3).broadcast_to([P, HALVES, LH, LD]), ALU.mult).then_inc(lh_sb, 1)

            g16 = aN[:, :, :].rearrange("p n (h k) -> p (n h) k", k=LD)
            b16 = bN[:, :, :].rearrange("p n (h k) -> p (n h) k", k=LD)
            G = NT * LH

            def head_norm(b):
                q = slice(b * G // NB, (b + 1) * G // NB)
                e.wait_ge(lh_sb, b + 1)
                done(e.tensor_tensor(b16[:, q, :], g16[:, q, :], g16[:, q, :], ALU.mult))
                done(e.tensor_reduce(hs1[:, q], b16[:, q, :], AX.X, ALU.add))

            for k in range(NLH):
                e.wait_ge(ls_ps, k + 1)
                if k >= 8 and k % 4 == 0:
                    e.wait_ge(lo_ps, k // 4 - 1)
                e.tensor_tensor(CL[:, k % 8, :], ps[:, k % 4, 0:384], K("causal"), ALU.mult).then_inc(lc_sb, 1)
                if k + LH < NLH:
                    one_head(k + LH)
                if k % LH == 6 and k > LH:
                    normalise(k // LH - 1)
                if k % LH == 0 and k >= 2 * LH:
                    head_norm(k // LH - 2)
            head_norm(NB - 2)
            normalise(NB - 1)
            head_norm(NB - 1)
            done(e.tensor_scalar(rs_v[:, 0:G], hs1[:, 0:G], 1.0 / LD, LN_EPS, ALU.mult, ALU.add))
            rsqrt(rs_v[:, 0:G], G)
            for h in range(2):
                q = slice(h * G // 2, (h + 1) * G // 2)
                e.tensor_tensor(g16[:, q, :], g16[:, q, :], rs_y[:, q].unsqueeze(2).broadcast_to([P, G // 2, LD]),
                                ALU.mult).then_inc(lm_ok, NT // 2)
            for h in range(2):
                e.wait_ge(ly_ps, h + 1)
                add_half(h, 4 + h, xN)
            layer_norm(zN, xN, ln_out, stats_taken=True)

        def turn_heads(ready):
            phases["pe"].append(lambda e: pe_turn(aN, ready, 0))
            phases["act"].append(lambda e: act_turn(oT))

        phases["pool"].append(pool_linear)
        phases["act"].append(act_linear)
        phases["dve"].append(dve_linear)
        phases["pe"].append(pe_linear)
        turn_heads(lm_ok)
        phases["pe"] += [pe_linear_out, lambda e: EARLY["values"](e)]
        turn(3)


        NR = 96
        ONES = float(np.array(0x3F803F80, np.uint32).view(np.float32))
        qf = work[:, 0:T]
        qr = work[:, T:2 * T]
        qp_early = work[:, 2 * T:3 * T + T // 2].bitcast(BF16).rearrange("p (c t) -> p c t", c=3)
        qp_last = arena[:, 14 * T:14 * T + 3 * S // 2].bitcast(BF16).rearrange("p (c t) -> p c t", c=3)

        def qp(c, b):
            return qp_early[:, c, b * S:(b + 1) * S] if b < NSLOT else qp_last[:, c, :]

        kf = work[:, 6 * T:7 * T]
        kr = work[:, 7 * T:8 * T]
        kp = work[:, 8 * T:9 * T + T // 2].bitcast(BF16).rearrange("p (c t) -> p c t", c=3)
        Qs_raw = [arena[:, 4 * T:6 * T], arena[:, 6 * T:8 * T], work[:, 6 * T:8 * T]]
        Ks_raw = [arena[:, 8 * T:10 * T], work[:, 9 * T:11 * T], work[:, 4 * T:6 * T]]
        NSLOT = 3
        Qt, Kt = ([a.bitcast(BF16).rearrange("p (h t) -> p h t", h=AH) for a in raw] for raw in (Qs_raw, Ks_raw))
        Vx = arena[:, 0:4 * T].rearrange("p (n h k) -> p n h k", n=NT, h=AH)
        Pb = work[:, 0:4 * T].rearrange("p (s c) -> p s c", s=8)
        Ox = work[:, 8 * T:9 * T]
        mS = sb("mS", [P, 2, 32])
        mt = sb("mt", [32, 2, P])
        mb = sb("mb", [32, 2, 3, P], BF16)
        xb = sb("xb", [P, NT, D])
        bq8 = sb("bq8", [P, 1])
        aq_ps = sem("aq_ps")
        av_ps = sem("av_ps")
        bq_ok = sem("bq_ok")
        aq_sb = sem("aq_sb")
        slot_clear = sem("slot_clear")
        av_sb = sem("av_sb")
        vx_one = sem("vx_one")
        qp_ok = [sem("qp_ok_first"), sem("qp_ok_rest")]
        pq_step = sem("pool_q_step")
        kp_ok = sem("kp_ok")
        kf_ps = sem("kf_ps")
        kstep = sem("k_split_step")
        slot_ld = [sem(f"slot_ld{i}") for i in range(NSLOT)]
        as_ps = sem("as_ps")
        as_used = sem("as_used")
        am_ps = sem("am_ps")
        am_parts = sem("am_parts")
        am_row = [sem("am_row0"), sem("am_row1")]
        at_ps = sem("at_ps")
        ap_sb = sem("ap_sb")
        ao_ps = sem("ao_ps")
        ao_sb = sem("ao_sb")
        ac_ps = sem("ac_ps")
        ah_sb = sem("ah_sb")
        ay_ps = sem("ay_ps")
        NSJ = 2 * AH // 2
        AHEAD = 22
        SBANK = (0, 1, 7)
        HBANK = (7, 0)
        WIDE = NB * AH - AHEAD + 4

        def lbank(t):
            return 2 + t % 2 if t < WIDE else (2, 3, 0, 1)[t % 4]


        def pe_keys(e):
            e.wait_ge(ld_l1, 16 * 12)
            for b in range(2):
                m = e.matmul(ps[:, 6 + b, :], axw[:, 1, :], ctxT[:, b * 512:(b + 1) * 512], start=True, stop=True)
            m.then_inc(kf_ps, 1)

        def act_keys(e):
            e.wait_ge(kf_ps, 1)
            e.activation(kf, ps[:, 6:8, :].rearrange("p b c -> p (b c)"), ACT.Identity, bias=abq[:, 1:2]).then_inc(kf_ok, 1)

        def pool_keys(e):
            e.wait_ge(kf_ok, 1)
            n = 0
            for i in range(3):
                j = e.tensor_copy(kp[:, i, :], kf if i == 0 else kr)
                if i == 2:
                    j.then_inc(kp_ok, 1)
                    break
                j.then_inc(kstep, 1)
                e.wait_ge(kstep, n + 1)
                e.tensor_tensor(kr, kf if i == 0 else kr, kp[:, i, :], ALU.subtract).then_inc(kstep, 1)
                e.wait_ge(kstep, n + 2)
                n += 2
            e.wait_ge(kp_out, 16 * NB)
            e.memset(Qs_raw[2], 0.0).then_inc(slot_clear, 1)
            e.memset(Ks_raw[1], ONES).then_inc(slot_clear, 1)

        def sync_keys(e):
            e.wait_ge(kp_ok, 1)
            for b in range(NB):
                e.dma_start(k_scr[b].rearrange("c d (h t) -> (d h) c t", t=S),
                            kp[:, :, b * S:(b + 1) * S]).then_inc(kp_out, 16)

        def pool_softmax(e):
            e.wait_ge(lo_ps, NLH // 4)
            e.memset(Ks_raw[0], ONES).then_inc(slot_clear, 1)
            e.memset(Qs_raw[0], 0.0).then_inc(slot_clear, 1)
            e.memset(Vx[:, :, :, AD:], 1.0).then_inc(vx_one, 1)
            e.memset(Qs_raw[1], 0.0).then_inc(slot_clear, 1)
            e.memset(Ks_raw[2], ONES).then_inc(slot_clear, 1)

        def pe_values(e):
            for n in range(NT):
                m = e.matmul(ps[:, 2 + n // 4, (n % 4) * P:(n % 4 + 1) * P], ctxT[:, n * P:(n + 1) * P], axw[:, 2, :],
                             start=True, stop=True)
            m.then_inc(av_ps, 1)

        def pe_softmax(e):
            for b in range(2):
                e.wait_ge(xt_sb, 9 + b)
                e.matmul(ps[:, b, :], axw[:, 0, :], xT[:, b * 512:(b + 1) * 512], start=True, stop=True).then_inc(aq_ps, 1)
            e.wait_ge(av_sb, 1)
            e.wait_ge(aq_sb, 2)

            def score(s):
                b, r = divmod(s, NSJ)
                f, hp = divmod(r, AH // 2)
                if s >= 3:
                    e.wait_ge(as_used, s - 2)
                for h in range(2):
                    m = e.matmul(ps[:, SBANK[s % 3], h * S:(h + 1) * S], Qt[b % NSLOT][0:NR, 2 * hp + h, f * P:(f + 1) * P],
                                 Kt[b % NSLOT][0:NR, 2 * hp + h, :], start=True, stop=True)
                m.then_inc(as_ps, 1)

            def turn_max(b):
                e.wait_ge(as_used, NSJ * (b + 1))
                if b >= 2:
                    e.wait_ge(ah_sb, 2 * (b - 2) + 1)
                e.transpose(ps[0:32, 6, 0:P], mS[:, b % 2, :], K("ident")).then_inc(am_ps, 1)

            def logits(t):
                b, h = divmod(t, AH)
                if t < WIDE + 2:
                    if t >= 2:
                        e.wait_ge(ap_sb, t - 1)
                elif t < WIDE + 4:
                    e.wait_ge(as_used, NB * NSJ)
                else:
                    e.wait_ge(ap_sb, t - 3)
                if h == 0:
                    e.wait_ge(am_row[b % 2], 48 * (b // 2 + 1))
                for f in range(HALVES):
                    m = e.matmul(ps[:, lbank(t), f * S:(f + 1) * S], Kt[b % NSLOT][:, h, f * P:(f + 1) * P], Qt[b % NSLOT][:, h, :],
                                 start=True, stop=True)
                m.then_inc(at_ps, 1)

            def mix(u, f):
                b, g = divmod(u, AH // 4)
                if f == 0:
                    e.wait_ge(ap_sb, 4 * (u + 1))
                    if g == 0 and b:
                        e.wait_ge(ao_sb, b)
                for i in range(4):
                    m = e.matmul(ps[32 * i:32 * i + 32, 4 + g // 2, (g % 2) * S:(g % 2 + 1) * S], Vx[:, 2 * b + f, 4 * g + i, :],
                                 Pb[:, (4 * u + i) % 8, f * S:(f + 1) * S], start=(f == 0), stop=(f == 1))
                if f == 1:
                    m.then_inc(ao_ps, 1)

            def to_tokens(b, f):
                e.wait_ge(ao_sb, b + 1)
                if b or f:
                    e.wait_ge(ah_sb, 2 * b + f)
                e.wait_ge(am_parts, 3 * min(b + 2 + f, NB))
                for g in range(4):
                    m = e.transpose(ps[:, 6, g * P:(g + 1) * P], Ox[:, g * S + f * P:g * S + (f + 1) * P], K("ident"))
                m.then_inc(ac_ps, 1)

            for t in range(-AHEAD, NB * AH):
                s = t + AHEAD
                if s < NB * NSJ:
                    if s % NSJ == 0:
                        b = s // NSJ
                        e.wait_ge(slot_ld[b % NSLOT], 16 * 9 * (b // NSLOT + 1))
                    score(s)
                if s % NSJ == 1 and 0 < s // NSJ <= NB:
                    turn_max(s // NSJ - 1)
                if t >= 0:
                    logits(t)
                    if t % 4 in (1, 2) and t > 4:
                        mix((t - 5) // 4, t % 4 - 1)
                    if s % NSJ in (14, 2) and t > AH:
                        to_tokens(t // AH - 1, int(s % NSJ == 2))
            mix(NB * AH // 4 - 1, 0)
            mix(NB * AH // 4 - 1, 1)
            pe_turn(aN, ah_sb, 0, HBANK, (0,))
            to_tokens(NB - 1, 0)
            to_tokens(NB - 1, 1)
            project_out(e, 0)
            pe_turn(aN, ah_sb, 0, HBANK, (1,))
            project_out(e, 1)

        def project_out(e, h):
            e.wait_ge(xt_sb, 11 + h)
            for n in range(4 * h, 4 * h + 4):
                m = e.matmul(ps[:, 2 + n // 4, (n % 4) * P:(n % 4 + 1) * P], oT[:, n * P:(n + 1) * P], axw[:, 3, :],
                             start=True, stop=True)
            m.then_inc(ay_ps, 1)

        def act_softmax(e):
            e.wait_ge(bq_ok, 1)
            for i in range(2):
                e.wait_ge(aq_ps, i + 1)
                e.activation(qf[:, i * 512:(i + 1) * 512], ps[:, i, :], ACT.Identity, bias=bq8[:, :],
                             scale=float(AD) ** -0.5).then_inc(aq_sb, 1)
            for t in range(NB * AH):
                e.wait_ge(at_ps, t + 1)
                if t >= 8 and t % 4 == 0:
                    e.wait_ge(ao_ps, t // 4 - 1)
                if t == 0:
                    e.wait_ge(pq_step, 2 * (NB - 2) + 1)
                if t == 2:
                    e.wait_ge(qp_ok[1], 3 * (NB - 1))
                e.activation(Pb[:, t % 8, :], ps[:, lbank(t), :], ACT.Exp).then_inc(ap_sb, 1)
                if t % AH == 2 and t > AH:
                    take(e, t // AH - 1)
            take(e, NB - 1)

        def take(e, b):
            e.wait_ge(ao_ps, AH // 4 * (b + 1))
            if b:
                e.wait_ge(ac_ps, 2 * b)
            e.copy(Ox[:, :], ps[:, 4:6, :].rearrange("p b c -> p (b c)")).then_inc(ao_sb, 1)

        def split_queries(e, b, parts, wait_rest):
            t = slice(b * S, (b + 1) * S)
            e.wait_ge(aq_sb, b // 2 + 1)
            for c in range(3):
                src = (qf if c == 0 else qr)[:, t]
                e.tensor_copy(qp(c, b), src).then_inc(parts, 1)
                if c < 2:
                    e.wait_ge(parts, parts_so_far(b) + c + 1)
                    wait_rest(e.tensor_tensor(qr[:, t], src, qp(c, b), ALU.subtract), c)

        def parts_so_far(b):
            return 3 * max(b - 1, 0)

        def pool_queries(e):
            e.wait_ge(ld_l1, 16 * 12)
            for b in range(1, NB):
                def wait_rest(i, c):
                    i.then_inc(pq_step, 1)
                    e.wait_ge(pq_step, 2 * (b - 1) + c + 1)
                split_queries(e, b, qp_ok[1], wait_rest)
            e.tensor_tensor(xb[:, :, :], xN[:, :, :], abr[:, 1:2, :].broadcast_to([P, NT, D]), ALU.add).then_inc(pq_step, 1)

        def dve_softmax(e):
            e.wait_ge(ld_l1, 16 * 12)
            e.tensor_scalar(bq8[:, :], abq[:, 0:1], float(AD) ** -0.5, None, ALU.mult).then_inc(bq_ok, 1)
            split_queries(e, 0, qp_ok[0], lambda i, c: done(i))
            e.wait_ge(vx_one, 1)
            e.wait_ge(av_ps, 1)
            for f in range(2):
                i = e.tensor_tensor(Vx[:, 4 * f:4 * f + 4, :, 0:AD],
                                    ps[:, 2 + f, :].rearrange("p (n h k) -> p n h k", h=AH, k=AD),
                                    abr[:, 0, :].rearrange("p (h k) -> p h k", k=AD).unsqueeze(1).broadcast_to([P, 4, AH, AD]),
                                    ALU.add)
            i.then_inc(av_sb, 1)

            def maxima(s):
                b, r = divmod(s, NSJ)
                f, hp = divmod(r, AH // 2)
                e.wait_ge(as_ps, s + 1)
                if r == 0 and b >= 2:
                    e.wait_ge(am_ps, b - 1)
                e.tensor_reduce(mS[:, b % 2, 4 * hp + f:4 * hp + f + 3:2], ps[:, SBANK[s % 3], :].rearrange("p (h k) -> p h k", h=2),
                                AX.X, ALU.max, negate=True).then_inc(as_used, 1)

            def parts_of_max(b):
                e.wait_ge(am_ps, b + 1)
                if b >= 2:
                    e.wait_ge(am_row[b % 2], 48 * (b // 2))
                o = mb[:, b % 2]
                done(e.tensor_copy(mt[:, 0, :], ps[0:32, 6, 0:P]))
                for i in range(3):
                    e.tensor_copy(o[:, i, :], mt[:, min(i, 1), :]).then_inc(am_parts, 1)
                    if i < 2:
                        e.wait_ge(am_parts, 3 * b + i + 1)
                        done(e.tensor_tensor(mt[:, 1, :], mt[:, i, :], o[:, i, :], ALU.subtract))

            def normalise(b, f):
                e.wait_ge(ac_ps, 2 * b + f + 1)
                tt = ps[:, 6, :].rearrange("p (h k) -> p h k", h=AH)
                done(e.reciprocal(nrm_s[:, f, :], tt[:, :, AD]))
                e.tensor_tensor(aN[:, 2 * b + f, :].rearrange("p (h k) -> p h k", k=AD), tt[:, :, 0:AD],
                                nrm_s[:, f, :].unsqueeze(2).broadcast_to([P, AH, AD]), ALU.mult).then_inc(ah_sb, 1)

            for b in range(NB):
                for r in range(NSJ):
                    maxima(b * NSJ + r)
                    if r == 2 and b >= 3:
                        normalise(b - 3, 1)
                    if r == NSJ - 2 and b >= 2:
                        normalise(b - 2, 0)
                parts_of_max(b)
            for b, f in ((NB - 3, 1), (NB - 2, 0), (NB - 2, 1), (NB - 1, 0), (NB - 1, 1)):
                normalise(b, f)
            e.wait_ge(pq_step, 2 * (NB - 1) + 1)
            for h in range(2):
                e.wait_ge(ay_ps, h + 1)
                add_half(h, 2 + h, xb)
            layer_norm(zN, xN, ln_out, stats_taken=True)

        PAIRS_Q = ((0, 3), (1, 2), (2, 1))
        PAIRS_K = ((0, 3), (0, 2), (0, 1))

        def sync_softmax(e):
            def load_keys(b):
                row = 0
                for c, n in PAIRS_K:
                    e.dma_start(Kt[b % NSLOT][row:row + n * AD, :, :].rearrange("p h t -> p (h t)"),
                                k_scr[b, c:c + n].rearrange("c d n -> (c d) n")).then_inc(slot_ld[b % NSLOT], 16)
                    row += n * AD

            def load_queries(b):
                row = 0
                for c, n in PAIRS_Q:
                    e.wait_ge(qp_ok[min(b, 1)], parts_so_far(b) + c + 1)
                    for _ in range(n):
                        e.dma_start(Qt[b % NSLOT][row:row + AD, :, :], qp(c, b)).then_inc(slot_ld[b % NSLOT], 16)
                        row += AD

            e.wait_ge(slot_clear, 3)
            load_keys(0)
            load_keys(1)
            e.wait_ge(slot_clear, 6)
            load_keys(2)
            for b in range(NSLOT):
                load_queries(b)

            def load_max(b):
                for i in range(3):
                    e.wait_ge(am_parts, 3 * b + i + 1)
                    e.dma_start(Qt[b % NSLOT][NR + i:NR + i + 1, :, :].rearrange("o h (f t) -> o (h f) t", f=2),
                                mb[:, b % 2, i, :]).then_inc(am_row[b % 2], 16)

            load_max(0)
            load_max(1)
            for b in range(NSLOT, NB):
                e.wait_ge(at_ps, AH * (b - NSLOT + 1))
                load_keys(b)
                load_queries(b)
            for b in range(2, NB):
                load_max(b)

        EARLY.update(values=pe_values, pe_keys=pe_keys, act_keys=act_keys, pool_keys=pool_keys, sync_keys=sync_keys)
        phases["sync"].append(sync_softmax)
        phases["pool"] += [pool_softmax, pool_queries]
        phases["act"].append(act_softmax)
        phases["dve"].append(dve_softmax)
        phases["pe"].append(pe_softmax)
        phases["act"].append(lambda e: act_turn(oT, HBANK))
        turn(4)

        fa = work[:, 0:4 * T].rearrange("p (b k t) -> p b k t", b=2, k=4)
        fb = work[:, 4 * T:8 * T].rearrange("p (b k t) -> p b k t", b=2, k=4)
        sg = work[:, 8 * T:10 * T].rearrange("p (s t) -> p s t", s=4)
        g_ps = sem("g_ps")
        fw3_ok = sem("fw3_ok")
        u_ps = sem("u_ps")
        sg_ok = sem("sg_ok")
        h1_ok = sem("h1_ok")
        gel_ps = sem("gel_ps")
        gel_ok = sem("gel_ok")
        fy_ps = sem("fy_ps")

        def pe_ffn(e):
            e.wait_ge(ld_ffn, 16 * 7)
            for j in range(8):
                blk, m = divmod(j, 4)
                if j == 0:
                    e.wait_ge(xt_sb, 13)
                if j == 3:
                    e.wait_ge(xt_sb, 14)
                if j >= 4:
                    e.wait_ge(h1_ok, j - 3)
                t = slice(blk * 512, (blk + 1) * 512)
                e.matmul(ps[:, 2 * (j % 4), :], fw1[:, m * P:(m + 1) * P], xT[:, t], start=True, stop=True).then_inc(g_ps, 1)
                e.matmul(ps[:, 2 * (j % 4) + 1, :], fw2[:, m * P:(m + 1) * P], xT[:, t], start=True, stop=True).then_inc(u_ps, 1)
            for j in range(16):
                layer, blk, m = j // 8, (j // 4) % 2, j % 4
                if j < 8:
                    e.wait_ge(h1_ok, max(4 * (blk + 1), j // 2 + 5))
                else:
                    e.wait_ge(gel_ok, max(4 * (blk + 1), j - 7))
                wt, src = ((fh1, fa), (fh2, fb))[layer]
                for k in range(4):
                    i = e.matmul(ps[:, j % 8, :], wt[:, k, m * P:(m + 1) * P], src[:, blk, k, :], start=(k == 0), stop=(k == 3))
                i.then_inc(gel_ps, 1)
            for n in range(NT):
                blk = n // 4
                if n == 0:
                    e.wait_ge(fw3_ok, 1)
                if n % 4 == 0:
                    e.wait_ge(gel_ok, 12 + 4 * blk)
                for k in range(4):
                    i = e.matmul(ps[:, blk, (n % 4) * P:(n % 4 + 1) * P], fa[:, blk, k, (n % 4) * P:(n % 4 + 1) * P], fw3[:, k, :],
                                 start=(k == 0), stop=(k == 3))
                if n % 4 == 3:
                    i.then_inc(fy_ps, 1)

        def act_ffn(e):
            for j in range(8):
                e.wait_ge(g_ps, j + 1)
                if j >= 4:
                    e.wait_ge(h1_ok, j - 3)
                e.activation(sg[:, j % 4, :], ps[:, 2 * (j % 4), :], ACT.Silu, scale=fsc[:, 0, j % 4:j % 4 + 1]).then_inc(sg_ok, 1)
            for j in range(16):
                layer, blk, m = j // 8, (j // 4) % 2, j % 4
                e.wait_ge(gel_ps, j + 1)
                if j >= 8:
                    e.wait_ge(gel_ps, 12 if blk == 0 else 16)
                dst = (fb, fa)[layer]
                e.activation(dst[:, blk, m, :], ps[:, j % 8, :], ACT.Gelu, scale=fsc[:, 2 + layer, m:m + 1]).then_inc(gel_ok, 1)

        def dve_ffn(e):
            e.wait_ge(ld_ffn, 16 * 7)
            e.tensor_tensor(fw3[:, :, :], fw3[:, :, :], fs3[:, :].unsqueeze(1).broadcast_to([P, 4, D]), ALU.mult).then_inc(fw3_ok, 1)
            for j in range(8):
                e.wait_ge(u_ps, j + 1)
                e.wait_ge(sg_ok, j + 1)
                e.scalar_tensor_tensor(fa[:, j // 4, j % 4, :], ps[:, 2 * (j % 4) + 1, :], fsc[:, 1, j % 4:j % 4 + 1],
                                       sg[:, j % 4, :], ALU.mult, ALU.mult).then_inc(h1_ok, 1)
            for h in range(2):
                e.wait_ge(fy_ps, h + 1)
                add_half(h, h, xN)
            layer_norm(zN, xN, ln_out, stats_taken=True)

        phases["act"].append(act_ffn)
        phases["dve"].append(dve_ffn)
        phases["pe"].append(pe_ffn)

        def sync_tail(e):
            for h in range(2):
                e.wait_ge(ln_out, NT * (N_NORMS - 1) + 4 * (h + 1))
                e.dma_start(out.rearrange("(n p) d -> p n d", p=P)[:, 4 * h:4 * h + 4, :], xN[:, 4 * h:4 * h + 4, :]).then_inc(fin, 16)
            e.wait_ge(fin, 32)
            for q, n in final_loads:
                e.wait_ge(q, n)

        final_loads = [(ld_ctx, 48), (ld_w1, 80), (ld_moe, 16 * 6), (ld_l1, 16 * 12), (ld_ffn, 16 * 7)]
        N_NORMS = 6

        @block.sync
        def _(e):
            sync_program(e)

        @block.gpsimd
        def _(e):
            for f in phases["pool"]:
                f(e)

        @block.scalar
        def _(e):
            for f in phases["act"]:
                f(e)

        @block.vector
        def _(e):
            for f in phases["dve"]:
                f(e)

        @block.tensor
        def _(e):
            for f in phases["pe"]:
                f(e)



def _arrays(inputs):

    def by_width(a):
        return np.swapaxes(a.reshape(a.shape[:-1] + (AH, AD)), -1, -2).reshape(a.shape)

    g = {k: np.asarray(a) for k, a in inputs.items()}
    p = np.arange(P)
    c = np.ascontiguousarray
    table = const_table()
    bf = np.zeros((P, 2 * P + 16 * P), np.float32)
    bf[:, 0:P] = np.eye(P)
    bf[:, P:2 * P] = np.where(p[:, None] <= p[None, :], 0, MASKED)
    sel = (p[:, None] % 32 == np.arange(16)[None, :]) & (p[:, None] < 96)
    bf[:, 2 * P:] = np.repeat(sel, P, 1)
    bf = (bf.view(np.uint32) >> 16).astype(np.uint16)
    return {
        "x": c(g["x"].reshape(T, D)), "ctx": c(g["ctx_1024"].reshape(T, D)),
        "xT": c(g["x"].reshape(T, D).T), "ctxT": c(g["ctx_1024"].reshape(T, D).T),
        "consts": table, "cbf": bf,
        "W0T": c(g["L0_attn_W"].T), "ln_gamma": g["L0_attn_ln_gamma"], "ln_beta": g["L0_attn_ln_beta"],
        "lam_logit": g["L0_attn_lam_logit"].reshape(1), "eta": g["L0_attn_eta"].reshape(1),
        "igate_kernel": g["L0_xattn_igate_kernel"], "fgate_kernel": g["L0_xattn_fgate_kernel"],
        "igate_bias": g["L0_xattn_igate_bias"], "fgate_bias": g["L0_xattn_fgate_bias"],
        "outnorm_scale": g["L0_xattn_outnorm_scale"],
        "router_w": g["L0_ffn_router_w"], "w1": g["L0_ffn_w1"], "b1": c(g["L0_ffn_b1"].reshape(E, 2, P).transpose(2, 0, 1).reshape(P, 2 * E)),
        "w2": g["L0_ffn_w2"], "b2": g["L0_ffn_b2"],
        "lqT": c(g["L1_attn_Wq"].T), "lkT": c(g["L1_attn_Wk"].T), "lvT": c(g["L1_attn_Wv"].T),
        "loT": c(g["L1_attn_Wo"].T), "norm_w": c(np.tile(g["L1_attn_norm_w"], LH)[:, None]),
        "aWq": c(by_width(g["L1_xattn_Wq"])), "aWk": c(by_width(g["L1_xattn_Wk"])), "aWv": g["L1_xattn_Wv"], "aWo": g["L1_xattn_Wo"],
        "abqk": c(np.stack([by_width(g["L1_xattn_bq"]), by_width(g["L1_xattn_bk"])], 1)), "abv": g["L1_xattn_bv"], "abo": g["L1_xattn_bo"],
        "w1T": c(g["L1_ffn_w1_w"].T), "w2T": c(g["L1_ffn_w2_w"].T), "h1T": c(g["L1_ffn_h1_w"].T),
        "h2T": c(g["L1_ffn_h2_w"].T), "w3T": c(g["L1_ffn_w3_w"].T),
        "hidden_scales": c(np.concatenate([g["L1_ffn_" + n].reshape(4, P).T for n in ("w1_s", "w2_s", "h1_s", "h2_s")], 1)),
        "w3_s": g["L1_ffn_w3_s"],
    }


def _program(nc, arrays, mybir_):
    a = {n: nc.dram_tensor("in_" + n, v.shape, mybir_.dt.from_np(v.dtype), kind="ExternalInput").ap()
         for n, v in arrays.items()}
    out = nc.dram_tensor("out_y", (T, D), F32, kind="ExternalOutput").ap()
    fixed = ("x", "ctx", "xT", "ctxT", "consts", "cbf")
    decoder(nc, a["x"], a["ctx"], a["xT"], a["ctxT"], a["consts"], a["cbf"],
            {n: v for n, v in a.items() if n not in fixed}, out)


def kernel(**inputs):
    import concourse.bacc as _bacc
    from concourse import mybir as _mybir
    from concourse.bass_utils import run_bass_kernel_spmd as _run

    arrays = _arrays(inputs)
    nc = _bacc.Bacc("TRN2", target_bir_lowering=False, num_devices=1)
    _program(nc, arrays, _mybir)
    r = _run(nc, [{"in_" + n: v for n, v in arrays.items()}], core_ids=[0])
    return np.asarray(r.results[0]["out_y"]).reshape(NB, S, D)
```
